# Optimizing a Trainium2 kernel written in Bass

```python
import numpy as np
import jax
import jax.numpy as jnp

def _softmax(x, axis=-1):
    return jax.nn.softmax(x, axis=axis)

def _gelu(x):
    return jax.nn.gelu(x, approximate=True)

def _silu(x):
    return jax.nn.silu(x)

def _sigmoid(x):
    return jax.nn.sigmoid(x)

def _layernorm(x, axis=-1, eps=1e-05):
    m = jnp.mean(x, axis=axis, keepdims=True)
    v = jnp.var(x, axis=axis, keepdims=True)
    return (x - m) / jnp.sqrt(v + eps)

def _scatter_add(tgt, idx, src, axis=0):
    return tgt.at[idx].add(src)

def _segment_sum(src, seg, n):
    return jax.ops.segment_sum(src, seg, n)
kernel_name = 'mk_perceiver_d1_seqx_r2_44a75c'

def setup_inputs(seed: int=0):
    np.random.seed(seed)
    _w = jnp.asarray

    def _rec_inputs():
        import jax
        import jax.numpy as jnp
        _rk = jax.random.key(seed)
        x = 0.0002417 + 0.9998 * jax.random.normal(jax.random.fold_in(_rk, 1), (8, 128, 512), jnp.float32)
        _lenS = 128 - jax.random.randint(jax.random.fold_in(_rk, 7), (8,), 0, max(1, 128 // 4) + 1, jnp.int32)
        _lenS2 = 2048 - jax.random.randint(jax.random.fold_in(_rk, 8), (8,), 0, max(1, 2048 // 4) + 1, jnp.int32)
        _ctx_1024P = jax.random.normal(jax.random.fold_in(_rk, 11), (8, 16, 512), jnp.float32)
        _ctx_1024c = jax.random.dirichlet(jax.random.fold_in(_rk, 511), 0.3 * jnp.ones((16,), jnp.float32), (8, 2048))
        _ctx_1024t = jnp.einsum('bsk,bkd->bsd', _ctx_1024c, _ctx_1024P)
        _ctx_1024t = _ctx_1024t * jax.lax.rsqrt(jnp.mean(jnp.square(_ctx_1024t)) + 1e-12) * 0.953939
        ctx_1024 = 7.22013e-05 + 1.00017 * (_ctx_1024t + 0.3 * jax.random.normal(jax.random.fold_in(_rk, 611), (8, 2048, 512), jnp.float32))
        _validS = jnp.arange(128)[None, :] < _lenS[:, None]
        _validS2 = jnp.arange(2048)[None, :] < _lenS2[:, None]
        _causal = jnp.tril(jnp.ones((128, 128), dtype=bool))
        mask_BxS2_bk1 = jnp.broadcast_to(_validS2[:, :], (8, 2048))
        return (x, ctx_1024, mask_BxS2_bk1)
    x, ctx_1024, mask_BxS2_bk1 = _rec_inputs()

    def _L0_xattn_setup():
        import jax, jax.numpy as jnp
        import numpy as np
        D_MODEL = 512
        NUM_HEADS = 16
        DEPTH = D_MODEL // NUM_HEADS
        B, S = (4, 1024)
        NEG_INF = float('-inf')

        def _split_heads(x, b):
            return x.reshape(b, -1, NUM_HEADS, DEPTH).transpose(0, 2, 1, 3)
        key = jax.random.key(seed)
        ks = jax.random.split(key, 12)
        inp = {'value': jax.random.normal(ks[0], (B, S, D_MODEL), jnp.float32), 'key': jax.random.normal(ks[1], (B, S, D_MODEL), jnp.float32), 'query': jax.random.normal(ks[2], (B, S, D_MODEL), jnp.float32), 'key_padding_mask': jnp.arange(S)[None, :] < 3 * S // 4}
        inp['key_padding_mask'] = jnp.broadcast_to(inp['key_padding_mask'], (B, S))
        scale = 1.0 / np.sqrt(D_MODEL)
        inp['Wq'] = jax.random.normal(ks[3], (D_MODEL, D_MODEL), jnp.float32) * scale
        inp['bq'] = jnp.zeros((D_MODEL,), jnp.float32)
        inp['Wk'] = jax.random.normal(ks[4], (D_MODEL, D_MODEL), jnp.float32) * scale
        inp['bk'] = jnp.zeros((D_MODEL,), jnp.float32)
        inp['Wv'] = jax.random.normal(ks[5], (D_MODEL, D_MODEL), jnp.float32) * scale
        inp['bv'] = jnp.zeros((D_MODEL,), jnp.float32)
        inp['Wo'] = jax.random.normal(ks[6], (D_MODEL, D_MODEL), jnp.float32) * scale
        inp['bo'] = jnp.zeros((D_MODEL,), jnp.float32)
        return inp
    _L0_xattn_all = _L0_xattn_setup()
    _L0_xattn_in = {k: v for k, v in _L0_xattn_all.items() if k in ('Wq', 'bq', 'Wk', 'bk', 'Wv', 'bv', 'Wo', 'bo')}
    del _L0_xattn_all

    def _L0_attn_setup():
        import jax, jax.numpy as jnp
        import numpy as np
        import math
        NUM_HEADS = 16
        SEGMENT_SIZE = 128
        DILATION = 2

        def hilbert_map(seq_len: int) -> np.ndarray:
            if seq_len <= 64:
                return np.arange(seq_len, dtype=np.int64)
            g = int(math.ceil(math.sqrt(seq_len)))
            fm = np.zeros(seq_len, dtype=np.int64)
            idx = 0
            for row in range(g):
                cols = range(g) if row % 2 == 0 else range(g - 1, -1, -1)
                for col in cols:
                    lp = row * g + col
                    if lp < seq_len and idx < seq_len:
                        fm[lp] = idx
                        idx += 1
            return fm
        key = jax.random.key(seed)
        k1, k2, k3 = jax.random.split(key, 3)
        B, S, D = (2, 4096, 512)
        x = jax.random.normal(k1, (B, S, D), dtype=jnp.float32)
        W_qkv = jax.random.normal(k2, (D, 3 * D), dtype=jnp.float32) * 0.02
        W_out = jax.random.normal(k3, (D, D), dtype=jnp.float32) * 0.02
        return {'x': x, 'W_qkv': W_qkv, 'W_out': W_out}
    _L0_attn_all = _L0_attn_setup()
    _L0_attn_in = {k: v for k, v in _L0_attn_all.items() if k in ('W_qkv', 'W_out')}
    del _L0_attn_all

    def _L0_ffn_setup():
        import jax, jax.numpy as jnp
        import numpy as np
        D, H, P, E, K, F = (512, 16, 64, 8, 2, 2048)
        B, S = (2, 1024)
        NROT = 32
        BASE = 10000.0
        EPS = 1e-05

        def _ln(x, g, b):
            m = jnp.mean(x, -1, keepdims=True)
            v = jnp.mean(jnp.square(x - m), -1, keepdims=True)
            return (x - m) * jax.lax.rsqrt(v + EPS) * g + b

        def _rope(x):
            xr, xp = (x[..., :NROT], x[..., NROT:])
            half = NROT // 2
            inv = BASE ** (-jnp.arange(half, dtype=jnp.float32) / half)
            ang = jnp.arange(x.shape[2], dtype=jnp.float32)[:, None] * inv[None, :]
            cos, sin = (jnp.cos(ang), jnp.sin(ang))
            x1, x2 = (xr[..., :half], xr[..., half:])
            xr = jnp.concatenate([x1 * cos - x2 * sin, x1 * sin + x2 * cos], -1)
            return jnp.concatenate([xr, xp], -1)

        def _gate(x, Wsel):
            s = jax.nn.sigmoid(jnp.einsum('bsd,hed->bhse', x, Wsel))
            _, idx = jax.lax.top_k(s, K)
            mask = jax.nn.one_hot(idx, E, dtype=s.dtype).sum(-2)
            return s * mask

        def _moe_attn(x, Wq, Wk, Wv, Wo, Wsel_v, Wsel_o):
            q = _rope(jnp.einsum('bsd,hdp->bhsp', x, Wq))
            k = _rope(jnp.einsum('bsd,hdp->bhsp', x, Wk))
            gv = _gate(x, Wsel_v)
            v = jnp.einsum('bsd,bhse,hedp->bhsp', x, gv, Wv)
            att = jax.nn.softmax(jnp.einsum('bhsp,bhtp->bhst', q, k) / np.sqrt(P), axis=-1)
            o = jnp.einsum('bhst,bhtp->bhsp', att, v)
            go = _gate(x, Wsel_o)
            return jnp.einsum('bhsp,bhse,hepd->bsd', o, go, Wo)
        key = jax.random.key(seed)
        ks = jax.random.split(key, 10)
        f = lambda k, sh: jax.random.normal(k, sh, jnp.float32) * 0.02
        return dict(src=jax.random.normal(ks[0], (B, S, D), jnp.float32), Wq=f(ks[1], (H, D, P)), Wk=f(ks[2], (H, D, P)), Wv=f(ks[3], (H, E, D, P)), Wo=f(ks[4], (H, E, P, D)), Wsel_v=f(ks[5], (H, E, D)), Wsel_o=f(ks[6], (H, E, D)), ln1_g=jnp.ones(D, jnp.float32), ln1_b=jnp.zeros(D, jnp.float32), ln2_g=jnp.ones(D, jnp.float32), ln2_b=jnp.zeros(D, jnp.float32), W1=f(ks[7], (D, F)), b1=jnp.zeros(F, jnp.float32), W2=f(ks[8], (F, D)), b2=jnp.zeros(D, jnp.float32))
    _L0_ffn_all = _L0_ffn_setup()
    _L0_ffn_in = {k: v for k, v in _L0_ffn_all.items() if k in ('Wq', 'Wk', 'Wv', 'Wo', 'Wsel_v', 'Wsel_o', 'ln1_g', 'ln1_b', 'ln2_g', 'ln2_b', 'W1', 'b1', 'W2', 'b2')}
    del _L0_ffn_all
    return {'x': x, 'ctx_1024': ctx_1024, 'mask_BxS2_bk1': mask_BxS2_bk1, 'L0_xattn_Wq': _L0_xattn_in['Wq'], 'L0_xattn_bq': _L0_xattn_in['bq'], 'L0_xattn_Wk': _L0_xattn_in['Wk'], 'L0_xattn_bk': _L0_xattn_in['bk'], 'L0_xattn_Wv': _L0_xattn_in['Wv'], 'L0_xattn_bv': _L0_xattn_in['bv'], 'L0_xattn_Wo': _L0_xattn_in['Wo'], 'L0_xattn_bo': _L0_xattn_in['bo'], 'L0_attn_W_qkv': _L0_attn_in['W_qkv'], 'L0_attn_W_out': _L0_attn_in['W_out'], 'L0_ffn_Wq': _L0_ffn_in['Wq'], 'L0_ffn_Wk': _L0_ffn_in['Wk'], 'L0_ffn_Wv': _L0_ffn_in['Wv'], 'L0_ffn_Wo': _L0_ffn_in['Wo'], 'L0_ffn_Wsel_v': _L0_ffn_in['Wsel_v'], 'L0_ffn_Wsel_o': _L0_ffn_in['Wsel_o'], 'L0_ffn_ln1_g': _L0_ffn_in['ln1_g'], 'L0_ffn_ln1_b': _L0_ffn_in['ln1_b'], 'L0_ffn_ln2_g': _L0_ffn_in['ln2_g'], 'L0_ffn_ln2_b': _L0_ffn_in['ln2_b'], 'L0_ffn_W1': _L0_ffn_in['W1'], 'L0_ffn_b1': _L0_ffn_in['b1'], 'L0_ffn_W2': _L0_ffn_in['W2'], 'L0_ffn_b2': _L0_ffn_in['b2']}

def reference(x, ctx_1024, mask_BxS2_bk1, L0_xattn_Wq, L0_xattn_bq, L0_xattn_Wk, L0_xattn_bk, L0_xattn_Wv, L0_xattn_bv, L0_xattn_Wo, L0_xattn_bo, L0_attn_W_qkv, L0_attn_W_out, L0_ffn_Wq, L0_ffn_Wk, L0_ffn_Wv, L0_ffn_Wo, L0_ffn_Wsel_v, L0_ffn_Wsel_o, L0_ffn_ln1_g, L0_ffn_ln1_b, L0_ffn_ln2_g, L0_ffn_ln2_b, L0_ffn_W1, L0_ffn_b1, L0_ffn_W2, L0_ffn_b2):
    import jax
    import jax.numpy as jnp

    def _L0_xattn_ref(value, key, query, key_padding_mask, Wq, bq, Wk, bk, Wv, bv, Wo, bo):
        import jax, jax.numpy as jnp
        import numpy as np
        D_MODEL = 512
        NUM_HEADS = 16
        DEPTH = D_MODEL // NUM_HEADS
        B, S = (4, 1024)
        NEG_INF = float('-inf')

        def _split_heads(x, b):
            return x.reshape(b, -1, NUM_HEADS, DEPTH).transpose(0, 2, 1, 3)
        b = query.shape[0]
        q = _split_heads(query @ Wq + bq, b)
        k = _split_heads(key @ Wk + bk, b)
        v = _split_heads(value @ Wv + bv, b)
        logits = jnp.einsum('bhqd,bhkd->bhqk', q, k) / jnp.sqrt(jnp.asarray(DEPTH, q.dtype))
        logits = jnp.where(key_padding_mask[:, None, None, :], logits, NEG_INF)
        attn = jax.nn.softmax(logits, axis=-1)
        out = jnp.einsum('bhqk,bhkd->bhqd', attn, v)
        out = out.transpose(0, 2, 1, 3).reshape(b, -1, D_MODEL)
        return out @ Wo + bo

    def _L0_attn_ref(x, W_qkv, W_out):
        import jax, jax.numpy as jnp
        import numpy as np
        import math
        NUM_HEADS = 16
        SEGMENT_SIZE = 128
        DILATION = 2

        def hilbert_map(seq_len: int) -> np.ndarray:
            if seq_len <= 64:
                return np.arange(seq_len, dtype=np.int64)
            g = int(math.ceil(math.sqrt(seq_len)))
            fm = np.zeros(seq_len, dtype=np.int64)
            idx = 0
            for row in range(g):
                cols = range(g) if row % 2 == 0 else range(g - 1, -1, -1)
                for col in cols:
                    lp = row * g + col
                    if lp < seq_len and idx < seq_len:
                        fm[lp] = idx
                        idx += 1
            return fm
        B, S, Dm = x.shape
        H, Dh = (NUM_HEADS, Dm // NUM_HEADS)
        seg, dil = (SEGMENT_SIZE, DILATION)
        scale = Dh ** (-0.5)
        qkv = (x @ W_qkv).reshape(B, S, 3, H, Dh)
        q = jnp.transpose(qkv[:, :, 0], (0, 2, 1, 3))
        k = jnp.transpose(qkv[:, :, 1], (0, 2, 1, 3))
        v = jnp.transpose(qkv[:, :, 2], (0, 2, 1, 3))
        m = jnp.asarray(hilbert_map(S))
        q, k, v = (q[:, :, m], k[:, :, m], v[:, :, m])
        nseg = S // seg
        qs = q.reshape(B, H, nseg, seg, Dh)
        ks = k.reshape(B, H, nseg, seg, Dh)[:, :, :, ::dil]
        vs = v.reshape(B, H, nseg, seg, Dh)[:, :, :, ::dil]
        scores = jnp.einsum('bhnqd,bhnkd->bhnqk', qs, ks) * scale
        attn = jax.nn.softmax(scores, axis=-1)
        out = jnp.einsum('bhnqk,bhnkd->bhnqd', attn, vs).reshape(B, H, S, Dh)
        inv = jnp.argsort(m)
        out = out[:, :, inv]
        out = jnp.transpose(out, (0, 2, 1, 3)).reshape(B, S, Dm)
        return out @ W_out

    def _L0_ffn_ref(src, Wq, Wk, Wv, Wo, Wsel_v, Wsel_o, ln1_g, ln1_b, ln2_g, ln2_b, W1, b1, W2, b2):
        import jax, jax.numpy as jnp
        import numpy as np
        D, H, P, E, K, F = (512, 16, 64, 8, 2, 2048)
        B, S = (2, 1024)
        NROT = 32
        BASE = 10000.0
        EPS = 1e-05

        def _ln(x, g, b):
            m = jnp.mean(x, -1, keepdims=True)
            v = jnp.mean(jnp.square(x - m), -1, keepdims=True)
            return (x - m) * jax.lax.rsqrt(v + EPS) * g + b

        def _rope(x):
            xr, xp = (x[..., :NROT], x[..., NROT:])
            half = NROT // 2
            inv = BASE ** (-jnp.arange(half, dtype=jnp.float32) / half)
            ang = jnp.arange(x.shape[2], dtype=jnp.float32)[:, None] * inv[None, :]
            cos, sin = (jnp.cos(ang), jnp.sin(ang))
            x1, x2 = (xr[..., :half], xr[..., half:])
            xr = jnp.concatenate([x1 * cos - x2 * sin, x1 * sin + x2 * cos], -1)
            return jnp.concatenate([xr, xp], -1)

        def _gate(x, Wsel):
            s = jax.nn.sigmoid(jnp.einsum('bsd,hed->bhse', x, Wsel))
            _, idx = jax.lax.top_k(s, K)
            mask = jax.nn.one_hot(idx, E, dtype=s.dtype).sum(-2)
            return s * mask

        def _moe_attn(x, Wq, Wk, Wv, Wo, Wsel_v, Wsel_o):
            q = _rope(jnp.einsum('bsd,hdp->bhsp', x, Wq))
            k = _rope(jnp.einsum('bsd,hdp->bhsp', x, Wk))
            gv = _gate(x, Wsel_v)
            v = jnp.einsum('bsd,bhse,hedp->bhsp', x, gv, Wv)
            att = jax.nn.softmax(jnp.einsum('bhsp,bhtp->bhst', q, k) / np.sqrt(P), axis=-1)
            o = jnp.einsum('bhst,bhtp->bhsp', att, v)
            go = _gate(x, Wsel_o)
            return jnp.einsum('bhsp,bhse,hepd->bsd', o, go, Wo)
        src2 = _moe_attn(src, Wq, Wk, Wv, Wo, Wsel_v, Wsel_o)
        src = src + src2
        src = _ln(src, ln1_g, ln1_b)
        src2 = jax.nn.relu(src @ W1 + b1) @ W2 + b2
        src = src + src2
        return _ln(src, ln2_g, ln2_b)
    x = x + _L0_xattn_ref(ctx_1024, ctx_1024, _layernorm(x, axis=-1), mask_BxS2_bk1, L0_xattn_Wq, L0_xattn_bq, L0_xattn_Wk, L0_xattn_bk, L0_xattn_Wv, L0_xattn_bv, L0_xattn_Wo, L0_xattn_bo)
    x = x + _L0_attn_ref(_layernorm(x, axis=-1), L0_attn_W_qkv, L0_attn_W_out)
    x = x + _L0_ffn_ref(_layernorm(x, axis=-1), L0_ffn_Wq, L0_ffn_Wk, L0_ffn_Wv, L0_ffn_Wo, L0_ffn_Wsel_v, L0_ffn_Wsel_o, L0_ffn_ln1_g, L0_ffn_ln1_b, L0_ffn_ln2_g, L0_ffn_ln2_b, L0_ffn_W1, L0_ffn_b1, L0_ffn_W2, L0_ffn_b2)
    return x

_drawn_inputs = setup_inputs


def setup_inputs(seed=0):
    import zlib

    import numpy as np

    out = dict(_drawn_inputs(seed))
    spreads = {'L0_xattn_bq': (0.0, 0.42),
     'L0_xattn_bk': (0.0, 0.8),
     'L0_xattn_bv': (0.0, 0.1),
     'L0_xattn_bo': (0.0, 0.1),
     'L0_ffn_ln1_g': (1.0, 0.2),
     'L0_ffn_ln1_b': (0.0, 0.1),
     'L0_ffn_ln2_g': (1.0, 0.2),
     'L0_ffn_ln2_b': (0.0, 0.1),
     'L0_ffn_b1': (0.0, 0.281),
     'L0_ffn_b2': (0.0, 0.1)}
    factors = {'L0_ffn_Wq': 8.0, 'L0_ffn_Wk': 8.0, 'L0_ffn_Wsel_v': 3.234}
    for name, (base, spread) in spreads.items():
        noise = np.random.default_rng([zlib.crc32(name.encode()), seed]).standard_normal(out[name].shape)
        drawn = base * np.exp(spread * noise) if base else spread * noise
        out[name] = jnp.asarray(drawn.astype(out[name].dtype))
    for name, factor in factors.items():
        out[name] = (out[name] * factor).astype(out[name].dtype)
    return out
```

```python
from contextlib import ExitStack

import concourse.bass as bass
from concourse import mybir
from concourse.alu_op_type import AluOpType as ALU

F32 = mybir.dt.float32
U8 = mybir.dt.uint8
HALF = mybir.dt.bfloat16
ACT = mybir.ActivationFunctionType
AX = mybir.AxisListType

P = 128
B = 8
D = 512
DC = D // P
SK = 2048
H = 16
DH = D // H
HG = P // DH
G = H // HG
EPS = 1e-5
MASKED = 1e30


class Link:

    def __init__(self, eng, sem, base=0):
        self.eng, self.sem, self.base, self.n = eng, sem, base, 0

    def mark(self, ins):
        self.n += 1
        ins.then_inc(self.sem, 1)
        return self.n

    def wait(self, n=None):
        self.eng.wait_ge(self.sem, self.base + (self.n if n is None else n))

    def now(self, ins):
        self.mark(ins)
        self.wait()


def split_product(nc, out, left_hi, left_lo, right_hi, right_lo, first=True, last=True, begun=None):
    n = len(left_hi)
    for c in range(n):
        ins = nc.tensor.matmul(out, left_hi[c], right_hi[c], start=(first and c == 0), stop=False)
        if begun is not None and c == 0:
            ins.then_inc(begun, 1)
        nc.tensor.matmul(out, left_hi[c], right_lo[c], start=False, stop=False)
        ins = nc.tensor.matmul(out, left_lo[c], right_hi[c], start=False, stop=(last and c == n - 1))
    return ins


def cross_attention(nc, x_tokens, identity, t, ctx_dram, mask_dram, x_dram):
    NT, NS, NO = 82, 48, 18
    KC = SK // 512
    with ExitStack() as ctx:
        def sb(name, shape, dt=F32):
            return ctx.enter_context(nc.sbuf_tensor(name, shape, dt))

        def sem(name):
            return ctx.enter_context(nc.semaphore(name))

        weights = {n: [sb(f"xa_{n}_{part}", [P, DC, D], HALF) for part in ("hi", "lo")] for n in ("wq", "wk", "wv", "wo")}
        raw = [sb(f"xa_raw{i}", [P, 4, D]) for i in range(2)]
        bq_col = sb("xa_bq_col", [P, G])
        bk_col = sb("xa_bk_col", [P, G])
        bv_row = sb("xa_bv_row", [P, D])
        bo_row = sb("xa_bo_row", [P, D])
        stats = sb("xa_stats", [P, B, 6])
        mean_var = sb("xa_mean_var", [P, B, 2])
        rstd = sb("xa_rstd", [P, B, 2])
        x_norm = sb("xa_x_norm", [P, D])
        xT = [sb(f"xa_xT_{p}", [P, DC, P], HALF) for p in ("hi", "lo")]
        q_full = sb("xa_q_full", [P, G, P])
        q_heads = [sb(f"xa_q_heads_{p}", [P, G, HG, P], HALF) for p in ("hi", "lo")]
        ctxT = [[sb(f"xa_ctxT{i}_{p}", [P, DC, 512], HALF) for p in ("hi", "lo")] for i in range(2)]
        kT = [sb(f"xa_kT_{p}", [P, G, SK], HALF) for p in ("hi", "lo")]
        v = sb("xa_v", [P, SK // P, H, 2, DH], HALF)
        mask_words = sb("xa_mask_words", [P, SK // 4], mybir.dt.int32)
        pool_one = sb("xa_pool_one", [P, 1])
        mask_add = sb("xa_mask_add", [P, SK])
        probs = [sb(f"xa_probs{i}", [P, SK]) for i in range(2)]
        row_max = sb("xa_row_max", [P, 2, 2])
        neg_max = sb("xa_neg_max", [P, 2])
        row_sum = sb("xa_row_sum", [P, H])
        inv_sum = sb("xa_inv_sum", [P, H])
        pT = [sb(f"xa_pT{i}", [P, 2, SK // P, P], HALF) for i in range(2)]
        o_part = sb("xa_o_part", [P, 2, DH])
        o_tokens = sb("xa_o_tokens", [P, D])
        oT, y = xT, x_norm

        psS = [ctx.enter_context(nc.psum_tensor(f"xa_psS{i}", [P, 2, 512], F32)) for i in range(2)]
        psT = [ctx.enter_context(nc.psum_tensor(f"xa_psT{i}", [P, 512], F32)) for i in range(2)]
        psO = [ctx.enter_context(nc.psum_tensor(f"xa_psO{i}", [P, 512], F32)) for i in range(2)]

        x_in, bias_in, ident_done = sem("xa_x_in"), sem("xa_bias_in"), sem("xa_ident")
        raw_in = [sem(f"xa_raw_in{i}") for i in range(2)]
        raw_used = sem("xa_raw_used")
        mask_in, mask_ready = sem("xa_mask_in"), sem("xa_mask_ready")
        w_hi, w_lo = sem("xa_w_hi"), sem("xa_w_lo")
        var_ready, std_ready = sem("xa_var_ready"), sem("xa_std_ready")
        norm_ready = sem("xa_norm_ready")
        T_full, T_hi, T_free = sem("xa_T_full"), sem("xa_T_hi"), sem("xa_T_free")
        S_full, S_hi, S_free = sem("xa_S_full"), sem("xa_S_hi"), sem("xa_S_free")
        O_full, O_free = sem("xa_O_full"), sem("xa_O_free")
        q_full_ready, q_hi_ready, q_ready = sem("xa_q_full"), sem("xa_q_hi"), sem("xa_q_ready")
        max_ready, probs_ready = sem("xa_max_ready"), sem("xa_probs_ready")
        link_sem, prep_sem, pool_sem = sem("xa_link"), sem("xa_prep"), sem("xa_pool")

        passed = {n: sem(f"xa_passed_{n}") for n in ("sp", "pool", "dve")}

        block = ctx.enter_context(nc.Block())

        @block.sync
        def _(sp):
            sp.dma_start(x_tokens[:], x_dram.rearrange("b p d -> p b d")).then_inc(x_in, 16)
            for i, n in enumerate(("wq", "wk", "wv", "wo")):
                if i >= 2:
                    sp.wait_ge(raw_used, i - 1)
                src = t[n].rearrange("(c p) n -> p c n", p=P) if n == "wo" else t[n].rearrange("(p c) n -> p c n", c=DC)
                sp.dma_start(raw[i % 2][:], src).then_inc(raw_in[i % 2], 16)
            with nc.allow_non_contiguous_dma("two short columns of biases"):
                sp.dma_start(bq_col[:], t["bq"].rearrange("(g p) -> p g", p=P)).then_inc(bias_in, 16)
                sp.dma_start(bk_col[:], t["bk"].rearrange("(g p) -> p g", p=P)).then_inc(bias_in, 16)
            sp.dma_start(bv_row[:], t["bv"].rearrange("(a d) -> a d", a=1).broadcast_to([P, D])).then_inc(bias_in, 16)
            sp.dma_start(bo_row[:], t["bo"].rearrange("(a d) -> a d", a=1).broadcast_to([P, D])).then_inc(bias_in, 16)
            with sp.Fori(0, B) as b:
                sp.wait_ge(mask_ready, b + 1)
                sp.sem_inc(passed["sp"], 1)
                sp.dma_start(mask_words[:], mask_dram[bass.ds(b, 1), :].broadcast_to([P, SK // 4])).then_inc(mask_in, 16)
                for kc in range(KC):
                    sp.wait_ge(raw_used, 4 * b + kc + 3)
                    src = ctx_dram[bass.ds(b, 1), kc * 512:(kc + 1) * 512, :].rearrange("a (k p) d -> p (a k) d", p=P)
                    sp.dma_start(raw[kc % 2][:], src).then_inc(raw_in[kc % 2], 16)

        @block.gpsimd
        def _(pool):
            link = Link(pool, pool_sem)
            link.now(nc.gpsimd.memset(identity[:], 0.0))
            nc.gpsimd.affine_select(out=identity[:], in_=identity[:], compare_op=ALU.not_equal, fill=1.0, base=0,
                                    pattern=[[-1, P]], channel_multiplier=1).then_inc(ident_done, 1)
            nc.gpsimd.memset(pool_one[:], 1.0).then_inc(mask_ready, 1)
            with pool.Fori(0, B) as b:
                pool.wait_ge(mask_in, 16 * b + 16)
                pool.wait_ge(S_free, 48 * b + 2)
                pool.sem_inc(passed["pool"], 1)
                nc.gpsimd.tensor_scalar(mask_add[:], mask_words[:].bitcast(U8), -1.0, MASKED, ALU.add, ALU.mult).then_inc(mask_ready, 1)

        @block.tensor
        def _(pe):
            pe.wait_ge(ident_done, 1)
            with pe.Fori(0, B) as b:
                def T_use(u):
                    pe.wait_ge(T_free, NT * b + u + 1)
                    return psT[u % 2]

                def S_use(u):
                    pe.wait_ge(S_free, NS * b + u + 1)
                    return psS[u % 2]

                def O_use(u):
                    pe.wait_ge(O_free, NO * b + u + 1)
                    return psO[u % 2]

                def transpose_ctx(kc, c):
                    out = T_use(1 + 4 * kc + c)
                    if c == 0:
                        pe.wait_ge(raw_in[kc % 2], 32 * b + 16 * (kc // 2) + 48)
                    for kt in range(4):
                        ins = nc.tensor.transpose(out[:, kt * P:(kt + 1) * P], raw[kc % 2][:, kt, c::DC], identity[:])
                    ins.then_inc(T_full, 1)
                    return ins

                def project_k(kc, gp):
                    out = S_use(4 * kc + gp)
                    pe.wait_ge(T_free, NT * b + 3 + 4 * (kc + 1))
                    for gl in range(2):
                        g = 2 * gp + gl
                        hi, lo = ([w[:, c, g * P:(g + 1) * P] for c in range(DC)] for w in weights["wk"])
                        ins = split_product(nc, out[:, gl, :], hi, lo, [ctxT[kc % 2][0][:, c, :] for c in range(DC)],
                                            [ctxT[kc % 2][1][:, c, :] for c in range(DC)],
                                            begun=raw_used if kc > 0 and g == 0 else None)
                    ins.then_inc(S_full, 1)

                def project_v(kc, kp):
                    out = S_use(4 * kc + 2 + kp)
                    for kl in range(2):
                        kt = 2 * kp + kl
                        hi, lo = ([x[:, c, kt * P:(kt + 1) * P] for c in range(DC)] for x in ctxT[kc % 2])
                        ins = split_product(nc, out[:, kl, :], hi, lo, [weights["wv"][0][:, c, :] for c in range(DC)],
                                            [weights["wv"][1][:, c, :] for c in range(DC)])
                    ins.then_inc(S_full, 1)

                def scores(h, r):
                    out = S_use(16 + 2 * h + r)
                    if h == 0 and r == 0:
                        pe.wait_ge(S_free, NS * b + 18)
                        pe.wait_ge(q_ready, b + 1)
                    g, i = h // HG, h % HG
                    for k in range(2):
                        keys = slice((2 * r + k) * 512, (2 * r + k + 1) * 512)
                        ins = split_product(nc, out[:, k, :], [q_heads[0][:, g, i, :]], [q_heads[1][:, g, i, :]],
                                            [kT[0][:, g, keys]], [kT[1][:, g, keys]])
                    ins.then_inc(S_full, 1)

                def transpose_probs(h, j):
                    out = T_use(17 + 4 * h + j)
                    if j == 0:
                        pe.wait_ge(probs_ready, H * b + h + 1)
                    for k in range(4):
                        kt = 4 * j + k
                        ins = nc.tensor.transpose(out[:, k * P:(k + 1) * P], probs[h % 2][:, kt * P:(kt + 1) * P], identity[:])
                    ins.then_inc(T_full, 1)

                def weigh_values(h):
                    out = O_use(1 + h)
                    for kt in range(SK // P):
                        if kt % 4 == 0:
                            pe.wait_ge(T_free, NT * b + 2 + 17 + 4 * h + kt // 4 + 1)
                        first, last = kt == 0, kt == SK // P - 1
                        both = (pT[h % 2][:, 0, kt, :], v[:, kt, h, :, :], out[:, 0:2 * DH])
                        high = (pT[h % 2][:, 1, kt, :], v[:, kt, h, 0, :], out[:, 0:DH])
                        for n, (left, right, to) in enumerate((high, both) if last else (both, high)):
                            ins = nc.tensor.matmul(to, left, right, start=(first and n == 0), stop=(last and n == 1))
                    ins.then_inc(O_full, 1)

                out = T_use(0)
                pe.wait_ge(norm_ready, b + 1)
                for c in range(DC):
                    ins = nc.tensor.transpose(out[:, c * P:(c + 1) * P], x_norm[:, c::DC], identity[:])
                ins.then_inc(T_full, 1)
                for c in range(DC):
                    transpose_ctx(0, c)
                out = O_use(0)
                pe.wait_ge(w_lo, 4)
                pe.wait_ge(T_free, NT * b + 3)
                for g in range(G):
                    hi, lo = ([w[:, c, g * P:(g + 1) * P] for c in range(DC)] for w in weights["wq"])
                    ins = split_product(nc, out[:, g * P:(g + 1) * P], hi, lo, [xT[0][:, c, :] for c in range(DC)],
                                        [xT[1][:, c, :] for c in range(DC)], begun=raw_used if g == 0 else None)
                ins.then_inc(O_full, 1)
                for kc in range(KC):
                    for c, step in enumerate((project_k, project_k, project_v, project_v)):
                        step(kc, c % 2)
                        if kc < KC - 1:
                            transpose_ctx(kc + 1, c)
                for h in range(2):
                    scores(h, 0)
                    scores(h, 1)
                for h in range(H):
                    transpose_probs(h, 0)
                    transpose_probs(h, 1)
                    if h + 2 < H:
                        scores(h + 2, 0)
                    transpose_probs(h, 2)
                    if h + 2 < H:
                        scores(h + 2, 1)
                    transpose_probs(h, 3)
                    if h >= 1:
                        weigh_values(h - 1)
                weigh_values(H - 1)
                out = T_use(NT - 1)
                pe.wait_ge(O_free, NO * b + 2 + 1 + H)
                for c in range(DC):
                    ins = nc.tensor.transpose(out[:, c * P:(c + 1) * P], o_tokens[:, c * P:(c + 1) * P], identity[:])
                ins.then_inc(T_full, 1)
                out = O_use(NO - 1)
                pe.wait_ge(T_free, NT * b + 2 + NT)
                ins = split_product(nc, out[:], [oT[0][:, c, :] for c in range(DC)], [oT[1][:, c, :] for c in range(DC)],
                                    [weights["wo"][0][:, c, :] for c in range(DC)], [weights["wo"][1][:, c, :] for c in range(DC)])
                ins.then_inc(O_full, 1)

        @block.scalar
        def _(act):
            act.wait_ge(var_ready, 1)
            nc.scalar.activation(rstd[:, :, 0], rstd[:, :, 0], ACT.Sqrt).then_inc(std_ready, 1)
            for i, n in enumerate(("wq", "wk", "wv", "wo")):
                act.wait_ge(raw_in[i % 2], 16 * (i // 2) + 16)
                nc.scalar.copy(weights[n][0][:], raw[i % 2][:]).then_inc(w_hi, 1)
            act.wait_ge(bias_in, 64)
            with act.Fori(0, B) as b:
                def T_high(u, out):
                    act.wait_ge(T_full, NT * b + u + 1)
                    nc.scalar.copy(out, psT[u % 2][:]).then_inc(T_hi, 1)

                def ctx_high(kc, c):
                    T_high(1 + 4 * kc + c, ctxT[kc % 2][0][:, c, :])

                T_high(0, xT[0][:].rearrange("p c k -> p (c k)"))
                for c in range(DC):
                    ctx_high(0, c)
                act.wait_ge(q_full_ready, b + 1)
                for i in range(HG):
                    rows = slice(i * DH, (i + 1) * DH)
                    ins = nc.scalar.copy(q_heads[0][rows, :, i, :], q_full[rows, :, :])
                ins.then_inc(q_hi_ready, 1)
                for kc in range(KC):
                    for s in range(4):
                        act.wait_ge(S_full, NS * b + 4 * kc + s + 1)
                        src = psS[s % 2]
                        if s < 2:
                            for gl in range(2):
                                g = 2 * s + gl
                                ins = nc.scalar.activation(kT[0][:, g, kc * 512:(kc + 1) * 512], src[:, gl, :], ACT.Identity, bias=bk_col[:, g:g + 1])
                        else:
                            kt = 4 * kc + 2 * (s - 2)
                            ins = nc.scalar.copy(v[:, kt:kt + 2, :, 0, :], src[:].rearrange("p k (h d) -> p k h d", d=DH))
                        ins.then_inc(S_hi, 1)
                        if kc < KC - 1:
                            ctx_high(kc + 1, s)
                for h in range(H):
                    act.wait_ge(max_ready, H * b + h + 1)
                    nc.scalar.activation(probs[h % 2][:], probs[h % 2][:], ACT.Exp, bias=neg_max[:, h % 2:h % 2 + 1], scale=1.0,
                                         accum_out=row_sum[:, h:h + 1]).then_inc(probs_ready, 1)
                    for j in range(4):
                        T_high(17 + 4 * h + j, pT[h % 2][:, 0, 4 * j:4 * j + 4, :].rearrange("p k q -> p (k q)"))
                T_high(NT - 1, oT[0][:].rearrange("p c k -> p (c k)"))

        @block.vector
        def _(dve):
            nc.vector.memset(q_heads[0][:], 0.0)
            nc.vector.memset(q_heads[1][:], 0.0)
            nc.vector.memset(row_max[:], 0.0).then_inc(T_free, 2)
            nc.vector.memset(neg_max[:], 0.0).then_inc(S_free, 2)
            nc.vector.memset(o_part[:], 0.0).then_inc(O_free, 2)
            prep = Link(dve, prep_sem)
            dve.wait_ge(x_in, 16)
            for b in range(B):
                prep.mark(nc.vector.bn_stats(stats[:, b, :], x_tokens[:, b, :]))
            prep.wait()
            for b in range(B):
                prep.mark(nc.vector.bn_aggr(mean_var[:, b, :], stats[:, b, :]))
            prep.wait()
            nc.vector.tensor_scalar(rstd[:, :, 0], mean_var[:, :, 1], EPS, None, ALU.add).then_inc(var_ready, 1)
            dve.wait_ge(std_ready, 1)
            prep.now(nc.vector.reciprocal(rstd[:, :, 1], rstd[:, :, 0]))
            for i, n in enumerate(("wq", "wk", "wv", "wo")):
                dve.wait_ge(w_hi, i + 1)
                nc.vector.tensor_tensor(weights[n][1][:], raw[i % 2][:], weights[n][0][:], ALU.subtract)\
                    .then_inc(raw_used, 1)
            nc.vector.memset(row_sum[:], 0.0).then_inc(w_lo, 4)
            dve.wait_ge(bias_in, 64)
            with dve.Fori(0, B) as b:
                link = Link(dve, link_sem, base=(2 * H + 1) * b)

                def T_low(u, out, high):
                    dve.wait_ge(T_hi, NT * b + u + 1)
                    nc.vector.tensor_tensor(out, psT[u % 2][:], high, ALU.subtract).then_inc(T_free, 1)

                def ctx_low(kc, c):
                    T_low(1 + 4 * kc + c, ctxT[kc % 2][1][:, c, :], ctxT[kc % 2][0][:, c, :])

                def mask_scores(h, r):
                    dve.wait_ge(S_full, NS * b + 16 + 2 * h + r + 1)
                    dve.sem_inc(passed["dve"], 1)
                    part = slice(1024 * r, 1024 * (r + 1))
                    nc.vector.tensor_tensor_reduce(probs[h % 2][:, part], psS[r][:].rearrange("p k n -> p (k n)"), mask_add[:, part],
                                                   DH ** -0.5, -3e38, ALU.add, ALU.max, row_max[:, h % 2, r:r + 1]).then_inc(S_free, 1)

                def largest(h):
                    dve.wait_ge(S_free, NS * b + 2 + 16 + 2 * h + 2)
                    nc.vector.tensor_reduce(neg_max[:, h % 2:h % 2 + 1], row_max[:, h % 2, :], AX.X, ALU.max, negate=True).then_inc(max_ready, 1)

                marks = {}

                def inverse(h):
                    marks[h, "inv"] = link.mark(nc.vector.reciprocal(inv_sum[:, h:h + 1], row_sum[:, h:h + 1]))

                def gather_o(h, part):
                    src, add = psO[(1 + h) % 2], bv_row[:, h * DH:(h + 1) * DH]
                    if part == 0:
                        dve.wait_ge(O_full, NO * b + 1 + h + 1)
                        link.wait(marks[h, "inv"])
                        marks[h, "o"] = link.mark(nc.vector.scalar_tensor_tensor(o_part[:, h % 2, :], src[:, 0:DH], inv_sum[:, h:h + 1],
                                                                                 add, ALU.mult, ALU.add))
                    else:
                        link.wait(marks[h, "o"])
                        return nc.vector.scalar_tensor_tensor(o_tokens[:, h * DH:(h + 1) * DH], src[:, DH:2 * DH], inv_sum[:, h:h + 1],
                                                              o_part[:, h % 2, :], ALU.mult, ALU.add).then_inc(O_free, 1)

                dve.wait_ge(O_free, NO * b + 2)
                nc.vector.tensor_scalar(x_norm[:], x_tokens[:, bass.ds(b, 1), :], mean_var[:, bass.ds(b, 1), 0], rstd[:, bass.ds(b, 1), 1],
                                        ALU.subtract, ALU.mult).then_inc(norm_ready, 1)
                T_low(0, xT[1][:].rearrange("p c k -> p (c k)"), xT[0][:].rearrange("p c k -> p (c k)"))
                for c in range(DC):
                    ctx_low(0, c)
                dve.wait_ge(O_full, NO * b + 1)
                nc.vector.tensor_tensor(q_full[:], psO[0][:].rearrange("p (g k) -> p g k", g=G), bq_col[:].unsqueeze(2).to_broadcast([P, G, P]),
                                        ALU.add).then_inc(q_full_ready, 1)
                nc.vector.memset(o_part[:], 0.0).then_inc(O_free, 1)
                dve.wait_ge(q_full_ready, b + 1)
                dve.wait_ge(q_hi_ready, b + 1)
                for i in range(HG):
                    rows = slice(i * DH, (i + 1) * DH)
                    ins = nc.vector.tensor_tensor(q_heads[1][rows, :, i, :], q_full[rows, :, :], q_heads[0][rows, :, i, :], ALU.subtract)
                ins.then_inc(q_ready, 1)
                for kc in range(KC):
                    for s in range(4):
                        dve.wait_ge(S_hi, 16 * b + 4 * kc + s + 1)
                        src = psS[s % 2]
                        if s < 2:
                            for gl in range(2):
                                g = 2 * s + gl
                                keys = slice(kc * 512, (kc + 1) * 512)
                                ins = nc.vector.scalar_tensor_tensor(kT[1][:, g, keys], src[:, gl, :], bk_col[:, g:g + 1], kT[0][:, g, keys],
                                                                     ALU.add, ALU.subtract)
                        else:
                            kt = 4 * kc + 2 * (s - 2)
                            ins = nc.vector.tensor_tensor(v[:, kt:kt + 2, :, 1, :], src[:].rearrange("p k (h d) -> p k h d", d=DH),
                                                          v[:, kt:kt + 2, :, 0, :], ALU.subtract)
                        ins.then_inc(S_free, 1)
                        if kc < KC - 1:
                            ctx_low(kc + 1, s)
                dve.wait_ge(mask_ready, b + 2)
                mask_scores(0, 0)
                mask_scores(0, 1)
                largest(0)
                for h in range(H):
                    if h + 1 < H:
                        mask_scores(h + 1, 0)
                    if h >= 2:
                        gather_o(h - 2, 0)
                    if h + 1 < H:
                        mask_scores(h + 1, 1)
                    if h >= 2:
                        gather_o(h - 2, 1)
                    if h + 1 < H:
                        largest(h + 1)
                    for j in range(4):
                        tiles = slice(4 * j, 4 * j + 4)
                        T_low(17 + 4 * h + j, pT[h % 2][:, 1, tiles, :].rearrange("p k q -> p (k q)"),
                              pT[h % 2][:, 0, tiles, :].rearrange("p k q -> p (k q)"))
                        if j == 0:
                            inverse(h)
                for h in (H - 2, H - 1):
                    gather_o(h, 0)
                    gather_o(h, 1)
                T_low(NT - 1, oT[1][:].rearrange("p c k -> p (c k)"), oT[0][:].rearrange("p c k -> p (c k)"))
                dve.wait_ge(O_full, NO * b + NO)
                link.now(nc.vector.tensor_tensor(y[:], psO[1][:], bo_row[:], ALU.add))
                nc.vector.tensor_tensor(x_tokens[:, bass.ds(b, 1), :], x_tokens[:, bass.ds(b, 1), :], y[:].unsqueeze(1), ALU.add).then_inc(O_free, 1)




class Steps:

    def __init__(self, sem, names):
        self.sem, self.names = sem, names.split()

    def start(self, ins):
        ins.then_inc(self.sem, len(self.names))

    def done(self, eng, name, j=0, before=False):
        eng.wait_ge(self.sem, len(self.names) * (j + (0 if before else 1)) + self.names.index(name) + 1)


def norm_stats_vector(nc, dve, x_tokens, stats, mean_var, rstd, chain, var_ready, std_ready):
    link = Link(dve, chain)
    for b in range(B):
        link.mark(nc.vector.bn_stats(stats[:, b, :], x_tokens[:, b, :]))
    link.wait()
    for b in range(B):
        link.mark(nc.vector.bn_aggr(mean_var[:, b, :], stats[:, b, :]))
    link.wait()
    nc.vector.tensor_scalar(rstd[:, :, 0], mean_var[:, :, 1], EPS, None, ALU.add).then_inc(var_ready, 1)
    dve.wait_ge(std_ready, 1)
    link.now(nc.vector.reciprocal(rstd[:, :, 1], rstd[:, :, 0]))
    return link


def norm_stats_scalar(nc, act, rstd, var_ready, std_ready):
    act.wait_ge(var_ready, 1)
    nc.scalar.activation(rstd[:, :, 0], rstd[:, :, 0], ACT.Sqrt).then_inc(std_ready, 1)


def every_second_key(xT):
    turns = xT[:, :, 0:120].rearrange("p n (r t) -> p n r t", t=24)
    return [(turns[:, :, :, 0:12:2], slice(0, 30)), (turns[:, :, :, 13:24:2], slice(30, 60)), (xT[:, :, 120:128:2], slice(60, 64))]


def segment_attention(nc, x_tokens, identity, w_qkv_dram, w_out_dram):
    SEL = P // 2
    scale = DH ** -0.5
    with ExitStack() as ctx:
        def sb(name, shape, dt=F32):
            return ctx.enter_context(nc.sbuf_tensor(name, shape, dt))

        def sem(name):
            return ctx.enter_context(nc.semaphore(name))

        raw = sb("sa_raw", [P, DC, 3 * D])
        raw_out = sb("sa_raw_out", [P, DC, D])
        w_qkv = [sb(f"sa_w_qkv_{p}", [P, DC, 3 * D], HALF) for p in ("hi", "lo")]
        w_out = [sb(f"sa_w_out_{p}", [P, DC, D], HALF) for p in ("hi", "lo")]
        stats, mean_var, rstd = sb("sa_stats", [P, B, 6]), sb("sa_mean_var", [P, B, 2]), sb("sa_rstd", [P, B, 2])
        x_norm = sb("sa_x_norm", [P, 2, D])
        xT = [sb(f"sa_xT_{p}", [P, DC, 2, P], HALF) for p in ("hi", "lo")]
        x_keys = [sb(f"sa_x_keys_{p}", [P, DC, 2, SEL], HALF) for p in ("hi", "lo")]
        qT = sb("sa_qT", [P, G, 2 * P])
        kT = sb("sa_kT", [P, G, 2 * SEL])
        v = sb("sa_v", [P, D])
        row_max = sb("sa_row_max", [P, HG, 2 * G])
        probs = sb("sa_probs", [P, HG, 2 * G, SEL])
        row_sum, inv_sum = sb("sa_row_sum", [P, HG, 2 * G]), sb("sa_inv_sum", [P, HG, G, 2])
        pT = sb("sa_pT", [P, HG, G, P])
        o_tokens = sb("sa_o_tokens", [P, 2, D])
        oT = [sb(f"sa_oT_{p}", [P, 2, DC, P], HALF) for p in ("hi", "lo")]
        bank = [ctx.enter_context(nc.psum_tensor(f"sa_bank{i}", [P, 512], F32)) for i in range(8)]

        w_in, w_out_in, passed = sem("sa_w_in"), sem("sa_w_out_in"), sem("sa_passed")
        w_hi, w_lo, chain, var_ready, std_ready = (sem(f"sa_{n}") for n in ("w_hi", "w_lo", "chain", "var_ready", "std_ready"))
        made = Steps(sem("sa_made"), "xT0 xT1 q0 q1 k v s0 s1 s2 s3 p0 p1 p2 p3 o0 o1 oT0 oT1 y0 y1")
        by_act = Steps(sem("sa_by_act"), "xT0 xT1 q0 v exp0 exp1 exp2 exp3 pT0 pT2 oT0 oT1")
        by_dve = Steps(sem("sa_by_dve"), "norm xT0 xT1 q1 k max0 max1 sub0 max2 sub1 max3 sub2 sub3 sum0 sum1 sum2 sum3 inv pT1 pT3 o0 o1 "
                                         "oT0 oT1 y0 y1")
        by_pool = Steps(sem("sa_by_pool"), "keys")

        block = ctx.enter_context(nc.Block())

        @block.sync
        def _(sp):
            sp.dma_start(raw[:], w_qkv_dram.rearrange("(p c) n -> p c n", c=DC)).then_inc(w_in, 16)
            sp.dma_start(raw_out[:], w_out_dram.rearrange("(c p) n -> p c n", p=P)).then_inc(w_out_in, 16)

        @block.gpsimd
        def _(pool):
            by_pool.start(nc.gpsimd.memset(pT[:, 0, 0, 0:1], 0.0))
            with pool.Fori(0, B // 2) as j:
                by_dve.done(pool, "xT1", j)
                pool.sem_inc(passed, 1)
                for part in range(2):
                    for src, to in every_second_key(xT[part][:].rearrange("p c l k -> p (c l) k")):
                        dst = x_keys[part][:].rearrange("p c l k -> p (c l) k")[:, :, to]
                        ins = nc.gpsimd.tensor_copy(dst.rearrange("p n (r t) -> p n r t", t=6) if to.stop <= 60 else dst, src)
                ins.then_inc(by_pool.sem, 1)

        @block.tensor
        def _(pe):
            made.start(nc.tensor.matmul(bank[0][0:1, 0:1], identity[:, 0:1], identity[:, 0:1], start=True, stop=True))
            with pe.Fori(0, B // 2) as j:
                for l in range(2):
                    by_dve.done(pe, f"oT{l}", j, before=True)
                    if l == 0:
                        by_dve.done(pe, "norm", j)
                    for c in range(DC):
                        ins = nc.tensor.transpose(bank[l][:, c * P:(c + 1) * P], x_norm[:, l, c::DC], identity[:])
                    ins.then_inc(made.sem, 1)
                pe.wait_ge(w_lo, 2)
                by_dve.done(pe, "xT1", j)
                right = [[x[:, c, :, :].rearrange("p l k -> p (l k)") for c in range(DC)] for x in xT]
                for half in range(2):
                    by_dve.done(pe, f"y{half}", j, before=True)
                    for gl in range(2):
                        g = 2 * half + gl
                        left = [[w[:, c, g * P:(g + 1) * P] for c in range(DC)] for w in w_qkv]
                        ins = split_product(nc, bank[2 + half][:, gl * 2 * P:(gl + 1) * 2 * P], *left, *right)
                    ins.then_inc(made.sem, 1)
                by_pool.done(pe, "keys", j)
                by_act.done(pe, "pT2", j, before=True)
                keys = [[x[:, c, :, :].rearrange("p l k -> p (l k)") for c in range(DC)] for x in x_keys]
                for g in range(G):
                    left = [[w[:, c, D + g * P:D + (g + 1) * P] for c in range(DC)] for w in w_qkv]
                    ins = split_product(nc, bank[4][:, g * P:(g + 1) * P], *left, *keys)
                ins.then_inc(made.sem, 1)
                by_dve.done(pe, "pT3", j, before=True)
                right = [[w[:, c, 2 * D:3 * D] for c in range(DC)] for w in w_qkv]
                split_product(nc, bank[5][:], *keys, *right).then_inc(made.sem, 1)
                by_act.done(pe, "q0", j)
                by_dve.done(pe, "k", j)
                for i in range(HG):
                    by_dve.done(pe, ("o0", "o1", "xT0", "xT1")[i], j, before=i < 2)
                    rows = slice(i * DH, (i + 1) * DH)
                    for g in range(G):
                        for l in range(2):
                            n = 2 * g + l
                            ins = nc.tensor.matmul(bank[(6 + i) % 8][:, n * SEL:(n + 1) * SEL], qT[rows, g, l * P:(l + 1) * P],
                                                   kT[rows, g, l * SEL:(l + 1) * SEL], start=True, stop=True)
                    ins.then_inc(made.sem, 1)
                for i in range(HG):
                    by_act.done(pe, f"exp{i}", j)
                    (by_act if i in (0, 3) else by_dve).done(pe, ("q0", "q1", "k", "v")[i], j)
                    for g in range(G):
                        ins = nc.tensor.transpose(bank[2 + i][:, g * P:(g + 1) * P], probs[:, i, 2 * g:2 * g + 2, :].rearrange("p n k -> p (n k)"), identity[:])
                    ins.then_inc(made.sem, 1)
                by_act.done(pe, "pT2", j)
                by_dve.done(pe, "pT3", j)
                for l in range(2):
                    by_dve.done(pe, f"sub{l}", j)
                    rows = slice(l * SEL, (l + 1) * SEL)
                    for g in range(G):
                        for i in range(HG):
                            cols = slice((HG * g + i) * DH, (HG * g + i + 1) * DH)
                            ins = nc.tensor.matmul(bank[6 + l][:, cols], pT[rows, i, g, :], v[rows, cols], start=True, stop=True)
                    ins.then_inc(made.sem, 1)
                for l in range(2):
                    by_dve.done(pe, f"o{l}", j)
                    for c in range(DC):
                        ins = nc.tensor.transpose(bank[l][:, c * P:(c + 1) * P], o_tokens[:, l, c * P:(c + 1) * P], identity[:])
                    ins.then_inc(made.sem, 1)
                for l in range(2):
                    by_dve.done(pe, f"oT{l}", j)
                    left = [[x[:, l, c, :] for c in range(DC)] for x in oT]
                    right = [[w[:, c, :] for c in range(DC)] for w in w_out]
                    split_product(nc, bank[2 + l][:], *left, *right).then_inc(made.sem, 1)

        @block.scalar
        def _(act):
            norm_stats_scalar(nc, act, rstd, var_ready, std_ready)
            act.wait_ge(w_in, 16)
            by_act.start(nc.scalar.copy(w_qkv[0][:], raw[:]))
            act.wait_ge(w_out_in, 16)
            nc.scalar.copy(w_out[0][:], raw_out[:]).then_inc(w_hi, 1)
            with act.Fori(0, B // 2) as j:
                for l in range(2):
                    made.done(act, f"xT{l}", j)
                    nc.scalar.copy(xT[0][:, :, l, :], bank[l][:].rearrange("p (c k) -> p c k", k=P)).then_inc(by_act.sem, 1)
                made.done(act, "q0", j)
                nc.scalar.copy(qT[:, 0:2, :].rearrange("p g k -> p (g k)"), bank[2][:]).then_inc(by_act.sem, 1)
                made.done(act, "v", j)
                nc.scalar.copy(v[:], bank[5][:]).then_inc(by_act.sem, 1)
                for i in range(HG):
                    by_dve.done(act, f"sub{i}", j)
                    p = probs[:, i, :, :].rearrange("p n k -> p (n k)")
                    nc.scalar.activation(p, p, ACT.Exp, scale=scale).then_inc(by_act.sem, 1)
                for i in (0, 2):
                    made.done(act, f"p{i}", j)
                    nc.scalar.copy(pT[:, i, :, :].rearrange("p g q -> p (g q)"), bank[2 + i][:]).then_inc(by_act.sem, 1)
                for l in range(2):
                    made.done(act, f"oT{l}", j)
                    nc.scalar.copy(oT[0][:, l, :, :].rearrange("p c k -> p (c k)"), bank[l][:]).then_inc(by_act.sem, 1)

        @block.vector
        def _(dve):
            norm_stats_vector(nc, dve, x_tokens, stats, mean_var, rstd, chain, var_ready, std_ready)
            by_dve.start(nc.vector.memset(row_max[:], 0.0))
            dve.wait_ge(w_hi, 1)
            nc.vector.tensor_tensor(w_qkv[1][:], raw[:], w_qkv[0][:], ALU.subtract).then_inc(w_lo, 1)
            nc.vector.tensor_tensor(w_out[1][:], raw_out[:], w_out[0][:], ALU.subtract).then_inc(w_lo, 1)
            with dve.Fori(0, B // 2) as j:
                made.done(dve, "y1", j, before=True)
                for l in range(2):
                    b = bass.ds(2 * j + l, 1)
                    ins = nc.vector.tensor_scalar(x_norm[:, l:l + 1, :], x_tokens[:, b, :], mean_var[:, b, 0], rstd[:, b, 1], ALU.subtract, ALU.mult)
                ins.then_inc(by_dve.sem, 1)
                for l in range(2):
                    by_act.done(dve, f"xT{l}", j)
                    nc.vector.tensor_tensor(xT[1][:, :, l, :], bank[l][:].rearrange("p (c k) -> p c k", k=P), xT[0][:, :, l, :],
                                            ALU.subtract).then_inc(by_dve.sem, 1)
                made.done(dve, "q1", j)
                nc.vector.tensor_copy(qT[:, 2:4, :].rearrange("p g k -> p (g k)"), bank[3][:]).then_inc(by_dve.sem, 1)
                made.done(dve, "k", j)
                nc.vector.tensor_copy(kT[:].rearrange("p g k -> p (g k)"), bank[4][:]).then_inc(by_dve.sem, 1)

                def logits(i):
                    return bank[(6 + i) % 8][:].rearrange("p (n k) -> p n k", k=SEL)

                def largest(i):
                    made.done(dve, f"s{i}", j)
                    nc.vector.tensor_reduce(row_max[:, i, :], logits(i), AX.X, ALU.max).then_inc(by_dve.sem, 1)

                def subtract(i):
                    by_dve.done(dve, f"max{i}", j)
                    nc.vector.tensor_tensor(probs[:, i, :, :], logits(i), row_max[:, i, :].unsqueeze(2).to_broadcast([P, 2 * G, SEL]),
                                            ALU.subtract).then_inc(by_dve.sem, 1)

                largest(0)
                for i in range(1, HG):
                    largest(i)
                    subtract(i - 1)
                subtract(HG - 1)
                for i in range(HG):
                    by_act.done(dve, f"exp{i}", j)
                    nc.vector.tensor_reduce(row_sum[:, i, :], probs[:, i, :, :], AX.X, ALU.add).then_inc(by_dve.sem, 1)
                by_dve.done(dve, f"sum{HG - 1}", j)
                nc.vector.reciprocal(inv_sum[:].rearrange("p i g l -> p (i g l)"), row_sum[:].rearrange("p i n -> p (i n)")).then_inc(by_dve.sem, 1)
                for i in (1, 3):
                    made.done(dve, f"p{i}", j)
                    nc.vector.tensor_copy(pT[:, i, :, :].rearrange("p g q -> p (g q)"), bank[2 + i][:]).then_inc(by_dve.sem, 1)
                for l in range(2):
                    made.done(dve, f"o{l}", j)
                    by_dve.done(dve, "inv", j)
                    nc.vector.tensor_tensor(o_tokens[:, l, :].rearrange("p (g i d) -> p g i d", g=G, i=HG),
                                            bank[6 + l][:].rearrange("p (g i d) -> p g i d", g=G, i=HG),
                                            inv_sum[:, :, :, l].rearrange("p i g -> p g i").unsqueeze(3).to_broadcast([P, G, HG, DH]),
                                            ALU.mult).then_inc(by_dve.sem, 1)
                for l in range(2):
                    by_act.done(dve, f"oT{l}", j)
                    nc.vector.tensor_tensor(oT[1][:, l, :, :].rearrange("p c k -> p (c k)"), bank[l][:],
                                            oT[0][:, l, :, :].rearrange("p c k -> p (c k)"), ALU.subtract).then_inc(by_dve.sem, 1)
                for l in range(2):
                    made.done(dve, f"y{l}", j)
                    b = bass.ds(2 * j + l, 1)
                    nc.vector.tensor_tensor(x_tokens[:, b, :], bank[2 + l][:].unsqueeze(1), x_tokens[:, b, :], ALU.add).then_inc(by_dve.sem, 1)




E = 8
PH = 64
ROT = 32
F = 2048
T = B


def gate_stage(nc, x_tokens, x_norm, xT, gates, identity, wsel_v, wsel_o):
    with ExitStack() as ctx:
        def sb(name, shape, dt=F32):
            return ctx.enter_context(nc.sbuf_tensor(name, shape, dt))

        def sem(name):
            return ctx.enter_context(nc.semaphore(f"ga_{name}"))

        stats, mean_var, rstd = sb("ga_stats", [P, B, 6]), sb("ga_mean_var", [P, B, 2]), sb("ga_rstd", [P, B, 2])
        wsel = sb("ga_wsel", [P, 2, D])
        wselT = sb("ga_wselT", [P, DC, 2 * P])
        xT_full = [sb(f"ga_xT_full{i}", [P, DC, P]) for i in range(2)]
        N = T * 2 * H
        first, rank, left = (sb(f"ga_{n}", [P, N, E]) for n in ("first", "rank", "left"))
        best = sb("ga_best", [P, N])
        order = sb("ga_order", [P, E])
        bank = [ctx.enter_context(nc.psum_tensor(f"ga_bank{i}", [P, 512], F32)) for i in range(8)]
        w_in, chain, var_ready, std_ready, order_ready = (sem(n) for n in ("w_in", "chain", "var_ready", "std_ready", "order"))
        norm_ready, wsel_turned, wsel_ready, turned, full, hi, lo, summed, taken = (
            sem(n) for n in ("norm_ready", "wsel_turned", "wsel_ready", "turned", "full", "hi", "lo", "summed", "taken"))
        block = ctx.enter_context(nc.Block())

        @block.sync
        def _(sp):
            for i, w in enumerate((wsel_v, wsel_o)):
                sp.dma_start(wsel[:, i, :], w.rearrange("h e d -> (h e) d")).then_inc(w_in, 16)

        @block.gpsimd
        def _(pool):
            for e in range(E):
                nc.gpsimd.memset(order[:, e:e + 1], float(E - e)).then_inc(order_ready, 1)

        @block.tensor
        def _(pe):
            pe.wait_ge(w_in, 32)
            for i in range(2):
                for c in range(DC):
                    ins = nc.tensor.transpose(bank[6 + i][:, c * P:(c + 1) * P], wsel[:, i, c::DC], identity[:])
                ins.then_inc(wsel_turned, 1)

            def turn(t):
                pe.wait_ge(norm_ready, t + 1)
                if t >= 4:
                    pe.wait_ge(lo, t - 3)
                for c in range(DC):
                    ins = nc.tensor.transpose(bank[t % 4][:, c * P:(c + 1) * P], x_norm[:, t, c::DC], identity[:])
                ins.then_inc(turned, 1)

            turn(0)
            for t in range(T):
                if t + 1 < T:
                    turn(t + 1)
                if t == 0:
                    pe.wait_ge(wsel_ready, 2)
                pe.wait_ge(full, t + 1)
                if t >= 2:
                    pe.wait_ge(taken, t - 1)
                for c in range(DC):
                    ins = nc.tensor.matmul(bank[4 + t % 2][:, 0:2 * P], xT_full[t % 2][:, c, :], wselT[:, c, :], start=(c == 0), stop=(c == DC - 1))
                ins.then_inc(summed, 1)

        @block.scalar
        def _(act):
            norm_stats_scalar(nc, act, rstd, var_ready, std_ready)

            def take(t):
                act.wait_ge(summed, t + 1)
                nc.scalar.activation(gates[:, t, :, :].rearrange("p n e -> p (n e)"), bank[4 + t % 2][:, 0:2 * P], ACT.Exp, scale=-1.0).then_inc(taken, 1)

            for t in range(T):
                act.wait_ge(turned, t + 1)
                if t >= 2:
                    act.wait_ge(summed, t - 1)
                nc.scalar.copy(xT_full[t % 2][:].rearrange("p c k -> p (c k)"), bank[t % 4][:]).then_inc(full, 1)
                nc.scalar.copy(xT[0][:, :, t * P:(t + 1) * P], bank[t % 4][:].rearrange("p (c k) -> p c k", k=P)).then_inc(hi, 1)
                if t >= 1:
                    take(t - 1)
            take(T - 1)

        @block.vector
        def _(dve):
            norm_stats_vector(nc, dve, x_tokens, stats, mean_var, rstd, chain, var_ready, std_ready)
            for t in range(T):
                nc.vector.tensor_scalar(x_norm[:, t, :], x_tokens[:, t, :], mean_var[:, t, 0:1], rstd[:, t, 1:2], ALU.subtract, ALU.mult).then_inc(norm_ready, 1)
            for i in range(2):
                dve.wait_ge(wsel_turned, i + 1)
                nc.vector.tensor_copy(wselT[:, :, i * P:(i + 1) * P], bank[6 + i][:].rearrange("p (c k) -> p c k", k=P)).then_inc(wsel_ready, 1)
            for t in range(T):
                dve.wait_ge(hi, t + 1)
                tile = slice(t * P, (t + 1) * P)
                nc.vector.tensor_tensor(xT[1][:, :, tile], bank[t % 4][:].rearrange("p (c k) -> p c k", k=P), xT[0][:, :, tile], ALU.subtract).then_inc(lo, 1)
            link = Link(dve, chain, base=2 * B + 1)
            g = gates[:].rearrange("p t n e -> p (t n) e")
            weight = order[:].unsqueeze(1).to_broadcast([P, N, E])

            def spread(row):
                return row[:].unsqueeze(2).to_broadcast([P, N, E])

            dve.wait_ge(taken, T)
            dve.wait_ge(order_ready, E)
            link.now(nc.vector.tensor_scalar(left[:], g, 1.0, None, ALU.add))
            link.now(nc.vector.reciprocal(g, left[:]))
            link.now(nc.vector.tensor_reduce(best[:], g, AX.X, ALU.max))
            link.now(nc.vector.tensor_tensor(rank[:], g, spread(best), ALU.is_equal))
            link.now(nc.vector.tensor_tensor(rank[:], rank[:], weight, ALU.mult))
            link.now(nc.vector.tensor_reduce(best[:], rank[:], AX.X, ALU.max))
            link.now(nc.vector.tensor_tensor(first[:], rank[:], spread(best), ALU.is_equal))
            link.now(nc.vector.scalar_tensor_tensor(left[:].rearrange("p n e -> p (n e)"), first[:].rearrange("p n e -> p (n e)"), -4.0,
                                                    g.rearrange("p n e -> p (n e)"), ALU.mult, ALU.add))
            link.now(nc.vector.tensor_reduce(best[:], left[:], AX.X, ALU.max))
            link.now(nc.vector.tensor_tensor(rank[:], left[:], spread(best), ALU.is_equal))
            link.now(nc.vector.tensor_tensor(rank[:], rank[:], weight, ALU.mult))
            link.now(nc.vector.tensor_reduce(best[:], rank[:], AX.X, ALU.max))
            link.now(nc.vector.tensor_tensor(rank[:], rank[:], spread(best), ALU.is_equal))
            link.now(nc.vector.tensor_tensor(first[:], first[:], rank[:], ALU.add))
            link.now(nc.vector.tensor_tensor(g, g, first[:], ALU.mult))


def expert_values(nc, xT, gates, v, wv_dram):
    with ExitStack() as ctx:
        def sb(name, shape, dt=F32):
            return ctx.enter_context(nc.sbuf_tensor(name, shape, dt))

        def sem(name):
            return ctx.enter_context(nc.semaphore(f"ev_{name}"))

        raw = [sb(f"ev_raw{i}", [P, E, DC, PH]) for i in range(2)]
        w = [[sb(f"ev_w{i}_{p}", [P, E, DC, PH], HALF) for p in ("hi", "lo")] for i in range(2)]
        gated = [sb(f"ev_gated{i}", [P, E, PH]) for i in range(4)]
        bank = [ctx.enter_context(nc.psum_tensor(f"ev_bank{i}", [P, 512], F32)) for i in range(8)]
        raw_in = [sem(f"raw_in{i}") for i in range(2)]
        passed, w_hi, w_ready, made, gated_ready, reduced = (sem(n) for n in ("passed", "w_hi", "w_ready", "made", "gated", "reduced"))
        by = wv_dram.rearrange("h e (q c) p -> h q e (c p)", c=DC)
        block = ctx.enter_context(nc.Block())

        @block.sync
        def _(sp):
            for i in range(2):
                sp.dma_start(raw[i][:].rearrange("q e c p -> q e (c p)"), by[i]).then_inc(raw_in[i], 16)
            with sp.Fori(1, H // 2) as j:
                for i in range(2):
                    sp.wait_ge(w_ready, 2 * j + i - 1)
                    sp.dma_start(raw[i][:].rearrange("q e c p -> q e (c p)"), by[bass.ds(2 * j + i, 1)].rearrange("h q e n -> (h q) e n")).then_inc(raw_in[i], 16)

        @block.gpsimd
        def _(pool):
            with pool.Fori(0, H // 2) as j:
                for i in range(2):
                    pool.wait_ge(raw_in[i], 16 * j + 16)
                    pool.wait_ge(made, T * (2 * j + i) + T)
                    pool.sem_inc(passed, 1)
                    nc.gpsimd.tensor_copy(w[i][0][:], raw[i][:]).then_inc(w_hi, 1)
                    pool.wait_ge(w_hi, 2 * j + i + 1)
                    nc.gpsimd.tensor_tensor(w[i][1][:], raw[i][:], w[i][0][:], ALU.subtract).then_inc(w_ready, 1)

        @block.tensor
        def _(pe):
            with pe.Fori(0, H // 2) as j:
                for i in range(2):
                    pe.wait_ge(w_ready, 2 * j + i + 1)
                    right = [[x[:, :, c, :] for c in range(DC)] for x in w[i]]
                    for t in range(T):
                        pe.wait_ge(gated_ready, T * (2 * j + i) + t + 1)
                        left = [[x[:, c, t * P:(t + 1) * P] for c in range(DC)] for x in xT]
                        split_product(nc, bank[t][:], *left, *right).then_inc(made, 1)

        @block.vector
        def _(dve):
            nc.vector.memset(gated[0][:], 0.0).then_inc(gated_ready, T)
            nc.vector.memset(gated[1][:], 0.0).then_inc(made, 2 * T)
            nc.vector.memset(gated[2][:], 0.0).then_inc(reduced, 4)
            with dve.Fori(0, H // 2) as j:
                for i in range(2):
                    head = bass.ds(2 * j + i, 1)

                    def total(t):
                        dve.wait_ge(gated_ready, T * (2 * j + i) + T + t + 1)
                        nc.vector.tensor_reduce(v[:, t, head, :], gated[t % 4][:].rearrange("p e q -> p q e").unsqueeze(1),
                                                AX.X, ALU.add).then_inc(reduced, 1)

                    for t in range(T):
                        n = T * (2 * j + i) + t
                        dve.wait_ge(made, 2 * T + n + 1)
                        dve.wait_ge(reduced, n + 1)
                        gate = gates[:, t, head, :].unsqueeze(3).to_broadcast([P, 1, E, PH])
                        nc.vector.tensor_tensor(gated[t % 4][:].unsqueeze(1), bank[t][:].rearrange("p (a e q) -> p a e q", a=1, e=E), gate, ALU.mult)\
                            .then_inc(gated_ready, 1)
                        if t >= 1:
                            total(t - 1)
                    total(T - 1)




def rotary_attention(nc, xT, v, identity, wq_dram, wk_dram, cos_dram, sin_dram):
    HALF_ROT = ROT // 2
    with ExitStack() as ctx:
        def sb(name, shape, dt=F32):
            return ctx.enter_context(nc.sbuf_tensor(name, shape, dt))

        def sem(name):
            return ctx.enter_context(nc.semaphore(f"ra_{name}"))

        w = [sb(f"ra_w_{p}", [P, 2 * H, DC, PH], HALF) for p in ("hi", "lo")]
        cos, sin = sb("ra_cos", [P, HALF_ROT]), sb("ra_sin", [P, HALF_ROT])
        qk = sb("ra_qk", [P, 2 * H, PH])
        by_cos, by_sin = (sb(f"ra_by_{n}", [P, 2 * H, 2, HALF_ROT]) for n in ("cos", "sin"))
        qkT = sb("ra_qkT", [P, H, P])
        row_max, row_sum, inv_sum = (sb(f"ra_{n}", [P, H]) for n in ("row_max", "row_sum", "inv_sum"))
        probs = sb("ra_probs", [P, H, P])
        pT = sb("ra_pT", [P, H, P])
        raw = [sb(f"ra_raw{i}", [P, H // 2, DC, PH]) for i in range(2)]
        bank = [ctx.enter_context(nc.psum_tensor(f"ra_bank{i}", [P, 512], F32)) for i in range(8)]
        raw_in = [sem(f"raw_in{i}") for i in range(2)]
        table_in, w_hi, w_lo = sem("table_in"), sem("w_hi"), sem("w_lo")
        qk_made, qk_taken, rotating, rotated = sem("qk_made"), sem("qk_taken"), sem("rotating"), sem("rotated")
        made = Steps(sem("made"), "qkT0 qkT1 qkT2 qkT3 s0 s1 s2 s3 pT0 pT1 pT2 pT3 o0 o1")
        by_act = Steps(sem("by_act"), "qkT0 qkT2 exp0 exp1 exp2 exp3 pT0 pT2")
        by_dve = Steps(sem("by_dve"), "qkT1 qkT3 max0 max1 sub0 max2 sub1 max3 sub2 sub3 sum0 sum1 sum2 sum3 inv pT1 pT3 o0 o1")

        def at(b):
            return bass.ds(b, 1)

        block = ctx.enter_context(nc.Block())

        @block.sync
        def _(sp):
            sp.dma_start(cos[:], cos_dram).then_inc(table_in, 16)
            sp.dma_start(sin[:], sin_dram).then_inc(table_in, 16)
            for n in range(4):
                if n >= 2:
                    sp.wait_ge(w_lo, n - 1)
                src = (wq_dram, wk_dram)[n // 2][8 * (n % 2):8 * (n % 2) + 8].rearrange("h (q c) p -> q h (c p)", c=DC)
                sp.dma_start(raw[n % 2][:].rearrange("q h c p -> q h (c p)"), src).then_inc(raw_in[n % 2], 16)

        @block.tensor
        def _(pe):
            made.start(nc.tensor.matmul(bank[7][0:1, 0:1], identity[:, 0:1], identity[:, 0:1], start=True, stop=True))

            def project(b):
                for n in range(4):
                    if isinstance(b, int):
                        pe.wait_ge(w_lo, n + 1)
                    else:
                        by_dve.done(pe, f"sub{n}", b - 1)
                    for c in range(DC):
                        left = [[x[:, c, b * P:(b + 1) * P] if isinstance(b, int) else x[:, c, bass.ds(b * P, P)]] for x in xT]
                        right = [[x[:, 8 * n:8 * n + 8, c, :]] for x in w]
                        ins = split_product(nc, bank[n][:], *left, *right, first=(c == 0), last=(c == DC - 1))
                    ins.then_inc(qk_made, 1)

            def body(b, last=False):
                pe.wait_ge(rotated, 2 * b + 2)
                for m in range(4):
                    if m < 2:
                        by_dve.done(pe, f"o{m}", b, before=True)
                    else:
                        (by_act if m == 2 else by_dve).done(pe, f"pT{m}", b, before=True)
                    for k in range(4):
                        pair = 4 * m + k
                        ins = nc.tensor.transpose(bank[4 + m][:, k * P:(k + 1) * P], qk[:, 2 * pair:2 * pair + 2, :].rearrange("p h d -> p (h d)"), identity[:])
                    ins.then_inc(made.sem, 1)
                by_act.done(pe, "qkT2", b)
                by_dve.done(pe, "qkT3", b)
                for m in range(4):
                    rows = slice(PH * (m // 2), PH * (m // 2) + PH)
                    for k in range(4):
                        pair = 4 * (m % 2) + k
                        ins = nc.tensor.matmul(bank[m][:, k * P:(k + 1) * P], qkT[rows, pair, :], qkT[rows, H // 2 + pair, :], start=True, stop=True)
                    ins.then_inc(made.sem, 1)
                if not last:
                    project(b + 1)
                for m in range(4):
                    by_act.done(pe, f"exp{m}", b)
                    for k in range(4):
                        ins = nc.tensor.transpose(bank[4 + m][:, k * P:(k + 1) * P], probs[:, 4 * m + k, :], identity[:])
                    ins.then_inc(made.sem, 1)
                by_act.done(pe, "pT2", b)
                by_dve.done(pe, "pT3", b)
                for m in range(2):
                    for k in range(8):
                        h = 8 * m + k
                        right = v[:, b, h, :] if last else v[:, at(b), h, :].rearrange("p a d -> p (a d)")
                        ins = nc.tensor.matmul(bank[4 + m][:, k * PH:(k + 1) * PH], pT[:, h // 2 + 8 * (h % 2), :], right, start=True, stop=True)
                    ins.then_inc(made.sem, 1)

            project(0)
            with pe.Fori(0, B - 1) as b:
                body(b)
            body(B - 1, last=True)

        @block.scalar
        def _(act):
            for n in range(4):
                act.wait_ge(raw_in[n % 2], 16 * (n // 2) + 16)
                nc.scalar.copy(w[0][:, 8 * n:8 * n + 8, :, :], raw[n % 2][:]).then_inc(w_hi, 1)
            act.wait_ge(table_in, 32)
            by_act.start(nc.scalar.copy(inv_sum[:, 0:1], cos[:, 0:1]))

            def take(b):
                for n in range(4):
                    act.wait_ge(qk_made, 4 * b + n + 1)
                    nc.scalar.copy(qk[:, 8 * n:8 * n + 8, :].rearrange("p h d -> p (h d)"), bank[n][:]).then_inc(qk_taken, 1)

            def body(b, last=False):
                for m in (0, 2):
                    made.done(act, f"qkT{m}", b)
                    nc.scalar.copy(qkT[:, 4 * m:4 * m + 4, :].rearrange("p h d -> p (h d)"), bank[4 + m][:]).then_inc(by_act.sem, 1)
                for m in range(4):
                    by_dve.done(act, f"sub{m}", b)
                    p = probs[:, 4 * m:4 * m + 4, :]
                    nc.scalar.activation(p, p, ACT.Exp, scale=PH ** -0.5).then_inc(by_act.sem, 1)
                if not last:
                    take(b + 1)
                for m in (0, 2):
                    made.done(act, f"pT{m}", b)
                    nc.scalar.copy(pT[:, 4 * m:4 * m + 4, :].rearrange("p h q -> p (h q)"), bank[4 + m][:]).then_inc(by_act.sem, 1)

            take(0)
            with act.Fori(0, B - 1) as b:
                body(b)
            body(B - 1, last=True)

        @block.vector
        def _(dve):
            by_dve.start(nc.vector.memset(row_max[:], 0.0))
            for n in range(4):
                dve.wait_ge(w_hi, n + 1)
                nc.vector.tensor_tensor(w[1][:, 8 * n:8 * n + 8, :, :], raw[n % 2][:], w[0][:, 8 * n:8 * n + 8, :, :], ALU.subtract).then_inc(w_lo, 1)
            dve.wait_ge(table_in, 32)

            def rotate(b):
                dve.wait_ge(qk_taken, 4 * b + 4)
                x = qk[:, :, 0:ROT]
                for table, to in ((cos, by_cos), (sin, by_sin)):
                    ins = nc.vector.tensor_tensor(to[:], x.rearrange("p h (a k) -> p h a k", a=2),
                                                  table[:].unsqueeze(1).unsqueeze(1).to_broadcast([P, 2 * H, 2, HALF_ROT]), ALU.mult)
                    ins.then_inc(rotating, 1)
                dve.wait_ge(rotating, 2 * b + 2)
                nc.vector.tensor_tensor(x[:, :, 0:HALF_ROT], by_cos[:, :, 0, :], by_sin[:, :, 1, :], ALU.subtract).then_inc(rotated, 1)
                nc.vector.tensor_tensor(x[:, :, HALF_ROT:ROT], by_cos[:, :, 1, :], by_sin[:, :, 0, :], ALU.add).then_inc(rotated, 1)

            def body(b, last=False):
                for m in (1, 3):
                    made.done(dve, f"qkT{m}", b)
                    nc.vector.tensor_copy(qkT[:, 4 * m:4 * m + 4, :].rearrange("p h d -> p (h d)"), bank[4 + m][:]).then_inc(by_dve.sem, 1)

                def logits(m):
                    return bank[m][:].rearrange("p (h k) -> p h k", k=P)

                def heads(m):
                    return slice(4 * m, 4 * m + 4)

                def largest(m):
                    made.done(dve, f"s{m}", b)
                    nc.vector.tensor_reduce(row_max[:, heads(m)], logits(m), AX.X, ALU.max).then_inc(by_dve.sem, 1)

                def subtract(m):
                    by_dve.done(dve, f"max{m}", b)
                    nc.vector.tensor_tensor(probs[:, heads(m), :], logits(m), row_max[:, heads(m)].unsqueeze(2).to_broadcast([P, 4, P]),
                                            ALU.subtract).then_inc(by_dve.sem, 1)

                largest(0)
                for m in range(1, 4):
                    largest(m)
                    subtract(m - 1)
                subtract(3)
                for m in range(4):
                    by_act.done(dve, f"exp{m}", b)
                    nc.vector.tensor_reduce(row_sum[:, heads(m)], probs[:, heads(m), :], AX.X, ALU.add).then_inc(by_dve.sem, 1)
                by_dve.done(dve, "sum3", b)
                nc.vector.reciprocal(inv_sum[:].rearrange("p (u i) -> p u i", i=2), row_sum[:].rearrange("p (i u) -> p u i", i=2)).then_inc(by_dve.sem, 1)
                for m in (1, 3):
                    made.done(dve, f"pT{m}", b)
                    nc.vector.tensor_copy(pT[:, heads(m), :].rearrange("p h q -> p (h q)"), bank[4 + m][:]).then_inc(by_dve.sem, 1)
                if not last:
                    rotate(b + 1)
                by_dve.done(dve, "inv", b)
                for m in range(2):
                    made.done(dve, f"o{m}", b)
                    out = v[:, b:b + 1, 8 * m:8 * m + 8, :] if last else v[:, at(b), 8 * m:8 * m + 8, :]
                    nc.vector.tensor_tensor(out.rearrange("p a h d -> p (a h) d"), bank[4 + m][:].rearrange("p (h d) -> p h d", d=PH),
                                            inv_sum[:, 8 * m:8 * m + 8].unsqueeze(2).to_broadcast([P, 8, PH]), ALU.mult).then_inc(by_dve.sem, 1)

            rotate(0)
            with dve.Fori(0, B - 1) as b:
                body(b)
            body(B - 1, last=True)


def expert_outputs(nc, x_norm, v, gates, identity, wo_dram):
    with ExitStack() as ctx:
        def sb(name, shape, dt=F32):
            return ctx.enter_context(nc.sbuf_tensor(name, shape, dt))

        def sem(name):
            return ctx.enter_context(nc.semaphore(f"eo_{name}"))

        raw = [sb(f"eo_raw{i}", [P, DC, D]) for i in range(2)]
        w = [[sb(f"eo_w{i}_{p}", [P, DC, D], HALF) for p in ("hi", "lo")] for i in range(4)]
        gated = [sb(f"eo_gated{i}", [P, E, PH]) for i in range(4)]
        start = sb("eo_start", [P, 3])
        gatedT = [[sb(f"eo_gatedT{i}_{p}", [P, DC, P], HALF) for p in ("hi", "lo")] for i in range(4)]
        psT = [ctx.enter_context(nc.psum_tensor(f"eo_psT{i}", [P, 512], F32)) for i in range(4)]
        psY = [ctx.enter_context(nc.psum_tensor(f"eo_psY{i}", [P, 512], F32)) for i in range(4)]
        raw_in = [sem(f"raw_in{i}") for i in range(2)]
        passed, w_hi, w_ready, gated_ready, turned, hi, lo, made, added = (sem(n) for n in ("passed", "w_hi", "w_ready", "gated", "turned", "hi", "lo", "made", "added"))
        NJ = 2 * T
        block = ctx.enter_context(nc.Block())

        @block.sync
        def _(sp):
            for i in range(2):
                sp.dma_start(raw[i][:], wo_dram[i].rearrange("e p n -> (e p) n").rearrange("(c q) n -> q c n", q=P)).then_inc(raw_in[i], 16)
            with sp.Fori(1, H // 2) as j:
                for i in range(2):
                    sp.wait_ge(w_ready, 2 * j + i - 1)
                    src = wo_dram[bass.ds(2 * j + i, 1)].rearrange("a e p n -> (a e p) n").rearrange("(c q) n -> q c n", q=P)
                    sp.dma_start(raw[i][:], src).then_inc(raw_in[i], 16)

        @block.gpsimd
        def _(pool):
            with pool.Fori(0, H // 4) as quad:
                for half in range(2):
                    j = 2 * quad + half
                    for i in range(2):
                        hi_part, lo_part = w[2 * half + i]
                        pool.wait_ge(raw_in[i], 16 * j + 16)
                        pool.wait_ge(made, T * j + T)
                        pool.sem_inc(passed, 1)
                        nc.gpsimd.tensor_copy(hi_part[:], raw[i][:]).then_inc(w_hi, 1)
                        pool.wait_ge(w_hi, 2 * j + i + 1)
                        nc.gpsimd.tensor_tensor(lo_part[:], raw[i][:], hi_part[:], ALU.subtract).then_inc(w_ready, 1)

        @block.tensor
        def _(pe):
            def pair(j, half):
                def turn(n):
                    pe.wait_ge(gated_ready, NJ * j + n + 1)
                    pe.wait_ge(lo, NJ * j + n + 1)
                    flat = gated[n % 4][:].rearrange("p e d -> p (e d)")
                    for c in range(DC):
                        ins = nc.tensor.transpose(psT[n % 4][:, c * P:(c + 1) * P], flat[:, c * P:(c + 1) * P], identity[:])
                    ins.then_inc(turned, 1)

                turn(0)
                turn(1)
                pe.wait_ge(w_ready, 2 * j + 2)
                for t in range(T):
                    pe.wait_ge(added, T * j + t + 1)
                    for i in range(2):
                        n = 2 * t + i
                        if n + 2 < NJ:
                            turn(n + 2)
                        pe.wait_ge(lo, NJ * j + 4 + n + 1)
                        left = [[x[:, c, :] for c in range(DC)] for x in gatedT[n % 4]]
                        right = [[x[:, c, :] for c in range(DC)] for x in w[2 * half + i]]
                        ins = split_product(nc, psY[t % 4][:], *left, *right, first=(i == 0), last=(i == 1))
                    ins.then_inc(made, 1)

            with pe.Fori(0, H // 4) as quad:
                pair(2 * quad, 0)
                pair(2 * quad + 1, 1)

        @block.scalar
        def _(act):
            with act.Fori(0, H // 2) as j:
                for n in range(NJ):
                    act.wait_ge(turned, NJ * j + n + 1)
                    nc.scalar.copy(gatedT[n % 4][0][:].rearrange("p c k -> p (c k)"), psT[n % 4][:]).then_inc(hi, 1)

        @block.vector
        def _(dve):
            nc.vector.memset(start[:, 0:1], 0.0).then_inc(lo, 4)
            nc.vector.memset(start[:, 1:2], 0.0).then_inc(added, 4)
            nc.vector.memset(start[:, 2:3], 0.0).then_inc(made, 2 * T)
            with dve.Fori(0, H // 2) as j:
                def gate(n):
                    t, i = n // 2, n % 2
                    h = bass.ds(2 * j + i, 1)
                    nc.vector.tensor_tensor(gated[n % 4][:].unsqueeze(1), gates[:, t, bass.ds(2 * j + i + H, 1), :].unsqueeze(3).to_broadcast([P, 1, E, PH]),
                                            v[:, t, h, :].unsqueeze(2).to_broadcast([P, 1, E, PH]), ALU.mult).then_inc(gated_ready, 1)

                def add(t):
                    dve.wait_ge(made, T * (j + 2) + t + 1)
                    nc.vector.tensor_tensor(x_norm[:, t, :], x_norm[:, t, :], psY[t % 4][:], ALU.add).then_inc(added, 1)

                dve.wait_ge(added, T * j + 4)
                for n in range(3):
                    gate(n)
                for n in range(NJ):
                    dve.wait_ge(hi, NJ * j + n + 1)
                    nc.vector.tensor_tensor(gatedT[n % 4][1][:].rearrange("p c k -> p (c k)"), psT[n % 4][:],
                                            gatedT[n % 4][0][:].rearrange("p c k -> p (c k)"), ALU.subtract).then_inc(lo, 1)
                    if n + 3 < NJ:
                        gate(n + 3)
                    if n % 2 == 1 and n >= 3:
                        add(n // 2 - 1)
                add(T - 1)


def feed_forward(nc, x_tokens, y, identity, t, out_dram):
    FT = F // P
    with ExitStack() as ctx:
        def sb(name, shape, dt=F32):
            return ctx.enter_context(nc.sbuf_tensor(name, shape, dt))

        def sem(name):
            return ctx.enter_context(nc.semaphore(f"ff_{name}"))

        stats, mean_var, rstd = sb("ff_stats", [P, B, 6]), sb("ff_mean_var", [P, B, 2]), sb("ff_rstd", [P, B, 2])
        rows = {n: sb(f"ff_{n}", [P, D]) for n in ("ln1_g", "ln1_b", "ln2_g", "ln2_b", "b2")}
        b1 = sb("ff_b1", [P, FT])
        w1 = [sb(f"ff_w1_{p}", [P, DC, F], HALF) for p in ("hi", "lo")]
        w2 = [sb(f"ff_w2_{p}", [P, FT, D], HALF) for p in ("hi", "lo")]
        yT = [sb(f"ff_yT_{p}", [P, DC, T * P], HALF) for p in ("hi", "lo")]
        hT = [sb(f"ff_hT_{p}", [P, FT, T * P], HALF) for p in ("hi", "lo")]
        raw = [sb(f"ff_raw{i}", [P, F // 2]) for i in range(2)]
        relu = [sb(f"ff_relu{i}", [P, 512]) for i in range(2)]
        bank = [ctx.enter_context(nc.psum_tensor(f"ff_bank{i}", [P, 512], F32)) for i in range(8)]
        raw_in = [sem(f"raw_in{i}") for i in range(2)]
        names = ("passed", "rows_in", "chain", "var_ready", "std_ready", "chain2", "var2_ready", "std2_ready", "w_hi", "w_lo", "normed", "turned", "turned_hi",
                 "turned_lo", "hidden", "rectified", "hidden_hi", "hidden_lo", "made", "stored", "bank_free", "ended")
        s = {n: sem(n) for n in names}
        NW = 16
        block = ctx.enter_context(nc.Block())

        def piece(i):
            if i < 8:
                c, half = i // 2, i % 2
                cols = slice(half * (F // 2), (half + 1) * (F // 2))
                return t["W1"].rearrange("(p c) n -> p c n", c=DC)[:, c, cols], [x[:, c, cols] for x in w1]
            n = i - 8
            return t["W2"].rearrange("(f p) n -> p f n", p=P)[:, 2 * n:2 * n + 2, :], [x[:, 2 * n:2 * n + 2, :].rearrange("p f n -> p (f n)") for x in w2]

        @block.sync
        def _(sp):
            for i in range(NW):
                if i >= 2:
                    sp.wait_ge(s["w_lo"], i - 1)
                src = piece(i)[0]
                to = raw[i % 2][:] if i < 8 else raw[i % 2][:].rearrange("p (f n) -> p f n", n=D)
                sp.dma_start(to, src).then_inc(raw_in[i % 2], 16)
                if i == 1:
                    for n, row in rows.items():
                        sp.dma_start(row[:], t[n].rearrange("(a d) -> a d", a=1).broadcast_to([P, D])).then_inc(s["rows_in"], 16)
                    with nc.allow_non_contiguous_dma("a short column of biases"):
                        sp.dma_start(b1[:], t["b1"].rearrange("(f p) -> p f", p=P)).then_inc(s["rows_in"], 16)
            for b in range(B):
                sp.wait_ge(s["ended"], b + 1)
                sp.dma_start(out_dram[b], x_tokens[:, b, :]).then_inc(s["stored"], 16)
            sp.wait_ge(s["stored"], 16 * B)

        @block.gpsimd
        def _(pool):
            for i in range(NW):
                hi, lo = piece(i)[1]
                if i >= 8:
                    pool.wait_ge(raw_in[i % 2], 16 * (i // 2) + 16)
                    nc.gpsimd.tensor_copy(hi, raw[i % 2][:]).then_inc(s["w_hi"], 1)
                pool.wait_ge(s["w_hi"], i + 1)
                nc.gpsimd.tensor_tensor(lo, raw[i % 2][:], hi, ALU.subtract).then_inc(s["w_lo"], 1)

        @block.tensor
        def _(pe):
            for b in range(T):
                pe.wait_ge(s["normed"], b + 1)
                if b >= 2:
                    pe.wait_ge(s["turned_lo"], b - 1)
                for c in range(DC):
                    ins = nc.tensor.transpose(bank[b % 2][:, c * P:(c + 1) * P], y[:, b, c::DC], identity[:])
                ins.then_inc(s["turned"], 1)
            pe.wait_ge(s["turned_lo"], T)
            pe.wait_ge(s["w_lo"], 8)
            with pe.Fori(0, FT) as f:
                for half in range(2):
                    pe.wait_ge(s["bank_free"], 2 * f + half + 1)
                    left = [[x[:, c, bass.ds(f * P, P)] for c in range(DC)] for x in w1]
                    right = [[x[:, c, half * 512:(half + 1) * 512] for c in range(DC)] for x in yT]
                    split_product(nc, bank[2 + half][:], *left, *right).then_inc(s["hidden"], 1)
            pe.wait_ge(s["hidden_lo"], 2 + 2 * FT)
            pe.wait_ge(s["w_lo"], NW)
            for b in range(T):
                if b >= 4:
                    pe.wait_ge(s["chain2"], 2 * (b - 4) + 1)
                left = [[x[:, f, b * P:(b + 1) * P] for f in range(FT)] for x in hT]
                right = [[x[:, f, :] for f in range(FT)] for x in w2]
                split_product(nc, bank[4 + b % 4][:], *left, *right).then_inc(s["made"], 1)

        @block.scalar
        def _(act):
            norm_stats_scalar(nc, act, rstd, s["var_ready"], s["std_ready"])

            def weights(pieces):
                for i in pieces:
                    act.wait_ge(raw_in[i % 2], 16 * (i // 2) + 16)
                    nc.scalar.copy(piece(i)[1][0], raw[i % 2][:]).then_inc(s["w_hi"], 1)

            weights(range(2))
            for b in range(T):
                act.wait_ge(s["turned"], b + 1)
                nc.scalar.copy(yT[0][:, :, b * P:(b + 1) * P], bank[b % 2][:].rearrange("p (c k) -> p c k", k=P)).then_inc(s["turned_hi"], 1)
            weights(range(2, 8))
            act.wait_ge(s["rows_in"], 96)
            with act.Fori(0, FT) as f:
                for half in range(2):
                    cols = slice(half * 512, (half + 1) * 512)
                    act.wait_ge(s["hidden"], 2 * f + half + 1)
                    act.wait_ge(s["hidden_lo"], 2 * f + half + 1)
                    act.sem_inc(s["passed"], 1)
                    nc.scalar.activation(relu[half][:], bank[2 + half][:], ACT.Relu, bias=b1[:, bass.ds(f, 1)]).then_inc(s["bank_free"], 1)
                    act.wait_ge(s["bank_free"], 2 * f + half + 3)
                    nc.scalar.copy(hT[0][:, bass.ds(f, 1), cols], relu[half][:].unsqueeze(1)).then_inc(s["hidden_hi"], 1)
            act.wait_ge(s["var2_ready"], 1)
            nc.scalar.activation(rstd[:, :, 0], rstd[:, :, 0], ACT.Sqrt).then_inc(s["std2_ready"], 1)

        @block.vector
        def _(dve):
            nc.vector.memset(relu[0][:], 0.0).then_inc(s["bank_free"], 2)
            nc.vector.memset(relu[1][:], 0.0).then_inc(s["hidden_lo"], 2)
            link = norm_stats_vector(nc, dve, y, stats, mean_var, rstd, s["chain"], s["var_ready"], s["std_ready"])
            dve.wait_ge(s["rows_in"], 96)
            for b in range(B):
                link.mark(nc.vector.tensor_scalar(y[:, b, :], y[:, b, :], mean_var[:, b, 0:1], rstd[:, b, 1:2], ALU.subtract, ALU.mult))
            link.wait()
            for b in range(B):
                link.mark(nc.vector.tensor_tensor(y[:, b, :], y[:, b, :], rows["ln1_g"][:], ALU.mult))
            link.wait()
            for b in range(B):
                nc.vector.tensor_tensor(y[:, b, :], y[:, b, :], rows["ln1_b"][:], ALU.add).then_inc(s["normed"], 1)
            for b in range(T):
                tile = slice(b * P, (b + 1) * P)
                dve.wait_ge(s["turned_hi"], b + 1)
                nc.vector.tensor_tensor(yT[1][:, :, tile], bank[b % 2][:].rearrange("p (c k) -> p c k", k=P), yT[0][:, :, tile], ALU.subtract).then_inc(s["turned_lo"], 1)
            with dve.Fori(0, FT) as f:
                for half in range(2):
                    cols = slice(half * 512, (half + 1) * 512)
                    dve.wait_ge(s["hidden_hi"], 2 * f + half + 1)
                    nc.vector.tensor_tensor(hT[1][:, bass.ds(f, 1), cols], relu[half][:].unsqueeze(1), hT[0][:, bass.ds(f, 1), cols], ALU.subtract)\
                        .then_inc(s["hidden_lo"], 1)
            for b in range(T):
                dve.wait_ge(s["made"], b + 1)
                nc.vector.tensor_tensor(y[:, b, :], y[:, b, :], bank[4 + b % 4][:], ALU.add).then_inc(s["chain2"], 1)
                dve.wait_ge(s["chain2"], 2 * b + 1)
                nc.vector.tensor_tensor(y[:, b, :], y[:, b, :], rows["b2"][:], ALU.add).then_inc(s["chain2"], 1)
            dve.wait_ge(s["chain2"], 2 * T)
            link = Link(dve, s["chain"], base=link.n)
            for b in range(B):
                link.mark(nc.vector.bn_stats(stats[:, b, :], y[:, b, :]))
            link.wait()
            for b in range(B):
                link.mark(nc.vector.bn_aggr(mean_var[:, b, :], stats[:, b, :]))
            link.wait()
            nc.vector.tensor_scalar(rstd[:, :, 0], mean_var[:, :, 1], EPS, None, ALU.add).then_inc(s["var2_ready"], 1)
            dve.wait_ge(s["std2_ready"], 1)
            link.now(nc.vector.reciprocal(rstd[:, :, 1], rstd[:, :, 0]))
            for b in range(B):
                link.mark(nc.vector.tensor_scalar(y[:, b, :], y[:, b, :], mean_var[:, b, 0:1], rstd[:, b, 1:2], ALU.subtract, ALU.mult))
            link.wait()
            for b in range(B):
                link.mark(nc.vector.tensor_tensor(y[:, b, :], y[:, b, :], rows["ln2_g"][:], ALU.mult))
            link.wait()
            for b in range(B):
                link.mark(nc.vector.tensor_tensor(y[:, b, :], y[:, b, :], rows["ln2_b"][:], ALU.add))
            link.wait()
            for b in range(B):
                nc.vector.tensor_tensor(x_tokens[:, b, :], x_tokens[:, b, :], y[:, b, :], ALU.add).then_inc(s["ended"], 1)




def perceiver(nc, x, ctx_1024, mask, t, cos, sin, out):
    xattn, ffn = ({k[len(pre):].replace("W", "w") if pre == "L0_xattn_" else k[len(pre):]: v for k, v in t.items() if k.startswith(pre)}
                  for pre in ("L0_xattn_", "L0_ffn_"))
    with ExitStack() as ctx:
        def sb(name, shape, dt=F32):
            return ctx.enter_context(nc.sbuf_tensor(name, shape, dt))

        x_tokens = sb("x_tokens", [P, B, D])
        identity = sb("identity", [P, P])
        cross_attention(nc, x_tokens, identity, xattn, ctx_1024, mask, x)
        segment_attention(nc, x_tokens, identity, t["L0_attn_W_qkv"], t["L0_attn_W_out"])
        x_norm = sb("x_norm", [P, T, D])
        with ExitStack() as moe:
            xT = [moe.enter_context(nc.sbuf_tensor(f"xT_{p}", [P, DC, T * P], HALF)) for p in ("hi", "lo")]
            gates = moe.enter_context(nc.sbuf_tensor("gates", [P, T, 2 * H, E], F32))
            v = moe.enter_context(nc.sbuf_tensor("v", [P, T, H, PH], F32))
            gate_stage(nc, x_tokens, x_norm, xT, gates, identity, ffn["Wsel_v"], ffn["Wsel_o"])
            expert_values(nc, xT, gates, v, ffn["Wv"])
            rotary_attention(nc, xT, v, identity, ffn["Wq"], ffn["Wk"], cos, sin)
            expert_outputs(nc, x_norm, v, gates, identity, ffn["Wo"])
        feed_forward(nc, x_tokens, x_norm, identity, ffn, out)


def kernel(**inputs):
    import numpy as _np
    import concourse.bacc as _bacc
    from concourse import mybir as _mybir
    from concourse.bass_utils import run_bass_kernel_spmd as _run

    nc = _bacc.Bacc("TRN2", target_bir_lowering=False, num_devices=1)
    arrays = {name: _np.ascontiguousarray(a) for name, a in inputs.items()}
    arrays["mask_BxS2_bk1"] = arrays["mask_BxS2_bk1"].view(_np.int32)
    freq = _np.float32(10000.0) ** (-_np.arange(ROT // 2, dtype=_np.float32) / _np.float32(ROT // 2))
    angle = _np.arange(P, dtype=_np.float32)[:, None] * freq[None, :]
    arrays["rope_cos"], arrays["rope_sin"] = _np.cos(angle), _np.sin(angle)
    args = {name: nc.dram_tensor(f"in_{name}", a.shape, _mybir.dt.from_np(a.dtype), kind="ExternalInput").ap() for name, a in arrays.items()}
    out = nc.dram_tensor("out_x", (B, P, D), F32, kind="ExternalOutput").ap()
    x, context, mask, cos, sin = (args.pop(n) for n in ("x", "ctx_1024", "mask_BxS2_bk1", "rope_cos", "rope_sin"))
    perceiver(nc, x, context, mask, args, cos, sin, out)
    return _run(nc, [{f"in_{name}": a for name, a in arrays.items()}], core_ids=[0]).results[0]["out_x"]
```

```python
from contextlib import ExitStack

import concourse.bass as bass
from concourse import mybir
from concourse.alu_op_type import AluOpType as ALU

F32 = mybir.dt.float32
U8 = mybir.dt.uint8
HALF = mybir.dt.bfloat16
ACT = mybir.ActivationFunctionType
AX = mybir.AxisListType

P = 128
B = 8
D = 512
DC = D // P
SK = 2048
H = 16
DH = D // H
HG = P // DH
G = H // HG
EPS = 1e-5
MASKED = 1e30


class Link:

    def __init__(self, eng, sem, base=0):
        self.eng, self.sem, self.base, self.n = eng, sem, base, 0

    def mark(self, ins):
        self.n += 1
        ins.then_inc(self.sem, 1)
        return self.n

    def wait(self, n=None):
        self.eng.wait_ge(self.sem, self.base + (self.n if n is None else n))

    def now(self, ins):
        self.mark(ins)
        self.wait()


def split_product(nc, out, left_hi, left_lo, right_hi, right_lo, first=True, last=True, begun=None):
    n = len(left_hi)
    for c in range(n):
        ins = nc.tensor.matmul(out, left_hi[c], right_hi[c], start=(first and c == 0), stop=False)
        if begun is not None and c == 0:
            ins.then_inc(begun, 1)
        nc.tensor.matmul(out, left_hi[c], right_lo[c], start=False, stop=False)
        ins = nc.tensor.matmul(out, left_lo[c], right_hi[c], start=False, stop=(last and c == n - 1))
    return ins


def cross_order(last):
    for h in range(H):
        nxt = not (last and h == H - 1)
        half = 1 - h // (H // 2)
        pieces = [2 * (h % (H // 2)), 2 * (h % (H // 2)) + 1] if half == 1 or not last else []
        extra = [2 * (h - 2), 2 * (h - 2) + 1] if 2 <= h < 10 and not last else []
        if nxt:
            for j in range(3):
                yield "score", (h + 1) % H, j
        yield "turn", h, 0
        if nxt:
            yield "score", (h + 1) % H, 3
        yield "turn", h, 1
        if extra:
            yield "context", extra[0], 0
        if nxt:
            yield "exp", (h + 1) % H, 0
        if h:
            yield "gather", h - 1, 0
        if h == 10 and not last:
            yield "norm", 0, 0
        if pieces:
            yield "project", half, pieces[0]
        yield "turn", h, 2
        yield "values", h, 0
        yield "turn", h, 3
        yield "values", h, 1
        if h == 5:
            yield "queries", 1, 0
        if h == 12 and not last:
            yield "queries", 0, 0
        if pieces and h < H - 1:
            yield "project", half, pieces[1]
        yield "values", h, 2
        if extra:
            yield "context", extra[1], 0
        if h == 10 and not last:
            yield "latents", 0, 0
        yield "values", h, 3
    yield "gather", H - 1, 0
    if not last:
        yield "project", half, pieces[1]
    yield "output", 0, 0


def cross_start():
    yield "latents", 0, 0
    for piece in range(4):
        yield "context", piece, 0
    yield "queries", 0, 0
    for piece in range(16):
        if piece < 12:
            yield "context", piece + 4, 0
        yield "project", 0, piece
    for j in range(4):
        yield "score", 0, j
    yield "exp", 0, 0


POOL_OF = {"score": "S", "turn": "T", "context": "T", "latents": "T", "project": "P", "queries": "P"}


class Walk:

    def __init__(self, items, base, odd):
        self.items, self.base, self.odd, self.n, self.at = list(items), base, odd, {k: 0 for k in base}, {}

    def __iter__(self):
        for kind, a, k in self.items:
            pools = ("T", "O") if kind == "output" else ("O",) if kind == "values" and k == 0 else (POOL_OF[kind],) if kind in POOL_OF else ()
            self.use = {p: self.base[p] + self.n[p] for p in pools}
            self.parity = {p: (self.odd[p] + self.n[p]) % 2 for p in pools}
            for p in pools:
                self.n[p] += 1
                self.at[kind, a, k] = self.base[p] + self.n[p]
            yield kind, a, k


def cross_attention(nc, x_tokens, identity, t, ctx_dram, mask_dram, x_dram):
    KEYS = SK // 8
    none = {p: 0 for p in "STPO"}
    count, turned = {p: {} for p in "STPO"}, {}
    for name, items in (("start", cross_start()), ("round", cross_order(False))):
        w = Walk(items, none, none)
        for _ in w:
            pass
        for p in "STPO":
            count[p][name] = w.n[p]
        turned[name] = [w.at["context", 2 * e + 1, 0] for e in range(8)]

    def walk(b):
        if b is None:
            return Walk(cross_start(), none, none)
        return Walk(cross_order(isinstance(b, int)), {p: count[p]["start"] + count[p]["round"] * b for p in "STPO"},
                    {p: count[p]["start"] % 2 for p in "STPO"})

    with ExitStack() as ctx:
        def sb(name, shape, dt=F32):
            return ctx.enter_context(nc.sbuf_tensor(name, shape, dt))

        def sem(name):
            return ctx.enter_context(nc.semaphore(f"xa_{name}"))

        weights = {n: [sb(f"xa_{n}_{part}", [P, DC, D], HALF) for part in ("hi", "lo")] for n in ("wq", "wk", "wv", "wo")}
        raw = [sb(f"xa_raw{i}", [P, 2, D]) for i in range(2)]
        bq_col, bk_col = sb("xa_bq_col", [P, G]), sb("xa_bk_col", [P, G])
        bv_row, bo_row = sb("xa_bv_row", [P, D]), sb("xa_bo_row", [P, D])
        stats, mean_var, rstd = sb("xa_stats", [P, B, 6]), sb("xa_mean_var", [P, B, 2]), sb("xa_rstd", [P, B, 2])
        x_norm = sb("xa_x_norm", [P, D])
        xT = [sb(f"xa_xT_{p}", [P, DC, P], HALF) for p in ("hi", "lo")]
        q_full = sb("xa_q_full", [P, 2, P])
        q_heads = [sb(f"xa_q_heads_{p}", [P, G, HG, P], HALF) for p in ("hi", "lo")]
        ctxT = [sb(f"xa_ctxT_{p}", [P, DC, SK], HALF) for p in ("hi", "lo")]
        kT = [sb(f"xa_kT_{p}", [P, G, SK], HALF) for p in ("hi", "lo")]
        v = sb("xa_v", [P, SK // P, H, 2, DH], HALF)
        mask_words = sb("xa_mask_words", [P, SK // 4], mybir.dt.int32)
        mask_add = sb("xa_mask_add", [P, SK], mybir.dt.bfloat16)
        probs = [sb(f"xa_probs{i}", [P, SK]) for i in range(2)]
        row_max, neg_max = sb("xa_row_max", [P, 2, 4]), sb("xa_neg_max", [P, 2])
        row_sum, inv_sum = sb("xa_row_sum", [P, H]), sb("xa_inv_sum", [P, H])
        pT = [sb(f"xa_pT_{p}", [P, SK // P, P], HALF) for p in ("hi", "lo")]
        o_part = sb("xa_o_part", [P, 2, DH])
        o_tokens = sb("xa_o_tokens", [P, D])
        oT = [sb(f"xa_oT_{p}", [P, DC, P], HALF) for p in ("hi", "lo")]
        start = sb("xa_start", [P, 6])
        y = x_norm

        psS = [ctx.enter_context(nc.psum_tensor(f"xa_psS{i}", [P, 512], F32)) for i in range(3)]
        psP = [ctx.enter_context(nc.psum_tensor(f"xa_psP{i}", [P, 512], F32)) for i in range(2)]
        psT = [ctx.enter_context(nc.psum_tensor(f"xa_psT{i}", [P, 512], F32)) for i in range(2)]
        psO = ctx.enter_context(nc.psum_tensor("xa_psO", [P, 512], F32))

        x_in, bias_in, ident_done = sem("x_in"), sem("bias_in"), sem("ident")
        w_in = [sem(f"w_in{i}") for i in range(4)]
        w_hi, w_lo = sem("w_hi"), sem("w_lo")
        raw_in = [sem(f"raw_in{i}") for i in range(2)]
        mask_in, mask_ready = sem("mask_in"), sem("mask_ready")
        var_ready, std_ready, norm_ready = sem("var_ready"), sem("std_ready"), sem("norm_ready")
        full = {p: sem(f"{p}_full") for p in "STPO"}
        high = {p: sem(f"{p}_high") for p in "TP"}
        free = {p: sem(f"{p}_free") for p in "STPO"}
        q_sum, q_hi, q_ready = sem("q_sum"), sem("q_hi"), sem("q_ready")
        max_ready, probs_ready = sem("max_ready"), sem("probs_ready")
        link_sem, prep_sem, pool_sem = sem("link"), sem("prep"), sem("pool")
        passed = {n: sem(f"passed_{n}") for n in ("sp", "pool", "dve")}

        def batch(b):
            return -1 if b is None else b

        def queries_of(b, half):
            return 1 if b is None else 2 * b + (2 if half else 3)

        def piece(half, i):
            kc, r = i // 4, i % 4
            return ("k", 2 * half + r, kc) if r < 2 else ("v", 4 * kc + 2 * (r - 2), kc)

        w_raw = [probs[i][:].rearrange("p (c n) -> p c n", c=DC) for i in range(2)]

        block = ctx.enter_context(nc.Block())

        @block.sync
        def _(sp):
            sp.dma_start(x_tokens[:], x_dram.rearrange("b p d -> p b d")).then_inc(x_in, 16)

            def load_context(b, e):
                if isinstance(b, int):
                    if e >= 2:
                        sp.wait_ge(full["T"], turned["start"][e - 2])
                else:
                    sp.wait_ge(full["T"], count["T"]["start"] + count["T"]["round"] * (b - 1) + (turned["round"][e - 2] if e >= 2 else 0))
                    sp.sem_inc(passed["sp"], 1)
                src = ctx_dram[b:b + 1] if isinstance(b, int) else ctx_dram[bass.ds(b, 1)]
                src = src[:, e * KEYS:(e + 1) * KEYS, :].rearrange("a (k p) d -> p (a k) d", p=P)
                sp.dma_start(raw[e % 2][:], src).then_inc(raw_in[e % 2], 16)

            def load_mask(b):
                sp.wait_ge(mask_ready, b + 1)
                sp.sem_inc(passed["sp"], 1)
                sp.dma_start(mask_words[:], mask_dram[b:b + 1, :].broadcast_to([P, SK // 4]) if isinstance(b, int) else
                             mask_dram[bass.ds(b, 1), :].broadcast_to([P, SK // 4])).then_inc(mask_in, 16)

            for i, n in enumerate(("wq", "wk", "wv", "wo")):
                if i >= 2:
                    sp.wait_ge(w_lo, i - 1)
                src = t[n].rearrange("(c p) n -> p c n", p=P) if n == "wo" else t[n].rearrange("(p c) n -> p c n", c=DC)
                sp.dma_start(w_raw[i % 2], src).then_inc(w_in[i], 16)
                if i == 1:
                    load_context(0, 0)
                    load_context(0, 1)
                    with nc.allow_non_contiguous_dma("two short columns of biases"):
                        sp.dma_start(bq_col[:], t["bq"].rearrange("(g p) -> p g", p=P)).then_inc(bias_in, 16)
                        sp.dma_start(bk_col[:], t["bk"].rearrange("(g p) -> p g", p=P)).then_inc(bias_in, 16)
                    sp.dma_start(bv_row[:], t["bv"].rearrange("(a d) -> a d", a=1).broadcast_to([P, D])).then_inc(bias_in, 16)
                    sp.dma_start(bo_row[:], t["bo"].rearrange("(a d) -> a d", a=1).broadcast_to([P, D])).then_inc(bias_in, 16)
            load_mask(0)
            for e in range(2, 8):
                load_context(0, e)
            with sp.Fori(1, B) as b:
                for e in range(8):
                    load_context(b, e)
                load_mask(b)

        @block.gpsimd
        def _(pool):
            link = Link(pool, pool_sem)
            link.now(nc.gpsimd.memset(identity[:], 0.0))
            nc.gpsimd.affine_select(out=identity[:], in_=identity[:], compare_op=ALU.not_equal, fill=1.0, base=0,
                                    pattern=[[-1, P]], channel_multiplier=1).then_inc(ident_done, 1)
            nc.gpsimd.memset(start[:, 0:1], 0.0).then_inc(mask_ready, 1)
            with pool.Fori(0, B) as b:
                pool.wait_ge(mask_in, 16 * b + 16)
                pool.wait_ge(free["S"], count["S"]["round"] * b + 1)
                pool.sem_inc(passed["pool"], 1)
                nc.gpsimd.tensor_scalar(mask_add[:], mask_words[:].bitcast(U8), -1.0, MASKED, ALU.add, ALU.mult).then_inc(mask_ready, 1)

        @block.tensor
        def _(pe):
            pe.wait_ge(ident_done, 1)

            def bank(pool, w):
                u = w.use[pool]
                pe.wait_ge(free[pool], u + 1)
                return {"T": psT, "P": psP}[pool][w.parity[pool]] if pool in "TP" else psO

            def run(b):
                w = walk(b)
                for kind, a, k in w:
                    if kind == "score":
                        h, j = a, k
                        out = psS[j % 3]
                        if j in (0, 3):
                            pe.wait_ge(free["S"], w.use["S"] - (2 if j == 3 else 0) + 1)
                        if h % (H // 2) == 0:
                            pe.wait_ge(free["P"], w.at["project", h // (H // 2), 4 * j + 1] + 2)
                            if j == 0:
                                pe.wait_ge(q_ready, queries_of(b, h // (H // 2)))
                        g, i = h // HG, h % HG
                        keys = slice(512 * j, 512 * (j + 1))
                        split_product(nc, out[:], [q_heads[0][:, g, i, :]], [q_heads[1][:, g, i, :]], [kT[0][:, g, keys]], [kT[1][:, g, keys]])\
                            .then_inc(full["S"], 1)
                    elif kind == "turn":
                        out = bank("T", w)
                        if k == 0:
                            pe.wait_ge(probs_ready, H * b + a + 1)
                        for n in range(4):
                            kt = 4 * k + n
                            ins = nc.tensor.transpose(out[:, n * P:(n + 1) * P], probs[a % 2][:, kt * P:(kt + 1) * P], identity[:])
                        ins.then_inc(full["T"], 1)
                    elif kind == "values":
                        if k == 0:
                            bank("O", w)
                            if a == 0:
                                pe.wait_ge(free["P"], w.base["P"] + 2)
                        if a == H // 2:
                            pe.wait_ge(free["P"], w.at["project", 1, 4 * k + 3] + 2)
                        pe.wait_ge(free["T"], w.at["turn", a, k] + 2)
                        for n in range(4):
                            kt = 4 * k + n
                            first, last = kt == 0, kt == SK // P - 1
                            both = (pT[0][:, kt, :], v[:, kt, a, :, :], psO[:, 0:2 * DH])
                            low = (pT[1][:, kt, :], v[:, kt, a, 0, :], psO[:, 0:DH])
                            for m, (left, right, to) in enumerate((low, both) if last else (both, low)):
                                ins = nc.tensor.matmul(to, left, right, start=(first and m == 0), stop=(last and m == 1))
                        if k == 3:
                            ins.then_inc(full["O"], 1)
                    elif kind == "context":
                        out = bank("T", w)
                        e, cp = a // 2, a % 2
                        if cp == 0:
                            pe.wait_ge(raw_in[e % 2], 64 * (batch(b) + 1) + 16 * (e // 2 + 1))
                        for c in range(2):
                            for n in range(2):
                                ins = nc.tensor.transpose(out[:, (2 * c + n) * P:(2 * c + n + 1) * P], raw[e % 2][:, n, 2 * cp + c::DC], identity[:])
                        ins.then_inc(full["T"], 1)
                    elif kind == "latents":
                        out = bank("T", w)
                        pe.wait_ge(norm_ready, batch(b) + 2)
                        for c in range(DC):
                            ins = nc.tensor.transpose(out[:, c * P:(c + 1) * P], x_norm[:, c::DC], identity[:])
                        ins.then_inc(full["T"], 1)
                    elif kind == "queries":
                        out = bank("P", w)
                        if b is None:
                            pe.wait_ge(w_lo, 1)
                        if a == 0:
                            pe.wait_ge(free["T"], w.at["latents", 0, 0] + 2)
                        for gl in range(2):
                            g = 2 * a + gl
                            left = [[x[:, c, g * P:(g + 1) * P] for c in range(DC)] for x in weights["wq"]]
                            ins = split_product(nc, out[:, gl * P:(gl + 1) * P], *left, *[[x[:, c, :] for c in range(DC)] for x in xT])
                        ins.then_inc(full["P"], 1)
                    elif kind == "project":
                        out = bank("P", w)
                        what, n, kc = piece(a, k)
                        if a == 0:
                            pe.wait_ge(free["T"], w.at["context", 4 * kc + 3, 0] + 2)
                        if b is None and k in (0, 2):
                            pe.wait_ge(w_lo, 2 if k == 0 else 3)
                        if what == "k":
                            left = [[x[:, c, n * P:(n + 1) * P] for c in range(DC)] for x in weights["wk"]]
                            ins = split_product(nc, out[:], *left, *[[x[:, c, kc * 512:(kc + 1) * 512] for c in range(DC)] for x in ctxT])
                        else:
                            for m in range(2):
                                left = [[x[:, c, (n + m) * P:(n + m + 1) * P] for c in range(DC)] for x in ctxT]
                                ins = split_product(nc, out[:, m * 256:(m + 1) * 256], *left, *[[x[:, c, a * 256:(a + 1) * 256] for c in range(DC)] for x in weights["wv"]])
                        ins.then_inc(full["P"], 1)
                    elif kind == "output":
                        out = bank("T", w)
                        pe.wait_ge(free["O"], w.use["O"] + 1)
                        for c in range(DC):
                            ins = nc.tensor.transpose(out[:, c * P:(c + 1) * P], o_tokens[:, c * P:(c + 1) * P], identity[:])
                        ins.then_inc(full["T"], 1)
                        pe.wait_ge(free["T"], w.use["T"] + 3)
                        split_product(nc, psO[:], *[[x[:, c, :] for c in range(DC)] for x in oT],
                                      *[[x[:, c, :] for c in range(DC)] for x in weights["wo"]]).then_inc(full["O"], 1)

            run(None)
            pe.wait_ge(w_lo, 4)
            with pe.Fori(0, B - 1) as b:
                run(b)
            run(B - 1)

        @block.scalar
        def _(act):
            norm_stats_scalar(nc, act, rstd, var_ready, std_ready)
            for i, n in enumerate(("wq", "wk", "wv", "wo")):
                act.wait_ge(w_in[i], 16)
                nc.scalar.copy(weights[n][0][:], w_raw[i % 2]).then_inc(w_hi, 1)
            act.wait_ge(bias_in, 64)

            def run(b):
                w = walk(b)
                for kind, a, k in w:
                    if kind in ("turn", "context", "latents", "output"):
                        act.wait_ge(full["T"], w.use["T"] + 1)
                        src = psT[w.parity["T"]][:]
                        if kind == "turn":
                            out = pT[0][:, 4 * k:4 * k + 4, :].rearrange("p k q -> p (k q)")
                        elif kind == "context":
                            out, src = ctxT[0][:, 2 * (a % 2):2 * (a % 2) + 2, (a // 2) * KEYS:(a // 2 + 1) * KEYS], src.rearrange("p (c k) -> p c k", c=2)
                        else:
                            out = (xT if kind == "latents" else oT)[0][:].rearrange("p c k -> p (c k)")
                        nc.scalar.copy(out, src).then_inc(high["T"], 1)
                    elif kind == "queries":
                        act.wait_ge(q_sum, queries_of(b, a))
                        for i in range(HG):
                            lanes = slice(i * DH, (i + 1) * DH)
                            ins = nc.scalar.copy(q_heads[0][lanes, 2 * a:2 * a + 2, i, :], q_full[lanes, :, :])
                            if i == 0:
                                ins.then_inc(high["P"], 1)
                        ins.then_inc(q_hi, 1)
                    elif kind == "project":
                        act.wait_ge(full["P"], w.use["P"] + 1)
                        src = psP[w.parity["P"]]
                        what, n, kc = piece(a, k)
                        if what == "k":
                            ins = nc.scalar.activation(kT[0][:, n, kc * 512:(kc + 1) * 512], src[:], ACT.Identity, bias=bk_col[:, n:n + 1])
                        else:
                            ins = nc.scalar.copy(v[:, n:n + 2, 8 * a:8 * a + 8, 0, :], src[:].rearrange("p (k h d) -> p k h d", k=2, d=DH))
                        ins.then_inc(high["P"], 1)
                    elif kind == "exp":
                        n = H * (batch(b) + (1 if a == 0 else 0)) + a
                        act.wait_ge(max_ready, n + 1)
                        nc.scalar.activation(probs[a % 2][:], probs[a % 2][:], ACT.Exp, bias=neg_max[:, a % 2:a % 2 + 1], scale=1.0,
                                             accum_out=row_sum[:, a:a + 1]).then_inc(probs_ready, 1)

            run(None)
            with act.Fori(0, B - 1) as b:
                run(b)
            run(B - 1)

        @block.vector
        def _(dve):
            nc.vector.memset(q_heads[0][:], 0.0)
            nc.vector.memset(q_heads[1][:], 0.0)
            for i, (s, n) in enumerate(((free["T"], 2), (free["P"], 2), (free["S"], 1), (free["O"], 1))):
                nc.vector.memset(start[:, i + 1:i + 2], 0.0).then_inc(s, n)
            dve.wait_ge(x_in, 16)
            norm_stats_vector(nc, dve, x_tokens, stats, mean_var, rstd, prep_sem, var_ready, std_ready)

            def norm(b):
                x, mean, scale = ((x_tokens[:, b, :], mean_var[:, b, 0:1], rstd[:, b, 1:2]) if isinstance(b, int) else
                                  (x_tokens[:, bass.ds(b, 1), :], mean_var[:, bass.ds(b, 1), 0], rstd[:, bass.ds(b, 1), 1]))
                nc.vector.tensor_scalar(x_norm[:], x, mean, scale, ALU.subtract, ALU.mult).then_inc(norm_ready, 1)

            norm(0)
            for i, n in enumerate(("wq", "wk", "wv", "wo")):
                dve.wait_ge(w_hi, i + 1)
                nc.vector.tensor_tensor(weights[n][1][:], w_raw[i % 2], weights[n][0][:], ALU.subtract).then_inc(w_lo, 1)
            dve.wait_ge(bias_in, 64)
            LINKS = 2 * H + 1

            def run(b):
                w = walk(b)
                link = None if b is None else Link(dve, link_sem, base=LINKS * b)
                inverse = {}
                for kind, a, k in w:
                    if kind == "score":
                        dve.wait_ge(full["S"], w.use["S"] + 1)
                        if a == 0 and k == 0:
                            dve.wait_ge(mask_ready, batch(b) + 3)
                        dve.sem_inc(passed["dve"], 1)
                        keys = slice(512 * k, 512 * (k + 1))
                        nc.vector.tensor_tensor_reduce(probs[a % 2][:, keys], psS[k % 3][:], mask_add[:, keys],
                                                       DH ** -0.5, -3e38, ALU.add, ALU.max, row_max[:, a % 2, k:k + 1]).then_inc(free["S"], 1)
                    elif kind == "exp":
                        dve.wait_ge(free["S"], w.at["score", a, 3] + 1)
                        nc.vector.tensor_reduce(neg_max[:, a % 2:a % 2 + 1], row_max[:, a % 2, :], AX.X, ALU.max, negate=True).then_inc(max_ready, 1)
                    elif kind == "norm":
                        dve.wait_ge(free["O"], w.base["O"] + 1)
                        norm(b + 1)
                    elif kind in ("turn", "context", "latents", "output"):
                        dve.wait_ge(high["T"], w.use["T"] + 1)
                        src = psT[w.parity["T"]][:]
                        if kind == "turn":
                            hi, out = (x[:, 4 * k:4 * k + 4, :].rearrange("p k q -> p (k q)") for x in pT)
                        elif kind == "context":
                            hi, out = (x[:, 2 * (a % 2):2 * (a % 2) + 2, (a // 2) * KEYS:(a // 2 + 1) * KEYS] for x in ctxT)
                            src = src.rearrange("p (c k) -> p c k", c=2)
                        else:
                            hi, out = (x[:].rearrange("p c k -> p (c k)") for x in (xT if kind == "latents" else oT))
                        nc.vector.tensor_tensor(out, src, hi, ALU.subtract).then_inc(free["T"], 1)
                        if kind == "turn" and k == 0:
                            inverse[a] = link.mark(nc.vector.reciprocal(inv_sum[:, a:a + 1], row_sum[:, a:a + 1]))
                    elif kind == "queries":
                        dve.wait_ge(full["P"], w.use["P"] + 1)
                        nc.vector.tensor_tensor(q_full[:], psP[w.parity["P"]][:, 0:2 * P].rearrange("p (g k) -> p g k", g=2),
                                                bq_col[:, 2 * a:2 * a + 2].unsqueeze(2).to_broadcast([P, 2, P]), ALU.add).then_inc(q_sum, 1)
                        dve.wait_ge(q_hi, queries_of(b, a))
                        for i in range(HG):
                            lanes = slice(i * DH, (i + 1) * DH)
                            ins = nc.vector.tensor_tensor(q_heads[1][lanes, 2 * a:2 * a + 2, i, :], q_full[lanes, :, :], q_heads[0][lanes, 2 * a:2 * a + 2, i, :],
                                                          ALU.subtract)
                            if i == 0:
                                ins.then_inc(free["P"], 1)
                        ins.then_inc(q_ready, 1)
                    elif kind == "project":
                        dve.wait_ge(high["P"], w.use["P"] + 1)
                        src = psP[w.parity["P"]]
                        what, n, kc = piece(a, k)
                        if what == "k":
                            hi, out = (x[:, n, kc * 512:(kc + 1) * 512] for x in kT)
                            ins = nc.vector.scalar_tensor_tensor(out, src[:], bk_col[:, n:n + 1], hi, ALU.add, ALU.subtract)
                        else:
                            hi, out = (v[:, n:n + 2, 8 * a:8 * a + 8, part, :] for part in range(2))
                            ins = nc.vector.tensor_tensor(out, src[:].rearrange("p (k h d) -> p k h d", k=2, d=DH), hi, ALU.subtract)
                        ins.then_inc(free["P"], 1)
                    elif kind == "gather":
                        cols = slice(a * DH, (a + 1) * DH)
                        dve.wait_ge(full["O"], w.at["values", a, 0])
                        link.wait(inverse[a])
                        link.now(nc.vector.scalar_tensor_tensor(o_part[:, a % 2, :], psO[:, 0:DH], inv_sum[:, a:a + 1], bv_row[:, cols], ALU.mult, ALU.add))
                        nc.vector.scalar_tensor_tensor(o_tokens[:, cols], psO[:, DH:2 * DH], inv_sum[:, a:a + 1], o_part[:, a % 2, :], ALU.mult, ALU.add)\
                            .then_inc(free["O"], 1)
                    if kind == "output":
                        dve.wait_ge(full["O"], w.use["O"] + 1)
                        link.now(nc.vector.tensor_tensor(y[:], psO[:], bo_row[:], ALU.add))
                        x = x_tokens[:, b:b + 1, :] if isinstance(b, int) else x_tokens[:, bass.ds(b, 1), :]
                        nc.vector.tensor_tensor(x, x, y[:].unsqueeze(1), ALU.add).then_inc(free["O"], 1)

            run(None)
            with dve.Fori(0, B - 1) as b:
                run(b)
            run(B - 1)




class Steps:

    def __init__(self, sem, names):
        self.sem, self.names = sem, names.split()

    def start(self, ins):
        ins.then_inc(self.sem, len(self.names))

    def done(self, eng, name, j=0, before=False):
        eng.wait_ge(self.sem, len(self.names) * (j + (0 if before else 1)) + self.names.index(name) + 1)


def norm_stats_vector(nc, dve, x_tokens, stats, mean_var, rstd, chain, var_ready, std_ready):
    link = Link(dve, chain)
    for b in range(B):
        link.mark(nc.vector.bn_stats(stats[:, b, :], x_tokens[:, b, :]))
    link.wait()
    for b in range(B):
        link.mark(nc.vector.bn_aggr(mean_var[:, b, :], stats[:, b, :]))
    link.wait()
    nc.vector.tensor_scalar(rstd[:, :, 0], mean_var[:, :, 1], EPS, None, ALU.add).then_inc(var_ready, 1)
    dve.wait_ge(std_ready, 1)
    link.now(nc.vector.reciprocal(rstd[:, :, 1], rstd[:, :, 0]))
    return link


def norm_stats_scalar(nc, act, rstd, var_ready, std_ready):
    act.wait_ge(var_ready, 1)
    nc.scalar.activation(rstd[:, :, 0], rstd[:, :, 0], ACT.Sqrt).then_inc(std_ready, 1)


def every_second_key(xT):
    turns = xT[:, :, 0:120].rearrange("p n (r t) -> p n r t", t=24)
    return [(turns[:, :, :, 0:12:2], slice(0, 30)), (turns[:, :, :, 13:24:2], slice(30, 60)), (xT[:, :, 120:128:2], slice(60, 64))]


def segment_attention(nc, x_tokens, identity, w_qkv_dram, w_out_dram):
    SEL = P // 2
    scale = DH ** -0.5
    with ExitStack() as ctx:
        def sb(name, shape, dt=F32):
            return ctx.enter_context(nc.sbuf_tensor(name, shape, dt))

        def sem(name):
            return ctx.enter_context(nc.semaphore(name))

        raw = sb("sa_raw", [P, DC, 3 * D])
        raw_out = sb("sa_raw_out", [P, DC, D])
        w_qkv = [sb(f"sa_w_qkv_{p}", [P, DC, 3 * D], HALF) for p in ("hi", "lo")]
        w_out = [sb(f"sa_w_out_{p}", [P, DC, D], HALF) for p in ("hi", "lo")]
        stats, mean_var, rstd = sb("sa_stats", [P, B, 6]), sb("sa_mean_var", [P, B, 2]), sb("sa_rstd", [P, B, 2])
        x_norm = sb("sa_x_norm", [P, 2, D])
        xT = [sb(f"sa_xT_{p}", [P, DC, 2, P], HALF) for p in ("hi", "lo")]
        x_keys = [sb(f"sa_x_keys_{p}", [P, DC, 2, SEL], HALF) for p in ("hi", "lo")]
        qT = sb("sa_qT", [P, G, 2 * P])
        kT = sb("sa_kT", [P, G, 2 * SEL])
        v = sb("sa_v", [P, D])
        row_max = sb("sa_row_max", [P, HG, 2 * G])
        probs = sb("sa_probs", [P, HG, 2 * G, SEL])
        row_sum, inv_sum = sb("sa_row_sum", [P, HG, 2 * G]), sb("sa_inv_sum", [P, HG, G, 2])
        pT = sb("sa_pT", [P, HG, G, P])
        o_tokens = sb("sa_o_tokens", [P, 2, D])
        oT = [sb(f"sa_oT_{p}", [P, 2, DC, P], HALF) for p in ("hi", "lo")]
        bank = [ctx.enter_context(nc.psum_tensor(f"sa_bank{i}", [P, 512], F32)) for i in range(8)]

        w_in, w_out_in, passed = sem("sa_w_in"), sem("sa_w_out_in"), sem("sa_passed")
        w_hi, w_lo, chain, var_ready, std_ready = (sem(f"sa_{n}") for n in ("w_hi", "w_lo", "chain", "var_ready", "std_ready"))
        made = Steps(sem("sa_made"), "xT0 xT1 q0 q1 k v s0 s1 s2 s3 p0 p1 p2 p3 o0 o1 oT0 oT1 y0 y1")
        by_act = Steps(sem("sa_by_act"), "xT0 xT1 q0 v exp0 exp1 exp2 exp3 pT0 pT2 oT0 oT1")
        by_dve = Steps(sem("sa_by_dve"), "norm xT0 xT1 q1 k max0 max1 sub0 max2 sub1 max3 sub2 sub3 sum0 sum1 sum2 sum3 inv pT1 pT3 o0 o1 "
                                         "oT0 oT1 y0 y1")
        by_pool = Steps(sem("sa_by_pool"), "keys")

        block = ctx.enter_context(nc.Block())

        @block.sync
        def _(sp):
            sp.dma_start(raw[:], w_qkv_dram.rearrange("(p c) n -> p c n", c=DC)).then_inc(w_in, 16)
            sp.dma_start(raw_out[:], w_out_dram.rearrange("(c p) n -> p c n", p=P)).then_inc(w_out_in, 16)

        @block.gpsimd
        def _(pool):
            by_pool.start(nc.gpsimd.memset(pT[:, 0, 0, 0:1], 0.0))
            with pool.Fori(0, B // 2) as j:
                by_dve.done(pool, "xT1", j)
                pool.sem_inc(passed, 1)
                for part in range(2):
                    for src, to in every_second_key(xT[part][:].rearrange("p c l k -> p (c l) k")):
                        dst = x_keys[part][:].rearrange("p c l k -> p (c l) k")[:, :, to]
                        ins = nc.gpsimd.tensor_copy(dst.rearrange("p n (r t) -> p n r t", t=6) if to.stop <= 60 else dst, src)
                ins.then_inc(by_pool.sem, 1)

        @block.tensor
        def _(pe):
            made.start(nc.tensor.matmul(bank[0][0:1, 0:1], identity[:, 0:1], identity[:, 0:1], start=True, stop=True))
            with pe.Fori(0, B // 2) as j:
                for l in range(2):
                    by_dve.done(pe, f"oT{l}", j, before=True)
                    if l == 0:
                        by_dve.done(pe, "norm", j)
                    for c in range(DC):
                        ins = nc.tensor.transpose(bank[l][:, c * P:(c + 1) * P], x_norm[:, l, c::DC], identity[:])
                    ins.then_inc(made.sem, 1)
                pe.wait_ge(w_lo, 2)
                by_dve.done(pe, "xT1", j)
                right = [[x[:, c, :, :].rearrange("p l k -> p (l k)") for c in range(DC)] for x in xT]
                for half in range(2):
                    by_dve.done(pe, f"y{half}", j, before=True)
                    for gl in range(2):
                        g = 2 * half + gl
                        left = [[w[:, c, g * P:(g + 1) * P] for c in range(DC)] for w in w_qkv]
                        ins = split_product(nc, bank[2 + half][:, gl * 2 * P:(gl + 1) * 2 * P], *left, *right)
                    ins.then_inc(made.sem, 1)
                by_pool.done(pe, "keys", j)
                by_act.done(pe, "pT2", j, before=True)
                keys = [[x[:, c, :, :].rearrange("p l k -> p (l k)") for c in range(DC)] for x in x_keys]
                for g in range(G):
                    left = [[w[:, c, D + g * P:D + (g + 1) * P] for c in range(DC)] for w in w_qkv]
                    ins = split_product(nc, bank[4][:, g * P:(g + 1) * P], *left, *keys)
                ins.then_inc(made.sem, 1)
                by_dve.done(pe, "pT3", j, before=True)
                right = [[w[:, c, 2 * D:3 * D] for c in range(DC)] for w in w_qkv]
                split_product(nc, bank[5][:], *keys, *right).then_inc(made.sem, 1)
                by_act.done(pe, "q0", j)
                by_dve.done(pe, "k", j)
                for i in range(HG):
                    by_dve.done(pe, ("o0", "o1", "xT0", "xT1")[i], j, before=i < 2)
                    rows = slice(i * DH, (i + 1) * DH)
                    for g in range(G):
                        for l in range(2):
                            n = 2 * g + l
                            ins = nc.tensor.matmul(bank[(6 + i) % 8][:, n * SEL:(n + 1) * SEL], qT[rows, g, l * P:(l + 1) * P],
                                                   kT[rows, g, l * SEL:(l + 1) * SEL], start=True, stop=True)
                    ins.then_inc(made.sem, 1)
                for i in range(HG):
                    by_act.done(pe, f"exp{i}", j)
                    (by_act if i in (0, 3) else by_dve).done(pe, ("q0", "q1", "k", "v")[i], j)
                    for g in range(G):
                        ins = nc.tensor.transpose(bank[2 + i][:, g * P:(g + 1) * P], probs[:, i, 2 * g:2 * g + 2, :].rearrange("p n k -> p (n k)"), identity[:])
                    ins.then_inc(made.sem, 1)
                by_act.done(pe, "pT2", j)
                by_dve.done(pe, "pT3", j)
                for l in range(2):
                    by_dve.done(pe, f"sub{l}", j)
                    rows = slice(l * SEL, (l + 1) * SEL)
                    for g in range(G):
                        for i in range(HG):
                            cols = slice((HG * g + i) * DH, (HG * g + i + 1) * DH)
                            ins = nc.tensor.matmul(bank[6 + l][:, cols], pT[rows, i, g, :], v[rows, cols], start=True, stop=True)
                    ins.then_inc(made.sem, 1)
                for l in range(2):
                    by_dve.done(pe, f"o{l}", j)
                    for c in range(DC):
                        ins = nc.tensor.transpose(bank[l][:, c * P:(c + 1) * P], o_tokens[:, l, c * P:(c + 1) * P], identity[:])
                    ins.then_inc(made.sem, 1)
                for l in range(2):
                    by_dve.done(pe, f"oT{l}", j)
                    left = [[x[:, l, c, :] for c in range(DC)] for x in oT]
                    right = [[w[:, c, :] for c in range(DC)] for w in w_out]
                    split_product(nc, bank[2 + l][:], *left, *right).then_inc(made.sem, 1)

        @block.scalar
        def _(act):
            norm_stats_scalar(nc, act, rstd, var_ready, std_ready)
            act.wait_ge(w_in, 16)
            by_act.start(nc.scalar.copy(w_qkv[0][:], raw[:]))
            act.wait_ge(w_out_in, 16)
            nc.scalar.copy(w_out[0][:], raw_out[:]).then_inc(w_hi, 1)
            with act.Fori(0, B // 2) as j:
                for l in range(2):
                    made.done(act, f"xT{l}", j)
                    nc.scalar.copy(xT[0][:, :, l, :], bank[l][:].rearrange("p (c k) -> p c k", k=P)).then_inc(by_act.sem, 1)
                made.done(act, "q0", j)
                nc.scalar.copy(qT[:, 0:2, :].rearrange("p g k -> p (g k)"), bank[2][:]).then_inc(by_act.sem, 1)
                made.done(act, "v", j)
                nc.scalar.copy(v[:], bank[5][:]).then_inc(by_act.sem, 1)
                for i in range(HG):
                    by_dve.done(act, f"sub{i}", j)
                    p = probs[:, i, :, :].rearrange("p n k -> p (n k)")
                    nc.scalar.activation(p, p, ACT.Exp, scale=scale).then_inc(by_act.sem, 1)
                for i in (0, 2):
                    made.done(act, f"p{i}", j)
                    nc.scalar.copy(pT[:, i, :, :].rearrange("p g q -> p (g q)"), bank[2 + i][:]).then_inc(by_act.sem, 1)
                for l in range(2):
                    made.done(act, f"oT{l}", j)
                    nc.scalar.copy(oT[0][:, l, :, :].rearrange("p c k -> p (c k)"), bank[l][:]).then_inc(by_act.sem, 1)

        @block.vector
        def _(dve):
            norm_stats_vector(nc, dve, x_tokens, stats, mean_var, rstd, chain, var_ready, std_ready)
            by_dve.start(nc.vector.memset(row_max[:], 0.0))
            dve.wait_ge(w_hi, 1)
            nc.vector.tensor_tensor(w_qkv[1][:], raw[:], w_qkv[0][:], ALU.subtract).then_inc(w_lo, 1)
            nc.vector.tensor_tensor(w_out[1][:], raw_out[:], w_out[0][:], ALU.subtract).then_inc(w_lo, 1)
            with dve.Fori(0, B // 2) as j:
                made.done(dve, "y1", j, before=True)
                for l in range(2):
                    b = bass.ds(2 * j + l, 1)
                    ins = nc.vector.tensor_scalar(x_norm[:, l:l + 1, :], x_tokens[:, b, :], mean_var[:, b, 0], rstd[:, b, 1], ALU.subtract, ALU.mult)
                ins.then_inc(by_dve.sem, 1)
                for l in range(2):
                    by_act.done(dve, f"xT{l}", j)
                    nc.vector.tensor_tensor(xT[1][:, :, l, :], bank[l][:].rearrange("p (c k) -> p c k", k=P), xT[0][:, :, l, :],
                                            ALU.subtract).then_inc(by_dve.sem, 1)
                made.done(dve, "q1", j)
                nc.vector.tensor_copy(qT[:, 2:4, :].rearrange("p g k -> p (g k)"), bank[3][:]).then_inc(by_dve.sem, 1)
                made.done(dve, "k", j)
                nc.vector.tensor_copy(kT[:].rearrange("p g k -> p (g k)"), bank[4][:]).then_inc(by_dve.sem, 1)

                def logits(i):
                    return bank[(6 + i) % 8][:].rearrange("p (n k) -> p n k", k=SEL)

                def largest(i):
                    made.done(dve, f"s{i}", j)
                    nc.vector.tensor_reduce(row_max[:, i, :], logits(i), AX.X, ALU.max).then_inc(by_dve.sem, 1)

                def subtract(i):
                    by_dve.done(dve, f"max{i}", j)
                    nc.vector.tensor_tensor(probs[:, i, :, :], logits(i), row_max[:, i, :].unsqueeze(2).to_broadcast([P, 2 * G, SEL]),
                                            ALU.subtract).then_inc(by_dve.sem, 1)

                largest(0)
                for i in range(1, HG):
                    largest(i)
                    subtract(i - 1)
                subtract(HG - 1)
                for i in range(HG):
                    by_act.done(dve, f"exp{i}", j)
                    nc.vector.tensor_reduce(row_sum[:, i, :], probs[:, i, :, :], AX.X, ALU.add).then_inc(by_dve.sem, 1)
                by_dve.done(dve, f"sum{HG - 1}", j)
                nc.vector.reciprocal(inv_sum[:].rearrange("p i g l -> p (i g l)"), row_sum[:].rearrange("p i n -> p (i n)")).then_inc(by_dve.sem, 1)
                for i in (1, 3):
                    made.done(dve, f"p{i}", j)
                    nc.vector.tensor_copy(pT[:, i, :, :].rearrange("p g q -> p (g q)"), bank[2 + i][:]).then_inc(by_dve.sem, 1)
                for l in range(2):
                    made.done(dve, f"o{l}", j)
                    by_dve.done(dve, "inv", j)
                    nc.vector.tensor_tensor(o_tokens[:, l, :].rearrange("p (g i d) -> p g i d", g=G, i=HG),
                                            bank[6 + l][:].rearrange("p (g i d) -> p g i d", g=G, i=HG),
                                            inv_sum[:, :, :, l].rearrange("p i g -> p g i").unsqueeze(3).to_broadcast([P, G, HG, DH]),
                                            ALU.mult).then_inc(by_dve.sem, 1)
                for l in range(2):
                    by_act.done(dve, f"oT{l}", j)
                    nc.vector.tensor_tensor(oT[1][:, l, :, :].rearrange("p c k -> p (c k)"), bank[l][:],
                                            oT[0][:, l, :, :].rearrange("p c k -> p (c k)"), ALU.subtract).then_inc(by_dve.sem, 1)
                for l in range(2):
                    made.done(dve, f"y{l}", j)
                    b = bass.ds(2 * j + l, 1)
                    nc.vector.tensor_tensor(x_tokens[:, b, :], bank[2 + l][:].unsqueeze(1), x_tokens[:, b, :], ALU.add).then_inc(by_dve.sem, 1)




E = 8
PH = 64
ROT = 32
F = 2048
T = B


def gate_stage(nc, x_tokens, x_norm, xT, gates, identity, wsel_v, wsel_o):
    with ExitStack() as ctx:
        def sb(name, shape, dt=F32):
            return ctx.enter_context(nc.sbuf_tensor(name, shape, dt))

        def sem(name):
            return ctx.enter_context(nc.semaphore(f"ga_{name}"))

        stats, mean_var, rstd = sb("ga_stats", [P, B, 6]), sb("ga_mean_var", [P, B, 2]), sb("ga_rstd", [P, B, 2])
        wsel = sb("ga_wsel", [P, 2, D])
        wselT = sb("ga_wselT", [P, DC, 2 * P])
        xT_full = [sb(f"ga_xT_full{i}", [P, DC, P]) for i in range(2)]
        N = T * 2 * H
        first, rank, left = (sb(f"ga_{n}", [P, N, E]) for n in ("first", "rank", "left"))
        best = sb("ga_best", [P, N])
        order = sb("ga_order", [P, E])
        bank = [ctx.enter_context(nc.psum_tensor(f"ga_bank{i}", [P, 512], F32)) for i in range(8)]
        w_in, chain, var_ready, std_ready, order_ready = (sem(n) for n in ("w_in", "chain", "var_ready", "std_ready", "order"))
        norm_ready, wsel_turned, wsel_ready, turned, full, hi, lo, summed, taken = (
            sem(n) for n in ("norm_ready", "wsel_turned", "wsel_ready", "turned", "full", "hi", "lo", "summed", "taken"))
        block = ctx.enter_context(nc.Block())

        @block.sync
        def _(sp):
            for i, w in enumerate((wsel_v, wsel_o)):
                sp.dma_start(wsel[:, i, :], w.rearrange("h e d -> (h e) d")).then_inc(w_in, 16)

        @block.gpsimd
        def _(pool):
            for e in range(E):
                nc.gpsimd.memset(order[:, e:e + 1], float(E - e)).then_inc(order_ready, 1)

        @block.tensor
        def _(pe):
            pe.wait_ge(w_in, 32)
            for i in range(2):
                for c in range(DC):
                    ins = nc.tensor.transpose(bank[6 + i][:, c * P:(c + 1) * P], wsel[:, i, c::DC], identity[:])
                ins.then_inc(wsel_turned, 1)

            def turn(t):
                pe.wait_ge(norm_ready, t + 1)
                if t >= 4:
                    pe.wait_ge(lo, t - 3)
                for c in range(DC):
                    ins = nc.tensor.transpose(bank[t % 4][:, c * P:(c + 1) * P], x_norm[:, t, c::DC], identity[:])
                ins.then_inc(turned, 1)

            turn(0)
            for t in range(T):
                if t + 1 < T:
                    turn(t + 1)
                if t == 0:
                    pe.wait_ge(wsel_ready, 2)
                pe.wait_ge(full, t + 1)
                if t >= 2:
                    pe.wait_ge(taken, t - 1)
                for c in range(DC):
                    ins = nc.tensor.matmul(bank[4 + t % 2][:, 0:2 * P], xT_full[t % 2][:, c, :], wselT[:, c, :], start=(c == 0), stop=(c == DC - 1))
                ins.then_inc(summed, 1)

        @block.scalar
        def _(act):
            norm_stats_scalar(nc, act, rstd, var_ready, std_ready)

            def take(t):
                act.wait_ge(summed, t + 1)
                nc.scalar.activation(gates[:, t, :, :].rearrange("p n e -> p (n e)"), bank[4 + t % 2][:, 0:2 * P], ACT.Exp, scale=-1.0).then_inc(taken, 1)

            for t in range(T):
                act.wait_ge(turned, t + 1)
                if t >= 2:
                    act.wait_ge(summed, t - 1)
                nc.scalar.copy(xT_full[t % 2][:].rearrange("p c k -> p (c k)"), bank[t % 4][:]).then_inc(full, 1)
                nc.scalar.copy(xT[0][:, :, t * P:(t + 1) * P], bank[t % 4][:].rearrange("p (c k) -> p c k", k=P)).then_inc(hi, 1)
                if t >= 1:
                    take(t - 1)
            take(T - 1)

        @block.vector
        def _(dve):
            norm_stats_vector(nc, dve, x_tokens, stats, mean_var, rstd, chain, var_ready, std_ready)
            for t in range(T):
                nc.vector.tensor_scalar(x_norm[:, t, :], x_tokens[:, t, :], mean_var[:, t, 0:1], rstd[:, t, 1:2], ALU.subtract, ALU.mult).then_inc(norm_ready, 1)
            for i in range(2):
                dve.wait_ge(wsel_turned, i + 1)
                nc.vector.tensor_copy(wselT[:, :, i * P:(i + 1) * P], bank[6 + i][:].rearrange("p (c k) -> p c k", k=P)).then_inc(wsel_ready, 1)
            for t in range(T):
                dve.wait_ge(hi, t + 1)
                tile = slice(t * P, (t + 1) * P)
                nc.vector.tensor_tensor(xT[1][:, :, tile], bank[t % 4][:].rearrange("p (c k) -> p c k", k=P), xT[0][:, :, tile], ALU.subtract).then_inc(lo, 1)
            link = Link(dve, chain, base=2 * B + 1)
            g = gates[:].rearrange("p t n e -> p (t n) e")
            weight = order[:].unsqueeze(1).to_broadcast([P, N, E])

            def spread(row):
                return row[:].unsqueeze(2).to_broadcast([P, N, E])

            dve.wait_ge(taken, T)
            dve.wait_ge(order_ready, E)
            link.now(nc.vector.tensor_scalar(left[:], g, 1.0, None, ALU.add))
            link.now(nc.vector.reciprocal(g, left[:]))
            link.now(nc.vector.tensor_reduce(best[:], g, AX.X, ALU.max))
            link.now(nc.vector.tensor_tensor(rank[:], g, spread(best), ALU.is_equal))
            link.now(nc.vector.tensor_tensor(rank[:], rank[:], weight, ALU.mult))
            link.now(nc.vector.tensor_reduce(best[:], rank[:], AX.X, ALU.max))
            link.now(nc.vector.tensor_tensor(first[:], rank[:], spread(best), ALU.is_equal))
            link.now(nc.vector.scalar_tensor_tensor(left[:].rearrange("p n e -> p (n e)"), first[:].rearrange("p n e -> p (n e)"), -4.0,
                                                    g.rearrange("p n e -> p (n e)"), ALU.mult, ALU.add))
            link.now(nc.vector.tensor_reduce(best[:], left[:], AX.X, ALU.max))
            link.now(nc.vector.tensor_tensor(rank[:], left[:], spread(best), ALU.is_equal))
            link.now(nc.vector.tensor_tensor(rank[:], rank[:], weight, ALU.mult))
            link.now(nc.vector.tensor_reduce(best[:], rank[:], AX.X, ALU.max))
            link.now(nc.vector.tensor_tensor(rank[:], rank[:], spread(best), ALU.is_equal))
            link.now(nc.vector.tensor_tensor(first[:], first[:], rank[:], ALU.add))
            link.now(nc.vector.tensor_tensor(g, g, first[:], ALU.mult))


def expert_values(nc, xT, gates, v, wv_dram):
    with ExitStack() as ctx:
        def sb(name, shape, dt=F32):
            return ctx.enter_context(nc.sbuf_tensor(name, shape, dt))

        def sem(name):
            return ctx.enter_context(nc.semaphore(f"ev_{name}"))

        raw = [sb(f"ev_raw{i}", [P, E, DC, PH]) for i in range(2)]
        w = [[sb(f"ev_w{i}_{p}", [P, E, DC, PH], HALF) for p in ("hi", "lo")] for i in range(2)]
        gated = [sb(f"ev_gated{i}", [P, E, PH]) for i in range(4)]
        bank = [ctx.enter_context(nc.psum_tensor(f"ev_bank{i}", [P, 512], F32)) for i in range(8)]
        raw_in = [sem(f"raw_in{i}") for i in range(2)]
        passed, w_hi, w_ready, made, gated_ready, reduced = (sem(n) for n in ("passed", "w_hi", "w_ready", "made", "gated", "reduced"))
        by = wv_dram.rearrange("h e (q c) p -> h q e (c p)", c=DC)
        block = ctx.enter_context(nc.Block())

        @block.sync
        def _(sp):
            for i in range(2):
                sp.dma_start(raw[i][:].rearrange("q e c p -> q e (c p)"), by[i]).then_inc(raw_in[i], 16)
            with sp.Fori(1, H // 2) as j:
                for i in range(2):
                    sp.wait_ge(w_ready, 2 * j + i - 1)
                    sp.dma_start(raw[i][:].rearrange("q e c p -> q e (c p)"), by[bass.ds(2 * j + i, 1)].rearrange("h q e n -> (h q) e n")).then_inc(raw_in[i], 16)

        @block.gpsimd
        def _(pool):
            with pool.Fori(0, H // 2) as j:
                for i in range(2):
                    pool.wait_ge(raw_in[i], 16 * j + 16)
                    pool.wait_ge(made, T * (2 * j + i) + T)
                    pool.sem_inc(passed, 1)
                    nc.gpsimd.tensor_copy(w[i][0][:], raw[i][:]).then_inc(w_hi, 1)
                    pool.wait_ge(w_hi, 2 * j + i + 1)
                    nc.gpsimd.tensor_tensor(w[i][1][:], raw[i][:], w[i][0][:], ALU.subtract).then_inc(w_ready, 1)

        @block.tensor
        def _(pe):
            with pe.Fori(0, H // 2) as j:
                for i in range(2):
                    pe.wait_ge(w_ready, 2 * j + i + 1)
                    right = [[x[:, :, c, :] for c in range(DC)] for x in w[i]]
                    for t in range(T):
                        pe.wait_ge(gated_ready, T * (2 * j + i) + t + 1)
                        left = [[x[:, c, t * P:(t + 1) * P] for c in range(DC)] for x in xT]
                        split_product(nc, bank[t][:], *left, *right).then_inc(made, 1)

        @block.vector
        def _(dve):
            nc.vector.memset(gated[0][:], 0.0).then_inc(gated_ready, T)
            nc.vector.memset(gated[1][:], 0.0).then_inc(made, 2 * T)
            nc.vector.memset(gated[2][:], 0.0).then_inc(reduced, 4)
            with dve.Fori(0, H // 2) as j:
                for i in range(2):
                    head = bass.ds(2 * j + i, 1)

                    def total(t):
                        dve.wait_ge(gated_ready, T * (2 * j + i) + T + t + 1)
                        nc.vector.tensor_reduce(v[:, t, head, :], gated[t % 4][:].rearrange("p e q -> p q e").unsqueeze(1),
                                                AX.X, ALU.add).then_inc(reduced, 1)

                    for t in range(T):
                        n = T * (2 * j + i) + t
                        dve.wait_ge(made, 2 * T + n + 1)
                        dve.wait_ge(reduced, n + 1)
                        gate = gates[:, t, head, :].unsqueeze(3).to_broadcast([P, 1, E, PH])
                        nc.vector.tensor_tensor(gated[t % 4][:].unsqueeze(1), bank[t][:].rearrange("p (a e q) -> p a e q", a=1, e=E), gate, ALU.mult)\
                            .then_inc(gated_ready, 1)
                        if t >= 1:
                            total(t - 1)
                    total(T - 1)




def rotary_attention(nc, xT, v, identity, wq_dram, wk_dram, cos_dram, sin_dram):
    HALF_ROT = ROT // 2
    with ExitStack() as ctx:
        def sb(name, shape, dt=F32):
            return ctx.enter_context(nc.sbuf_tensor(name, shape, dt))

        def sem(name):
            return ctx.enter_context(nc.semaphore(f"ra_{name}"))

        w = [sb(f"ra_w_{p}", [P, 2 * H, DC, PH], HALF) for p in ("hi", "lo")]
        cos, sin = sb("ra_cos", [P, HALF_ROT]), sb("ra_sin", [P, HALF_ROT])
        qk = sb("ra_qk", [P, 2 * H, PH])
        by_cos, by_sin = (sb(f"ra_by_{n}", [P, 2 * H, 2, HALF_ROT]) for n in ("cos", "sin"))
        qkT = sb("ra_qkT", [P, H, P])
        row_max, row_sum, inv_sum = (sb(f"ra_{n}", [P, H]) for n in ("row_max", "row_sum", "inv_sum"))
        probs = sb("ra_probs", [P, H, P])
        pT = sb("ra_pT", [P, H, P])
        raw = [sb(f"ra_raw{i}", [P, H // 2, DC, PH]) for i in range(2)]
        bank = [ctx.enter_context(nc.psum_tensor(f"ra_bank{i}", [P, 512], F32)) for i in range(8)]
        raw_in = [sem(f"raw_in{i}") for i in range(2)]
        table_in, w_hi, w_lo = sem("table_in"), sem("w_hi"), sem("w_lo")
        qk_made, qk_taken, rotating, rotated = sem("qk_made"), sem("qk_taken"), sem("rotating"), sem("rotated")
        made = Steps(sem("made"), "qkT0 qkT1 qkT2 qkT3 s0 s1 s2 s3 pT0 pT1 pT2 pT3 o0 o1")
        by_act = Steps(sem("by_act"), "qkT0 qkT2 exp0 exp1 exp2 exp3 pT0 pT2")
        by_dve = Steps(sem("by_dve"), "qkT1 qkT3 max0 max1 sub0 max2 sub1 max3 sub2 sub3 sum0 sum1 sum2 sum3 inv pT1 pT3 o0 o1")

        def at(b):
            return bass.ds(b, 1)

        block = ctx.enter_context(nc.Block())

        @block.sync
        def _(sp):
            sp.dma_start(cos[:], cos_dram).then_inc(table_in, 16)
            sp.dma_start(sin[:], sin_dram).then_inc(table_in, 16)
            for n in range(4):
                if n >= 2:
                    sp.wait_ge(w_lo, n - 1)
                src = (wq_dram, wk_dram)[n // 2][8 * (n % 2):8 * (n % 2) + 8].rearrange("h (q c) p -> q h (c p)", c=DC)
                sp.dma_start(raw[n % 2][:].rearrange("q h c p -> q h (c p)"), src).then_inc(raw_in[n % 2], 16)

        @block.tensor
        def _(pe):
            made.start(nc.tensor.matmul(bank[7][0:1, 0:1], identity[:, 0:1], identity[:, 0:1], start=True, stop=True))

            def project(b):
                for n in range(4):
                    if isinstance(b, int):
                        pe.wait_ge(w_lo, n + 1)
                    else:
                        by_dve.done(pe, f"sub{n}", b - 1)
                    for c in range(DC):
                        left = [[x[:, c, b * P:(b + 1) * P] if isinstance(b, int) else x[:, c, bass.ds(b * P, P)]] for x in xT]
                        right = [[x[:, 8 * n:8 * n + 8, c, :]] for x in w]
                        ins = split_product(nc, bank[n][:], *left, *right, first=(c == 0), last=(c == DC - 1))
                    ins.then_inc(qk_made, 1)

            def body(b, last=False):
                pe.wait_ge(rotated, 2 * b + 2)
                for m in range(4):
                    if m < 2:
                        by_dve.done(pe, f"o{m}", b, before=True)
                    else:
                        (by_act if m == 2 else by_dve).done(pe, f"pT{m}", b, before=True)
                    for k in range(4):
                        pair = 4 * m + k
                        ins = nc.tensor.transpose(bank[4 + m][:, k * P:(k + 1) * P], qk[:, 2 * pair:2 * pair + 2, :].rearrange("p h d -> p (h d)"), identity[:])
                    ins.then_inc(made.sem, 1)
                by_act.done(pe, "qkT2", b)
                by_dve.done(pe, "qkT3", b)
                for m in range(4):
                    rows = slice(PH * (m // 2), PH * (m // 2) + PH)
                    for k in range(4):
                        pair = 4 * (m % 2) + k
                        ins = nc.tensor.matmul(bank[m][:, k * P:(k + 1) * P], qkT[rows, pair, :], qkT[rows, H // 2 + pair, :], start=True, stop=True)
                    ins.then_inc(made.sem, 1)
                if not last:
                    project(b + 1)
                for m in range(4):
                    by_act.done(pe, f"exp{m}", b)
                    for k in range(4):
                        ins = nc.tensor.transpose(bank[4 + m][:, k * P:(k + 1) * P], probs[:, 4 * m + k, :], identity[:])
                    ins.then_inc(made.sem, 1)
                by_act.done(pe, "pT2", b)
                by_dve.done(pe, "pT3", b)
                for m in range(2):
                    for k in range(8):
                        h = 8 * m + k
                        right = v[:, b, h, :] if last else v[:, at(b), h, :].rearrange("p a d -> p (a d)")
                        ins = nc.tensor.matmul(bank[4 + m][:, k * PH:(k + 1) * PH], pT[:, h // 2 + 8 * (h % 2), :], right, start=True, stop=True)
                    ins.then_inc(made.sem, 1)

            project(0)
            with pe.Fori(0, B - 1) as b:
                body(b)
            body(B - 1, last=True)

        @block.scalar
        def _(act):
            for n in range(4):
                act.wait_ge(raw_in[n % 2], 16 * (n // 2) + 16)
                nc.scalar.copy(w[0][:, 8 * n:8 * n + 8, :, :], raw[n % 2][:]).then_inc(w_hi, 1)
            act.wait_ge(table_in, 32)
            by_act.start(nc.scalar.copy(inv_sum[:, 0:1], cos[:, 0:1]))

            def take(b):
                for n in range(4):
                    act.wait_ge(qk_made, 4 * b + n + 1)
                    nc.scalar.copy(qk[:, 8 * n:8 * n + 8, :].rearrange("p h d -> p (h d)"), bank[n][:]).then_inc(qk_taken, 1)

            def body(b, last=False):
                for m in (0, 2):
                    made.done(act, f"qkT{m}", b)
                    nc.scalar.copy(qkT[:, 4 * m:4 * m + 4, :].rearrange("p h d -> p (h d)"), bank[4 + m][:]).then_inc(by_act.sem, 1)
                for m in range(4):
                    by_dve.done(act, f"sub{m}", b)
                    p = probs[:, 4 * m:4 * m + 4, :]
                    nc.scalar.activation(p, p, ACT.Exp, scale=PH ** -0.5).then_inc(by_act.sem, 1)
                if not last:
                    take(b + 1)
                for m in (0, 2):
                    made.done(act, f"pT{m}", b)
                    nc.scalar.copy(pT[:, 4 * m:4 * m + 4, :].rearrange("p h q -> p (h q)"), bank[4 + m][:]).then_inc(by_act.sem, 1)

            take(0)
            with act.Fori(0, B - 1) as b:
                body(b)
            body(B - 1, last=True)

        @block.vector
        def _(dve):
            by_dve.start(nc.vector.memset(row_max[:], 0.0))
            for n in range(4):
                dve.wait_ge(w_hi, n + 1)
                nc.vector.tensor_tensor(w[1][:, 8 * n:8 * n + 8, :, :], raw[n % 2][:], w[0][:, 8 * n:8 * n + 8, :, :], ALU.subtract).then_inc(w_lo, 1)
            dve.wait_ge(table_in, 32)

            def rotate(b):
                dve.wait_ge(qk_taken, 4 * b + 4)
                x = qk[:, :, 0:ROT]
                for table, to in ((cos, by_cos), (sin, by_sin)):
                    ins = nc.vector.tensor_tensor(to[:], x.rearrange("p h (a k) -> p h a k", a=2),
                                                  table[:].unsqueeze(1).unsqueeze(1).to_broadcast([P, 2 * H, 2, HALF_ROT]), ALU.mult)
                    ins.then_inc(rotating, 1)
                dve.wait_ge(rotating, 2 * b + 2)
                nc.vector.tensor_tensor(x[:, :, 0:HALF_ROT], by_cos[:, :, 0, :], by_sin[:, :, 1, :], ALU.subtract).then_inc(rotated, 1)
                nc.vector.tensor_tensor(x[:, :, HALF_ROT:ROT], by_cos[:, :, 1, :], by_sin[:, :, 0, :], ALU.add).then_inc(rotated, 1)

            def body(b, last=False):
                for m in (1, 3):
                    made.done(dve, f"qkT{m}", b)
                    nc.vector.tensor_copy(qkT[:, 4 * m:4 * m + 4, :].rearrange("p h d -> p (h d)"), bank[4 + m][:]).then_inc(by_dve.sem, 1)

                def logits(m):
                    return bank[m][:].rearrange("p (h k) -> p h k", k=P)

                def heads(m):
                    return slice(4 * m, 4 * m + 4)

                def largest(m):
                    made.done(dve, f"s{m}", b)
                    nc.vector.tensor_reduce(row_max[:, heads(m)], logits(m), AX.X, ALU.max).then_inc(by_dve.sem, 1)

                def subtract(m):
                    by_dve.done(dve, f"max{m}", b)
                    nc.vector.tensor_tensor(probs[:, heads(m), :], logits(m), row_max[:, heads(m)].unsqueeze(2).to_broadcast([P, 4, P]),
                                            ALU.subtract).then_inc(by_dve.sem, 1)

                largest(0)
                for m in range(1, 4):
                    largest(m)
                    subtract(m - 1)
                subtract(3)
                for m in range(4):
                    by_act.done(dve, f"exp{m}", b)
                    nc.vector.tensor_reduce(row_sum[:, heads(m)], probs[:, heads(m), :], AX.X, ALU.add).then_inc(by_dve.sem, 1)
                by_dve.done(dve, "sum3", b)
                nc.vector.reciprocal(inv_sum[:].rearrange("p (u i) -> p u i", i=2), row_sum[:].rearrange("p (i u) -> p u i", i=2)).then_inc(by_dve.sem, 1)
                for m in (1, 3):
                    made.done(dve, f"pT{m}", b)
                    nc.vector.tensor_copy(pT[:, heads(m), :].rearrange("p h q -> p (h q)"), bank[4 + m][:]).then_inc(by_dve.sem, 1)
                if not last:
                    rotate(b + 1)
                by_dve.done(dve, "inv", b)
                for m in range(2):
                    made.done(dve, f"o{m}", b)
                    out = v[:, b:b + 1, 8 * m:8 * m + 8, :] if last else v[:, at(b), 8 * m:8 * m + 8, :]
                    nc.vector.tensor_tensor(out.rearrange("p a h d -> p (a h) d"), bank[4 + m][:].rearrange("p (h d) -> p h d", d=PH),
                                            inv_sum[:, 8 * m:8 * m + 8].unsqueeze(2).to_broadcast([P, 8, PH]), ALU.mult).then_inc(by_dve.sem, 1)

            rotate(0)
            with dve.Fori(0, B - 1) as b:
                body(b)
            body(B - 1, last=True)


def expert_outputs(nc, x_norm, v, gates, identity, wo_dram):
    with ExitStack() as ctx:
        def sb(name, shape, dt=F32):
            return ctx.enter_context(nc.sbuf_tensor(name, shape, dt))

        def sem(name):
            return ctx.enter_context(nc.semaphore(f"eo_{name}"))

        raw = [sb(f"eo_raw{i}", [P, DC, D]) for i in range(2)]
        w = [[sb(f"eo_w{i}_{p}", [P, DC, D], HALF) for p in ("hi", "lo")] for i in range(4)]
        gated = [sb(f"eo_gated{i}", [P, E, PH]) for i in range(4)]
        start = sb("eo_start", [P, 3])
        gatedT = [[sb(f"eo_gatedT{i}_{p}", [P, DC, P], HALF) for p in ("hi", "lo")] for i in range(4)]
        psT = [ctx.enter_context(nc.psum_tensor(f"eo_psT{i}", [P, 512], F32)) for i in range(4)]
        psY = [ctx.enter_context(nc.psum_tensor(f"eo_psY{i}", [P, 512], F32)) for i in range(4)]
        raw_in = [sem(f"raw_in{i}") for i in range(2)]
        passed, w_hi, w_ready, gated_ready, turned, hi, lo, made, added = (sem(n) for n in ("passed", "w_hi", "w_ready", "gated", "turned", "hi", "lo", "made", "added"))
        NJ = 2 * T
        block = ctx.enter_context(nc.Block())

        @block.sync
        def _(sp):
            for i in range(2):
                sp.dma_start(raw[i][:], wo_dram[i].rearrange("e p n -> (e p) n").rearrange("(c q) n -> q c n", q=P)).then_inc(raw_in[i], 16)
            with sp.Fori(1, H // 2) as j:
                for i in range(2):
                    sp.wait_ge(w_ready, 2 * j + i - 1)
                    src = wo_dram[bass.ds(2 * j + i, 1)].rearrange("a e p n -> (a e p) n").rearrange("(c q) n -> q c n", q=P)
                    sp.dma_start(raw[i][:], src).then_inc(raw_in[i], 16)

        @block.gpsimd
        def _(pool):
            with pool.Fori(0, H // 4) as quad:
                for half in range(2):
                    j = 2 * quad + half
                    for i in range(2):
                        hi_part, lo_part = w[2 * half + i]
                        pool.wait_ge(raw_in[i], 16 * j + 16)
                        pool.wait_ge(made, T * j + T)
                        pool.sem_inc(passed, 1)
                        nc.gpsimd.tensor_copy(hi_part[:], raw[i][:]).then_inc(w_hi, 1)
                        pool.wait_ge(w_hi, 2 * j + i + 1)
                        nc.gpsimd.tensor_tensor(lo_part[:], raw[i][:], hi_part[:], ALU.subtract).then_inc(w_ready, 1)

        @block.tensor
        def _(pe):
            def pair(j, half):
                def turn(n):
                    pe.wait_ge(gated_ready, NJ * j + n + 1)
                    pe.wait_ge(lo, NJ * j + n + 1)
                    flat = gated[n % 4][:].rearrange("p e d -> p (e d)")
                    for c in range(DC):
                        ins = nc.tensor.transpose(psT[n % 4][:, c * P:(c + 1) * P], flat[:, c * P:(c + 1) * P], identity[:])
                    ins.then_inc(turned, 1)

                turn(0)
                turn(1)
                pe.wait_ge(w_ready, 2 * j + 2)
                for t in range(T):
                    pe.wait_ge(added, T * j + t + 1)
                    for i in range(2):
                        n = 2 * t + i
                        if n + 2 < NJ:
                            turn(n + 2)
                        pe.wait_ge(lo, NJ * j + 4 + n + 1)
                        left = [[x[:, c, :] for c in range(DC)] for x in gatedT[n % 4]]
                        right = [[x[:, c, :] for c in range(DC)] for x in w[2 * half + i]]
                        ins = split_product(nc, psY[t % 4][:], *left, *right, first=(i == 0), last=(i == 1))
                    ins.then_inc(made, 1)

            with pe.Fori(0, H // 4) as quad:
                pair(2 * quad, 0)
                pair(2 * quad + 1, 1)

        @block.scalar
        def _(act):
            with act.Fori(0, H // 2) as j:
                for n in range(NJ):
                    act.wait_ge(turned, NJ * j + n + 1)
                    nc.scalar.copy(gatedT[n % 4][0][:].rearrange("p c k -> p (c k)"), psT[n % 4][:]).then_inc(hi, 1)

        @block.vector
        def _(dve):
            nc.vector.memset(start[:, 0:1], 0.0).then_inc(lo, 4)
            nc.vector.memset(start[:, 1:2], 0.0).then_inc(added, 4)
            nc.vector.memset(start[:, 2:3], 0.0).then_inc(made, 2 * T)
            with dve.Fori(0, H // 2) as j:
                def gate(n):
                    t, i = n // 2, n % 2
                    h = bass.ds(2 * j + i, 1)
                    nc.vector.tensor_tensor(gated[n % 4][:].unsqueeze(1), gates[:, t, bass.ds(2 * j + i + H, 1), :].unsqueeze(3).to_broadcast([P, 1, E, PH]),
                                            v[:, t, h, :].unsqueeze(2).to_broadcast([P, 1, E, PH]), ALU.mult).then_inc(gated_ready, 1)

                def add(t):
                    dve.wait_ge(made, T * (j + 2) + t + 1)
                    nc.vector.tensor_tensor(x_norm[:, t, :], x_norm[:, t, :], psY[t % 4][:], ALU.add).then_inc(added, 1)

                dve.wait_ge(added, T * j + 4)
                for n in range(3):
                    gate(n)
                for n in range(NJ):
                    dve.wait_ge(hi, NJ * j + n + 1)
                    nc.vector.tensor_tensor(gatedT[n % 4][1][:].rearrange("p c k -> p (c k)"), psT[n % 4][:],
                                            gatedT[n % 4][0][:].rearrange("p c k -> p (c k)"), ALU.subtract).then_inc(lo, 1)
                    if n + 3 < NJ:
                        gate(n + 3)
                    if n % 2 == 1 and n >= 3:
                        add(n // 2 - 1)
                add(T - 1)


def feed_forward(nc, x_tokens, y, identity, t, out_dram):
    FT = F // P
    with ExitStack() as ctx:
        def sb(name, shape, dt=F32):
            return ctx.enter_context(nc.sbuf_tensor(name, shape, dt))

        def sem(name):
            return ctx.enter_context(nc.semaphore(f"ff_{name}"))

        stats, mean_var, rstd = sb("ff_stats", [P, B, 6]), sb("ff_mean_var", [P, B, 2]), sb("ff_rstd", [P, B, 2])
        rows = {n: sb(f"ff_{n}", [P, D]) for n in ("ln1_g", "ln1_b", "ln2_g", "ln2_b", "b2")}
        b1 = sb("ff_b1", [P, FT])
        w1 = [sb(f"ff_w1_{p}", [P, DC, F], HALF) for p in ("hi", "lo")]
        w2 = [sb(f"ff_w2_{p}", [P, FT, D], HALF) for p in ("hi", "lo")]
        yT = [sb(f"ff_yT_{p}", [P, DC, T * P], HALF) for p in ("hi", "lo")]
        hT = [sb(f"ff_hT_{p}", [P, FT, T * P], HALF) for p in ("hi", "lo")]
        raw = [sb(f"ff_raw{i}", [P, F // 2]) for i in range(2)]
        relu = [sb(f"ff_relu{i}", [P, 512]) for i in range(2)]
        bank = [ctx.enter_context(nc.psum_tensor(f"ff_bank{i}", [P, 512], F32)) for i in range(8)]
        raw_in = [sem(f"raw_in{i}") for i in range(2)]
        names = ("passed", "rows_in", "chain", "var_ready", "std_ready", "chain2", "var2_ready", "std2_ready", "w_hi", "w_lo", "normed", "turned", "turned_hi",
                 "turned_lo", "hidden", "rectified", "hidden_hi", "hidden_lo", "made", "stored", "bank_free", "ended")
        s = {n: sem(n) for n in names}
        NW = 16
        block = ctx.enter_context(nc.Block())

        def piece(i):
            if i < 8:
                c, half = i // 2, i % 2
                cols = slice(half * (F // 2), (half + 1) * (F // 2))
                return t["W1"].rearrange("(p c) n -> p c n", c=DC)[:, c, cols], [x[:, c, cols] for x in w1]
            n = i - 8
            return t["W2"].rearrange("(f p) n -> p f n", p=P)[:, 2 * n:2 * n + 2, :], [x[:, 2 * n:2 * n + 2, :].rearrange("p f n -> p (f n)") for x in w2]

        @block.sync
        def _(sp):
            for i in range(NW):
                if i >= 2:
                    sp.wait_ge(s["w_lo"], i - 1)
                src = piece(i)[0]
                to = raw[i % 2][:] if i < 8 else raw[i % 2][:].rearrange("p (f n) -> p f n", n=D)
                sp.dma_start(to, src).then_inc(raw_in[i % 2], 16)
                if i == 1:
                    for n, row in rows.items():
                        sp.dma_start(row[:], t[n].rearrange("(a d) -> a d", a=1).broadcast_to([P, D])).then_inc(s["rows_in"], 16)
                    with nc.allow_non_contiguous_dma("a short column of biases"):
                        sp.dma_start(b1[:], t["b1"].rearrange("(f p) -> p f", p=P)).then_inc(s["rows_in"], 16)
            for b in range(B):
                sp.wait_ge(s["ended"], b + 1)
                sp.dma_start(out_dram[b], x_tokens[:, b, :]).then_inc(s["stored"], 16)
            sp.wait_ge(s["stored"], 16 * B)

        @block.gpsimd
        def _(pool):
            for i in range(NW):
                hi, lo = piece(i)[1]
                if i >= 8:
                    pool.wait_ge(raw_in[i % 2], 16 * (i // 2) + 16)
                    nc.gpsimd.tensor_copy(hi, raw[i % 2][:]).then_inc(s["w_hi"], 1)
                pool.wait_ge(s["w_hi"], i + 1)
                nc.gpsimd.tensor_tensor(lo, raw[i % 2][:], hi, ALU.subtract).then_inc(s["w_lo"], 1)

        @block.tensor
        def _(pe):
            for b in range(T):
                pe.wait_ge(s["normed"], b + 1)
                if b >= 2:
                    pe.wait_ge(s["turned_lo"], b - 1)
                for c in range(DC):
                    ins = nc.tensor.transpose(bank[b % 2][:, c * P:(c + 1) * P], y[:, b, c::DC], identity[:])
                ins.then_inc(s["turned"], 1)
            pe.wait_ge(s["turned_lo"], T)
            pe.wait_ge(s["w_lo"], 8)
            with pe.Fori(0, FT) as f:
                for half in range(2):
                    pe.wait_ge(s["bank_free"], 2 * f + half + 1)
                    left = [[x[:, c, bass.ds(f * P, P)] for c in range(DC)] for x in w1]
                    right = [[x[:, c, half * 512:(half + 1) * 512] for c in range(DC)] for x in yT]
                    split_product(nc, bank[2 + half][:], *left, *right).then_inc(s["hidden"], 1)
            pe.wait_ge(s["hidden_lo"], 2 + 2 * FT)
            pe.wait_ge(s["w_lo"], NW)
            for b in range(T):
                if b >= 4:
                    pe.wait_ge(s["chain2"], 2 * (b - 4) + 1)
                left = [[x[:, f, b * P:(b + 1) * P] for f in range(FT)] for x in hT]
                right = [[x[:, f, :] for f in range(FT)] for x in w2]
                split_product(nc, bank[4 + b % 4][:], *left, *right).then_inc(s["made"], 1)

        @block.scalar
        def _(act):
            norm_stats_scalar(nc, act, rstd, s["var_ready"], s["std_ready"])

            def weights(pieces):
                for i in pieces:
                    act.wait_ge(raw_in[i % 2], 16 * (i // 2) + 16)
                    nc.scalar.copy(piece(i)[1][0], raw[i % 2][:]).then_inc(s["w_hi"], 1)

            weights(range(2))
            for b in range(T):
                act.wait_ge(s["turned"], b + 1)
                nc.scalar.copy(yT[0][:, :, b * P:(b + 1) * P], bank[b % 2][:].rearrange("p (c k) -> p c k", k=P)).then_inc(s["turned_hi"], 1)
            weights(range(2, 8))
            act.wait_ge(s["rows_in"], 96)
            with act.Fori(0, FT) as f:
                for half in range(2):
                    cols = slice(half * 512, (half + 1) * 512)
                    act.wait_ge(s["hidden"], 2 * f + half + 1)
                    act.wait_ge(s["hidden_lo"], 2 * f + half + 1)
                    act.sem_inc(s["passed"], 1)
                    nc.scalar.activation(relu[half][:], bank[2 + half][:], ACT.Relu, bias=b1[:, bass.ds(f, 1)]).then_inc(s["bank_free"], 1)
                    act.wait_ge(s["bank_free"], 2 * f + half + 3)
                    nc.scalar.copy(hT[0][:, bass.ds(f, 1), cols], relu[half][:].unsqueeze(1)).then_inc(s["hidden_hi"], 1)
            act.wait_ge(s["var2_ready"], 1)
            nc.scalar.activation(rstd[:, :, 0], rstd[:, :, 0], ACT.Sqrt).then_inc(s["std2_ready"], 1)

        @block.vector
        def _(dve):
            nc.vector.memset(relu[0][:], 0.0).then_inc(s["bank_free"], 2)
            nc.vector.memset(relu[1][:], 0.0).then_inc(s["hidden_lo"], 2)
            link = norm_stats_vector(nc, dve, y, stats, mean_var, rstd, s["chain"], s["var_ready"], s["std_ready"])
            dve.wait_ge(s["rows_in"], 96)
            for b in range(B):
                link.mark(nc.vector.tensor_scalar(y[:, b, :], y[:, b, :], mean_var[:, b, 0:1], rstd[:, b, 1:2], ALU.subtract, ALU.mult))
            link.wait()
            for b in range(B):
                link.mark(nc.vector.tensor_tensor(y[:, b, :], y[:, b, :], rows["ln1_g"][:], ALU.mult))
            link.wait()
            for b in range(B):
                nc.vector.tensor_tensor(y[:, b, :], y[:, b, :], rows["ln1_b"][:], ALU.add).then_inc(s["normed"], 1)
            for b in range(T):
                tile = slice(b * P, (b + 1) * P)
                dve.wait_ge(s["turned_hi"], b + 1)
                nc.vector.tensor_tensor(yT[1][:, :, tile], bank[b % 2][:].rearrange("p (c k) -> p c k", k=P), yT[0][:, :, tile], ALU.subtract).then_inc(s["turned_lo"], 1)
            with dve.Fori(0, FT) as f:
                for half in range(2):
                    cols = slice(half * 512, (half + 1) * 512)
                    dve.wait_ge(s["hidden_hi"], 2 * f + half + 1)
                    nc.vector.tensor_tensor(hT[1][:, bass.ds(f, 1), cols], relu[half][:].unsqueeze(1), hT[0][:, bass.ds(f, 1), cols], ALU.subtract)\
                        .then_inc(s["hidden_lo"], 1)
            for b in range(T):
                dve.wait_ge(s["made"], b + 1)
                nc.vector.tensor_tensor(y[:, b, :], y[:, b, :], bank[4 + b % 4][:], ALU.add).then_inc(s["chain2"], 1)
                dve.wait_ge(s["chain2"], 2 * b + 1)
                nc.vector.tensor_tensor(y[:, b, :], y[:, b, :], rows["b2"][:], ALU.add).then_inc(s["chain2"], 1)
            dve.wait_ge(s["chain2"], 2 * T)
            link = Link(dve, s["chain"], base=link.n)
            for b in range(B):
                link.mark(nc.vector.bn_stats(stats[:, b, :], y[:, b, :]))
            link.wait()
            for b in range(B):
                link.mark(nc.vector.bn_aggr(mean_var[:, b, :], stats[:, b, :]))
            link.wait()
            nc.vector.tensor_scalar(rstd[:, :, 0], mean_var[:, :, 1], EPS, None, ALU.add).then_inc(s["var2_ready"], 1)
            dve.wait_ge(s["std2_ready"], 1)
            link.now(nc.vector.reciprocal(rstd[:, :, 1], rstd[:, :, 0]))
            for b in range(B):
                link.mark(nc.vector.tensor_scalar(y[:, b, :], y[:, b, :], mean_var[:, b, 0:1], rstd[:, b, 1:2], ALU.subtract, ALU.mult))
            link.wait()
            for b in range(B):
                link.mark(nc.vector.tensor_tensor(y[:, b, :], y[:, b, :], rows["ln2_g"][:], ALU.mult))
            link.wait()
            for b in range(B):
                link.mark(nc.vector.tensor_tensor(y[:, b, :], y[:, b, :], rows["ln2_b"][:], ALU.add))
            link.wait()
            for b in range(B):
                nc.vector.tensor_tensor(x_tokens[:, b, :], x_tokens[:, b, :], y[:, b, :], ALU.add).then_inc(s["ended"], 1)




def perceiver(nc, x, ctx_1024, mask, t, cos, sin, out):
    xattn, ffn = ({k[len(pre):].replace("W", "w") if pre == "L0_xattn_" else k[len(pre):]: v for k, v in t.items() if k.startswith(pre)}
                  for pre in ("L0_xattn_", "L0_ffn_"))
    with ExitStack() as ctx:
        def sb(name, shape, dt=F32):
            return ctx.enter_context(nc.sbuf_tensor(name, shape, dt))

        x_tokens = sb("x_tokens", [P, B, D])
        identity = sb("identity", [P, P])
        cross_attention(nc, x_tokens, identity, xattn, ctx_1024, mask, x)
        segment_attention(nc, x_tokens, identity, t["L0_attn_W_qkv"], t["L0_attn_W_out"])
        x_norm = sb("x_norm", [P, T, D])
        with ExitStack() as moe:
            xT = [moe.enter_context(nc.sbuf_tensor(f"xT_{p}", [P, DC, T * P], HALF)) for p in ("hi", "lo")]
            gates = moe.enter_context(nc.sbuf_tensor("gates", [P, T, 2 * H, E], F32))
            v = moe.enter_context(nc.sbuf_tensor("v", [P, T, H, PH], F32))
            gate_stage(nc, x_tokens, x_norm, xT, gates, identity, ffn["Wsel_v"], ffn["Wsel_o"])
            expert_values(nc, xT, gates, v, ffn["Wv"])
            rotary_attention(nc, xT, v, identity, ffn["Wq"], ffn["Wk"], cos, sin)
            expert_outputs(nc, x_norm, v, gates, identity, ffn["Wo"])
        feed_forward(nc, x_tokens, x_norm, identity, ffn, out)


def kernel(**inputs):
    import numpy as _np
    import concourse.bacc as _bacc
    from concourse import mybir as _mybir
    from concourse.bass_utils import run_bass_kernel_spmd as _run

    nc = _bacc.Bacc("TRN2", target_bir_lowering=False, num_devices=1)
    arrays = {name: _np.ascontiguousarray(a) for name, a in inputs.items()}
    arrays["mask_BxS2_bk1"] = arrays["mask_BxS2_bk1"].view(_np.int32)
    freq = _np.float32(10000.0) ** (-_np.arange(ROT // 2, dtype=_np.float32) / _np.float32(ROT // 2))
    angle = _np.arange(P, dtype=_np.float32)[:, None] * freq[None, :]
    arrays["rope_cos"], arrays["rope_sin"] = _np.cos(angle), _np.sin(angle)
    args = {name: nc.dram_tensor(f"in_{name}", a.shape, _mybir.dt.from_np(a.dtype), kind="ExternalInput").ap() for name, a in arrays.items()}
    out = nc.dram_tensor("out_x", (B, P, D), F32, kind="ExternalOutput").ap()
    x, context, mask, cos, sin = (args.pop(n) for n in ("x", "ctx_1024", "mask_BxS2_bk1", "rope_cos", "rope_sin"))
    perceiver(nc, x, context, mask, args, cos, sin, out)
    return _run(nc, [{f"in_{name}": a for name, a in arrays.items()}], core_ids=[0]).results[0]["out_x"]
```

```python
from contextlib import ExitStack

import concourse.bass as bass
from concourse import mybir
from concourse.alu_op_type import AluOpType as ALU

F32 = mybir.dt.float32
U8 = mybir.dt.uint8
HALF = mybir.dt.bfloat16
ACT = mybir.ActivationFunctionType
AX = mybir.AxisListType

P = 128
B = 8
D = 512
DC = D // P
SK = 2048
H = 16
DH = D // H
HG = P // DH
G = H // HG
EPS = 1e-5
MASKED = 1e30


class Link:

    def __init__(self, eng, sem, base=0):
        self.eng, self.sem, self.base, self.n = eng, sem, base, 0

    def mark(self, ins):
        self.n += 1
        ins.then_inc(self.sem, 1)
        return self.n

    def wait(self, n=None):
        self.eng.wait_ge(self.sem, self.base + (self.n if n is None else n))

    def now(self, ins):
        self.mark(ins)
        self.wait()


def split_product(nc, out, left_hi, left_lo, right_hi, right_lo, first=True, last=True, begun=None):
    n = len(left_hi)
    for c in range(n):
        ins = nc.tensor.matmul(out, left_hi[c], right_hi[c], start=(first and c == 0), stop=False)
        if begun is not None and c == 0:
            ins.then_inc(begun, 1)
        nc.tensor.matmul(out, left_hi[c], right_lo[c], start=False, stop=False)
        ins = nc.tensor.matmul(out, left_lo[c], right_hi[c], start=False, stop=(last and c == n - 1))
    return ins


def cross_order(last):
    K, V = (lambda n, kc: ("project", ("k", n), kc)), (lambda n, kc: ("project", ("v", n), kc))
    context_at = {(10, 1): [0], (10, 2): [1], (11, 0): [2, 3], (11, 1): [4], (11, 2): [5, 6], (12, 0): [7], (12, 1): [8, 9], (12, 2): [10, 11],
                  (13, 0): [12, 13], (13, 1): [14, 15]}

    def context(h, place):
        for a in context_at.get((h, place), []) if not last else []:
            yield "context", a, 0
            if a % 2 and a // 2 + 2 < 8:
                yield "load", a // 2 + 2, 0

    for h in range(H):
        n, r = h // HG + 1, h % HG
        kind, kc = K if r < 2 else V, r % 2 * 2
        early, late = ([kind(n % G, kc)], [kind(n % G, kc + 1)]) if n < G or not last else ([], [])
        if h == 8 and not last:
            yield "load", 0, 0
            yield "load", 1, 0
            yield "mask", 0, 0
        if h:
            yield "values", h - 1, 3
        yield "turn", h, 0
        if not (last and h + 1 == H):
            yield "score", (h + 1) % H, 2
        yield "turn", h, 1
        if not (last and h + 1 == H):
            yield "score", (h + 1) % H, 3
        yield from context(h, 0)
        if not (last and h + 1 == H):
            yield "exp", (h + 1) % H, 0
        if h:
            yield "gather", h - 1, 0
        if h == 4 and not last:
            yield "norm", 0, 0
        yield from early
        yield "turn", h, 2
        yield "values", h, 0
        yield "turn", h, 3
        yield "values", h, 1
        yield from context(h, 1)
        if not (last and h + 2 >= H):
            yield "score", (h + 2) % H, 0
            yield "score", (h + 2) % H, 1
        if h == 3:
            yield "queries", 1, 0
        if h == 7 and not last:
            yield "queries", 0, 0
        if h < H - 1:
            yield from late
        if late and r < 2:
            yield "ship", n % G, r
        if h == 13 and not last:
            yield "masked", 0, 0
        yield from context(h, 2)
        if h == 5 and not last:
            yield "latents", 0, 0
        yield "values", h, 2
    yield "values", H - 1, 3
    yield "gather", H - 1, 0
    yield from late
    yield "output", 0, 0


def cross_start():
    yield "weight", 0, 0
    for a in range(4):
        yield "context", a, 0
        if a % 2:
            yield "load", a // 2 + 2, 0
    yield "weight", 1, 0
    for kc in range(4):
        for what in "kv":
            for a in (4 * kc + 4, 4 * kc + 5) if what == "k" else (4 * kc + 6, 4 * kc + 7):
                if a < 16:
                    yield "context", a, 0
                    if a % 2 and a // 2 + 2 < 8:
                        yield "load", a // 2 + 2, 0
            yield "project", (what, 0), kc
            if what == "k" and kc % 2:
                yield "ship", 0, kc // 2
            yield from {"k0": [("norm", 0, 0)], "v0": [("weight", 2, 0), ("latents", 0, 0)], "k1": [("masked", 0, 0)], "v1": [("queries", 0, 0)],
                        "k2": [("weight", 3, 0)]}.get(f"{what}{kc}", [])
    for j in range(4):
        yield "score", 0, j
    yield "exp", 0, 0
    for j in range(2):
        yield "score", 1, j


POOL_OF = {"score": "S", "turn": "T", "context": "T", "latents": "T", "queries": "T", "project": "P"}
BANKS = {"S": 2, "T": 3, "P": 2, "O": 1}
SPLIT_ORDER = ("wk", "wv", "wq", "wo")


class Walk:

    def __init__(self, items, base, ahead):
        self.items, self.base, self.ahead, self.n, self.at = list(items), base, ahead, {k: 0 for k in base}, {}

    def __iter__(self):
        for kind, a, k in self.items:
            pools = ("T", "O") if kind == "output" else ("O",) if kind == "values" and k == 0 else (POOL_OF[kind],) if kind in POOL_OF else ()
            self.use = {p: self.base[p] + self.n[p] for p in pools}
            self.bank = {p: (self.ahead[p] + self.n[p]) % BANKS[p] for p in pools}
            for p in pools:
                self.n[p] += 1
                self.at[kind, a, k] = self.base[p] + self.n[p]
            yield kind, a, k


def cross_attention(nc, x_tokens, identity, t, ctx_dram, mask_dram, x_dram):
    KEYS = SK // 8
    none = {p: 0 for p in "STPO"}
    count = {p: {} for p in "STPO"}
    for name, items in (("start", cross_start()), ("round", cross_order(False))):
        w = Walk(items, none, none)
        for _ in w:
            pass
        for p in "STPO":
            count[p][name] = w.n[p]

    def walk(b):
        if b is None:
            return Walk(cross_start(), none, none)
        return Walk(cross_order(isinstance(b, int)), {p: count[p]["start"] + count[p]["round"] * b for p in "STPO"},
                    {p: count[p]["start"] for p in "STPO"})

    with ExitStack() as ctx:
        def sb(name, shape, dt=F32):
            return ctx.enter_context(nc.sbuf_tensor(name, shape, dt))

        def sem(name):
            return ctx.enter_context(nc.semaphore(f"xa_{name}"))

        weights = {n: [sb(f"xa_{n}_{part}", [P, DC, D], HALF) for part in ("hi", "lo")] for n in ("wq", "wk", "wv", "wo")}
        raw = [sb(f"xa_raw{i}", [P, 2, D]) for i in range(2)]
        bq_col, bk_col = sb("xa_bq_col", [P, G]), sb("xa_bk_col", [P, G])
        bv_row, bo_row = sb("xa_bv_row", [P, D]), sb("xa_bo_row", [P, D])
        stats, mean_var, rstd = sb("xa_stats", [P, B, 6]), sb("xa_mean_var", [P, B, 2]), sb("xa_rstd", [P, B, 2])
        x_norm = sb("xa_x_norm", [P, D])
        xT = [sb(f"xa_xT_{p}", [P, DC, P], HALF) for p in ("hi", "lo")]
        q_full = sb("xa_q_full", [P, 2, P])
        q_parts = [sb(f"xa_q_{p}", [P, 2, P], HALF) for p in ("hi", "lo")]
        q_lanes = sb("xa_q_lanes", [P, H, P], HALF)
        ctxT = [sb(f"xa_ctxT_{p}", [P, DC, SK], HALF) for p in ("hi", "lo")]
        k_parts = [sb(f"xa_k_{p}", [P, SK], HALF) for p in ("hi", "lo")]
        k_lanes = sb("xa_k_lanes", [P, 2 * HG, SK], HALF)
        v = sb("xa_v", [P, SK // P, 2, HG, 2, DH], HALF)
        mask_words = sb("xa_mask_words", [P, SK // 4], mybir.dt.int32)
        mask_add = sb("xa_mask_add", [P, SK], mybir.dt.bfloat16)
        probs = [sb(f"xa_probs{i}", [P, SK]) for i in range(2)]
        row_max, neg_max = sb("xa_row_max", [P, 2, 4]), sb("xa_neg_max", [P, 2])
        row_sum, inv_sum = sb("xa_row_sum", [P, H]), sb("xa_inv_sum", [P, H])
        pT = [sb(f"xa_pT_{p}", [P, SK // P, P], HALF) for p in ("hi", "lo")]
        o_part = sb("xa_o_part", [P, 2, DH])
        o_tokens = sb("xa_o_tokens", [P, D])
        oT = [sb(f"xa_oT_{p}", [P, DC, P], HALF) for p in ("hi", "lo")]
        start = sb("xa_start", [P, 6])
        y = x_norm

        psum = {p: [ctx.enter_context(nc.psum_tensor(f"xa_ps{p}{i}", [P, 512], F32)) for i in range(BANKS[p])] for p in "STPO"}
        psO = psum["O"][0]

        x_in, bias_in, ident_done = sem("x_in"), sem("bias_in"), sem("ident")
        w_in = [sem(f"w_in{i}") for i in range(4)]
        w_hi, w_lo = sem("w_hi"), sem("w_lo")
        raw_in = [sem(f"raw_in{i}") for i in range(2)]
        mask_in, mask_ready = sem("mask_in"), sem("mask_ready")
        var_ready, std_ready, norm_ready = sem("var_ready"), sem("std_ready"), sem("norm_ready")
        full = {p: sem(f"{p}_full") for p in "STPO"}
        high = {p: sem(f"{p}_high") for p in "TP"}
        free = {p: sem(f"{p}_free") for p in "STPO"}
        q_sum, q_hi, q_ready = sem("q_sum"), sem("q_hi"), sem("q_ready")
        k_in, q_in = [sem(f"k_in{i}") for i in range(2)], sem("q_in")
        max_ready, probs_ready = sem("max_ready"), sem("probs_ready")
        link_sem, prep_sem, pool_sem = sem("link"), sem("prep"), sem("pool")
        passed = {n: sem(f"passed_{n}") for n in ("sp", "pool", "dve")}

        def batch(b):
            return -1 if b is None else b

        def queries_of(b, half):
            return 1 if b is None else 2 * b + (2 if half else 3)

        SHIPPED = 16 * 3 * HG

        def keys_of(b, n):
            return 1 if b is None else 4 * b + (n + 1 if n else 5)

        w_raw = [probs[i][:].rearrange("p (c n) -> p c n", c=DC) for i in range(2)]

        block = ctx.enter_context(nc.Block())

        @block.sync
        def _(sp):
            def load_weight(i):
                n = SPLIT_ORDER[i]
                src = t[n].rearrange("(c p) n -> p c n", p=P) if n == "wo" else t[n].rearrange("(p c) n -> p c n", c=DC)
                sp.dma_start(w_raw[i % 2], src).then_inc(w_in[i], 16)

            def load_mask(b):
                sp.wait_ge(mask_ready, b + 1)
                sp.sem_inc(passed["sp"], 1)
                sp.dma_start(mask_words[:], mask_dram[b:b + 1, :].broadcast_to([P, SK // 4]) if isinstance(b, int) else
                             mask_dram[bass.ds(b, 1), :].broadcast_to([P, SK // 4])).then_inc(mask_in, 16)

            def run(b):
                w = walk(b)
                for kind, a, k in w:
                    if kind == "mask":
                        load_mask(b + 1)
                    elif kind == "ship":
                        sp.wait_ge(free["P"], w.at["project", ("k", a), 2 * k + 1] + 2)
                        sp.sem_inc(passed["sp"], 1)
                        keys = slice(1024 * k, 1024 * (k + 1))
                        for i in range(HG):
                            for lanes, part in enumerate((0, 1, 0)):
                                sp.dma_start(k_lanes[lanes * DH:(lanes + 1) * DH, a % 2 * HG + i, keys],
                                             k_parts[part][i * DH:(i + 1) * DH, keys]).then_inc(k_in[k], 16)
                    elif kind == "queries":
                        sp.wait_ge(q_ready, queries_of(b, a))
                        sp.sem_inc(passed["sp"], 1)
                        for i in range(HG):
                            for lanes, part in enumerate((0, 0, 1)):
                                sp.dma_start(q_lanes[lanes * DH:(lanes + 1) * DH, 8 * a + i:8 * a + i + HG + 1:HG, :],
                                             q_parts[part][i * DH:(i + 1) * DH, :, :]).then_inc(q_in, 16)

            load_weight(0)
            load_weight(1)
            with nc.allow_non_contiguous_dma("two short columns of biases"):
                sp.dma_start(bk_col[:], t["bk"].rearrange("(g p) -> p g", p=P)).then_inc(bias_in, 16)
                sp.dma_start(bq_col[:], t["bq"].rearrange("(g p) -> p g", p=P)).then_inc(bias_in, 16)
            sp.dma_start(bv_row[:], t["bv"].rearrange("(a d) -> a d", a=1).broadcast_to([P, D])).then_inc(bias_in, 16)
            sp.dma_start(bo_row[:], t["bo"].rearrange("(a d) -> a d", a=1).broadcast_to([P, D])).then_inc(bias_in, 16)
            sp.dma_start(x_tokens[:], x_dram.rearrange("b p d -> p b d")).then_inc(x_in, 16)
            for i in (2, 3):
                sp.wait_ge(w_lo, i - 1)
                load_weight(i)
            load_mask(0)
            run(None)
            with sp.Fori(0, B - 1) as b:
                run(b)
            run(B - 1)

        @block.gpsimd
        def _(pool):
            link = Link(pool, pool_sem)
            link.now(nc.gpsimd.memset(identity[:], 0.0))
            nc.gpsimd.affine_select(out=identity[:], in_=identity[:], compare_op=ALU.not_equal, fill=1.0, base=0,
                                    pattern=[[-1, P]], channel_multiplier=1).then_inc(ident_done, 1)
            nc.gpsimd.memset(start[:, 0:1], 0.0).then_inc(mask_ready, 1)

            def load_context(b, e):
                src = ctx_dram[b:b + 1] if isinstance(b, int) else ctx_dram[bass.ds(b, 1)]
                src = src[:, e * KEYS:(e + 1) * KEYS, :].rearrange("a (k p) d -> p (a k) d", p=P)
                pool.dma_start(raw[e % 2][:], src).then_inc(raw_in[e % 2], 16)

            def mask(b):
                pool.wait_ge(mask_in, 16 * b + 16)
                pool.wait_ge(free["S"], count["S"]["round"] * b + BANKS["S"])
                pool.sem_inc(passed["pool"], 1)
                nc.gpsimd.tensor_scalar(mask_add[:], mask_words[:].bitcast(U8), -1.0, MASKED, ALU.add, ALU.mult).then_inc(mask_ready, 1)

            load_context(0, 0)
            load_context(0, 1)

            def run(b):
                w = walk(b)
                for kind, a, k in w:
                    if kind == "load":
                        if a >= 2:
                            pool.wait_ge(full["T"], w.at["context", 2 * (a - 2) + 1, 0])
                        else:
                            pool.wait_ge(full["T"], w.base["T"])
                        pool.sem_inc(passed["pool"], 1)
                        load_context(0 if b is None else b + 1, a)
                    elif kind == "masked":
                        mask(0 if b is None else b + 1)

            run(None)
            with pool.Fori(0, B - 1) as b:
                run(b)

        @block.tensor
        def _(pe):
            pe.wait_ge(ident_done, 1)

            def bank(pool, w):
                pe.wait_ge(free[pool], w.use[pool] + 1)
                return psum[pool][w.bank[pool]]

            def run(b):
                w = walk(b)
                for kind, a, k in w:
                    if kind == "score":
                        h, j = a, k
                        out = bank("S", w)
                        if h % (H // 2) == 0 and j == 0:
                            pe.wait_ge(q_in, SHIPPED * queries_of(b, h // (H // 2)))
                        if h % HG == 0 and j % 2 == 0:
                            pe.wait_ge(k_in[j // 2], SHIPPED * keys_of(b, h // HG))
                        nc.tensor.matmul(out[:], q_lanes[0:3 * DH, h, :], k_lanes[0:3 * DH, h % (2 * HG), 512 * j:512 * (j + 1)],
                                         start=True, stop=True).then_inc(full["S"], 1)
                    elif kind == "turn":
                        out = bank("T", w)
                        if k == 0:
                            pe.wait_ge(probs_ready, H * b + a + 1)
                        for n in range(4):
                            kt = 4 * k + n
                            ins = nc.tensor.transpose(out[:, n * P:(n + 1) * P], probs[a % 2][:, kt * P:(kt + 1) * P], identity[:])
                        ins.then_inc(full["T"], 1)
                    elif kind == "values":
                        if k == 0:
                            bank("O", w)
                            if a == 0:
                                pe.wait_ge(free["P"], w.base["P"] + 2)
                        if a and a % HG == 0:
                            pe.wait_ge(free["P"], w.at["project", ("v", a // HG), k] + 2)
                        pe.wait_ge(free["T"], w.at["turn", a, k] + BANKS["T"])
                        for n in range(4):
                            kt = 4 * k + n
                            first, last = kt == 0, kt == SK // P - 1
                            both = (pT[0][:, kt, :], v[:, kt, a // HG % 2, a % HG, :, :], psO[:, 0:2 * DH])
                            low = (pT[1][:, kt, :], v[:, kt, a // HG % 2, a % HG, 0, :], psO[:, 0:DH])
                            for m, (left, right, to) in enumerate((low, both) if last else (both, low)):
                                ins = nc.tensor.matmul(to, left, right, start=(first and m == 0), stop=(last and m == 1))
                        if k == 3:
                            ins.then_inc(full["O"], 1)
                    elif kind == "context":
                        out = bank("T", w)
                        e, cp = a // 2, a % 2
                        if cp == 0:
                            pe.wait_ge(raw_in[e % 2], 64 * (batch(b) + 1) + 16 * (e // 2 + 1))
                        for c in range(2):
                            for n in range(2):
                                ins = nc.tensor.transpose(out[:, (2 * c + n) * P:(2 * c + n + 1) * P], raw[e % 2][:, n, 2 * cp + c::DC], identity[:])
                        ins.then_inc(full["T"], 1)
                    elif kind == "latents":
                        out = bank("T", w)
                        pe.wait_ge(norm_ready, batch(b) + 2)
                        for c in range(DC):
                            ins = nc.tensor.transpose(out[:, c * P:(c + 1) * P], x_norm[:, c::DC], identity[:])
                        ins.then_inc(full["T"], 1)
                    elif kind == "queries":
                        out = bank("T", w)
                        if b is None:
                            pe.wait_ge(w_lo, 3)
                        if a == 0:
                            pe.wait_ge(free["T"], w.at["latents", 0, 0] + BANKS["T"])
                        for gl in range(2):
                            g = 2 * a + gl
                            left = [[x[:, c, g * P:(g + 1) * P] for c in range(DC)] for x in weights["wq"]]
                            ins = split_product(nc, out[:, gl * P:(gl + 1) * P], *left, *[[x[:, c, :] for c in range(DC)] for x in xT])
                        ins.then_inc(full["T"], 1)
                    elif kind == "project":
                        out = bank("P", w)
                        (what, n), kc = a, k
                        if n == 0:
                            pe.wait_ge(free["T"], w.at["context", 4 * kc + 3, 0] + BANKS["T"])
                        if b is None and kc == 0:
                            pe.wait_ge(w_lo, 1 if what == "k" else 2)
                        lanes = slice(n * P, (n + 1) * P)
                        if what == "k":
                            left = [[x[:, c, lanes] for c in range(DC)] for x in weights["wk"]]
                            ins = split_product(nc, out[:], *left, *[[x[:, c, kc * 512:(kc + 1) * 512] for c in range(DC)] for x in ctxT])
                        else:
                            for m in range(4):
                                left = [[x[:, c, (4 * kc + m) * P:(4 * kc + m + 1) * P] for c in range(DC)] for x in ctxT]
                                ins = split_product(nc, out[:, m * P:(m + 1) * P], *left, *[[x[:, c, lanes] for c in range(DC)] for x in weights["wv"]])
                        ins.then_inc(full["P"], 1)
                    elif kind == "output":
                        out = bank("T", w)
                        pe.wait_ge(free["O"], w.use["O"] + 1)
                        for c in range(DC):
                            ins = nc.tensor.transpose(out[:, c * P:(c + 1) * P], o_tokens[:, c * P:(c + 1) * P], identity[:])
                        ins.then_inc(full["T"], 1)
                        pe.wait_ge(free["T"], w.use["T"] + 1 + BANKS["T"])
                        split_product(nc, psO[:], *[[x[:, c, :] for c in range(DC)] for x in oT],
                                      *[[x[:, c, :] for c in range(DC)] for x in weights["wo"]]).then_inc(full["O"], 1)

            run(None)
            pe.wait_ge(w_lo, 4)
            with pe.Fori(0, B - 1) as b:
                run(b)
            run(B - 1)

        @block.scalar
        def _(act):

            def run(b):
                w = walk(b)
                for kind, a, k in w:
                    if kind == "weight":
                        act.wait_ge(w_in[a], 16)
                        nc.scalar.copy(weights[SPLIT_ORDER[a]][0][:], w_raw[a % 2]).then_inc(w_hi, 1)
                        if a == 1:
                            act.wait_ge(bias_in, 64)
                    elif kind == "norm" and b is None:
                        norm_stats_scalar(nc, act, rstd, var_ready, std_ready)
                    elif kind in ("turn", "context", "latents", "output"):
                        act.wait_ge(full["T"], w.use["T"] + 1)
                        src = psum["T"][w.bank["T"]][:]
                        if kind == "turn":
                            out = pT[0][:, 4 * k:4 * k + 4, :].rearrange("p k q -> p (k q)")
                        elif kind == "context":
                            out, src = ctxT[0][:, 2 * (a % 2):2 * (a % 2) + 2, (a // 2) * KEYS:(a // 2 + 1) * KEYS], src.rearrange("p (c k) -> p c k", c=2)
                        else:
                            out = (xT if kind == "latents" else oT)[0][:].rearrange("p c k -> p (c k)")
                        nc.scalar.copy(out, src).then_inc(high["T"], 1)
                    elif kind == "queries":
                        act.wait_ge(q_sum, queries_of(b, a))
                        if b is not None:
                            act.wait_ge(q_in, SHIPPED * (queries_of(b, a) - 1))
                        for i in range(2):
                            nc.scalar.copy(q_parts[0][:, i, :], q_full[:, i, :]).then_inc((high["T"], q_hi)[i], 1)
                    elif kind == "project":
                        act.wait_ge(full["P"], w.use["P"] + 1)
                        src = psum["P"][w.bank["P"]]
                        (what, n), kc = a, k
                        if what == "k":
                            if b is not None:
                                act.wait_ge(k_in[kc // 2], SHIPPED * (keys_of(b, n) - 1))
                            ins = nc.scalar.activation(k_parts[0][:, kc * 512:(kc + 1) * 512], src[:], ACT.Identity, bias=bk_col[:, n:n + 1])
                        else:
                            ins = nc.scalar.copy(v[:, 4 * kc:4 * kc + 4, n % 2, :, 0, :], src[:].rearrange("p (k h d) -> p k h d", k=4, d=DH))
                        ins.then_inc(high["P"], 1)
                    elif kind == "exp":
                        n = H * (batch(b) + (1 if a == 0 else 0)) + a
                        act.wait_ge(max_ready, n + 1)
                        nc.scalar.activation(probs[a % 2][:], probs[a % 2][:], ACT.Exp, bias=neg_max[:, a % 2:a % 2 + 1], scale=1.0,
                                             accum_out=row_sum[:, a:a + 1]).then_inc(probs_ready, 1)

            run(None)
            with act.Fori(0, B - 1) as b:
                run(b)
            run(B - 1)

        @block.vector
        def _(dve):
            for i, (s, n) in enumerate(tuple((free[p], BANKS[p]) for p in "STPO")):
                nc.vector.memset(start[:, i + 1:i + 2], 0.0).then_inc(s, n)

            def norm(b):
                x, mean, scale = ((x_tokens[:, b, :], mean_var[:, b, 0:1], rstd[:, b, 1:2]) if isinstance(b, int) else
                                  (x_tokens[:, bass.ds(b, 1), :], mean_var[:, bass.ds(b, 1), 0], rstd[:, bass.ds(b, 1), 1]))
                nc.vector.tensor_scalar(x_norm[:], x, mean, scale, ALU.subtract, ALU.mult).then_inc(norm_ready, 1)

            LINKS = 2 * H + 1

            def run(b):
                w = walk(b)
                link = None if b is None else Link(dve, link_sem, base=LINKS * b)
                inverse = {}
                for kind, a, k in w:
                    if kind == "score":
                        dve.wait_ge(full["S"], w.use["S"] + 1)
                        if a == 0 and k == 0:
                            dve.wait_ge(mask_ready, batch(b) + 3)
                        dve.sem_inc(passed["dve"], 1)
                        keys = slice(512 * k, 512 * (k + 1))
                        nc.vector.tensor_tensor_reduce(probs[a % 2][:, keys], psum["S"][w.bank["S"]][:], mask_add[:, keys],
                                                       DH ** -0.5, -3e38, ALU.add, ALU.max, row_max[:, a % 2, k:k + 1]).then_inc(free["S"], 1)
                    elif kind == "exp":
                        dve.wait_ge(free["S"], w.at["score", a, 3] + BANKS["S"])
                        nc.vector.tensor_reduce(neg_max[:, a % 2:a % 2 + 1], row_max[:, a % 2, :], AX.X, ALU.max, negate=True).then_inc(max_ready, 1)
                    elif kind == "weight":
                        dve.wait_ge(w_hi, a + 1)
                        nc.vector.tensor_tensor(weights[SPLIT_ORDER[a]][1][:], w_raw[a % 2], weights[SPLIT_ORDER[a]][0][:], ALU.subtract).then_inc(w_lo, 1)
                        if a == 1:
                            dve.wait_ge(bias_in, 64)
                    elif kind == "norm" and b is None:
                        dve.wait_ge(x_in, 16)
                        norm_stats_vector(nc, dve, x_tokens, stats, mean_var, rstd, prep_sem, var_ready, std_ready)
                        norm(0)
                    elif kind == "norm":
                        dve.wait_ge(free["O"], w.base["O"] + 1)
                        norm(b + 1)
                    elif kind in ("turn", "context", "latents", "output"):
                        dve.wait_ge(high["T"], w.use["T"] + 1)
                        src = psum["T"][w.bank["T"]][:]
                        if kind == "turn":
                            hi, out = (x[:, 4 * k:4 * k + 4, :].rearrange("p k q -> p (k q)") for x in pT)
                        elif kind == "context":
                            hi, out = (x[:, 2 * (a % 2):2 * (a % 2) + 2, (a // 2) * KEYS:(a // 2 + 1) * KEYS] for x in ctxT)
                            src = src.rearrange("p (c k) -> p c k", c=2)
                        else:
                            hi, out = (x[:].rearrange("p c k -> p (c k)") for x in (xT if kind == "latents" else oT))
                        nc.vector.tensor_tensor(out, src, hi, ALU.subtract).then_inc(free["T"], 1)
                        if kind == "turn" and k == 0:
                            inverse[a] = link.mark(nc.vector.reciprocal(inv_sum[:, a:a + 1], row_sum[:, a:a + 1]))
                    elif kind == "queries":
                        dve.wait_ge(full["T"], w.use["T"] + 1)
                        nc.vector.tensor_tensor(q_full[:], psum["T"][w.bank["T"]][:, 0:2 * P].rearrange("p (g k) -> p g k", g=2),
                                                bq_col[:, 2 * a:2 * a + 2].unsqueeze(2).to_broadcast([P, 2, P]), ALU.add).then_inc(q_sum, 1)
                        dve.wait_ge(q_hi, queries_of(b, a))
                        for i in range(2):
                            nc.vector.tensor_tensor(q_parts[1][:, i, :], q_full[:, i, :], q_parts[0][:, i, :], ALU.subtract).then_inc((free["T"], q_ready)[i], 1)
                    elif kind == "project":
                        dve.wait_ge(high["P"], w.use["P"] + 1)
                        src = psum["P"][w.bank["P"]]
                        (what, n), kc = a, k
                        if what == "k":
                            hi, out = (x[:, kc * 512:(kc + 1) * 512] for x in k_parts)
                            ins = nc.vector.scalar_tensor_tensor(out, src[:], bk_col[:, n:n + 1], hi, ALU.add, ALU.subtract)
                        else:
                            hi, out = (v[:, 4 * kc:4 * kc + 4, n % 2, :, part, :] for part in range(2))
                            ins = nc.vector.tensor_tensor(out, src[:].rearrange("p (k h d) -> p k h d", k=4, d=DH), hi, ALU.subtract)
                        ins.then_inc(free["P"], 1)
                    elif kind == "gather":
                        cols = slice(a * DH, (a + 1) * DH)
                        dve.wait_ge(full["O"], w.at["values", a, 0])
                        link.wait(inverse[a])
                        link.now(nc.vector.scalar_tensor_tensor(o_part[:, a % 2, :], psO[:, 0:DH], inv_sum[:, a:a + 1], bv_row[:, cols], ALU.mult, ALU.add))
                        nc.vector.scalar_tensor_tensor(o_tokens[:, cols], psO[:, DH:2 * DH], inv_sum[:, a:a + 1], o_part[:, a % 2, :], ALU.mult, ALU.add)\
                            .then_inc(free["O"], 1)
                    if kind == "output":
                        dve.wait_ge(full["O"], w.use["O"] + 1)
                        link.now(nc.vector.tensor_tensor(y[:], psO[:], bo_row[:], ALU.add))
                        x = x_tokens[:, b:b + 1, :] if isinstance(b, int) else x_tokens[:, bass.ds(b, 1), :]
                        nc.vector.tensor_tensor(x, x, y[:].unsqueeze(1), ALU.add).then_inc(free["O"], 1)

            run(None)
            with dve.Fori(0, B - 1) as b:
                run(b)
            run(B - 1)




class Steps:

    def __init__(self, sem, names):
        self.sem, self.names = sem, names.split()

    def start(self, ins):
        ins.then_inc(self.sem, len(self.names))

    def done(self, eng, name, j=0, before=False):
        eng.wait_ge(self.sem, len(self.names) * (j + (0 if before else 1)) + self.names.index(name) + 1)


def norm_stats_vector(nc, dve, x_tokens, stats, mean_var, rstd, chain, var_ready, std_ready):
    link = Link(dve, chain)
    for b in range(B):
        link.mark(nc.vector.bn_stats(stats[:, b, :], x_tokens[:, b, :]))
    link.wait()
    for b in range(B):
        link.mark(nc.vector.bn_aggr(mean_var[:, b, :], stats[:, b, :]))
    link.wait()
    nc.vector.tensor_scalar(rstd[:, :, 0], mean_var[:, :, 1], EPS, None, ALU.add).then_inc(var_ready, 1)
    dve.wait_ge(std_ready, 1)
    link.now(nc.vector.reciprocal(rstd[:, :, 1], rstd[:, :, 0]))
    return link


def norm_stats_scalar(nc, act, rstd, var_ready, std_ready):
    act.wait_ge(var_ready, 1)
    nc.scalar.activation(rstd[:, :, 0], rstd[:, :, 0], ACT.Sqrt).then_inc(std_ready, 1)


def every_second_key(xT):
    turns = xT[:, :, 0:120].rearrange("p n (r t) -> p n r t", t=24)
    return [(turns[:, :, :, 0:12:2], slice(0, 30)), (turns[:, :, :, 13:24:2], slice(30, 60)), (xT[:, :, 120:128:2], slice(60, 64))]


def segment_attention(nc, x_tokens, identity, w_qkv_dram, w_out_dram):
    SEL = P // 2
    scale = DH ** -0.5
    with ExitStack() as ctx:
        def sb(name, shape, dt=F32):
            return ctx.enter_context(nc.sbuf_tensor(name, shape, dt))

        def sem(name):
            return ctx.enter_context(nc.semaphore(name))

        raw = sb("sa_raw", [P, DC, 3 * D])
        raw_out = sb("sa_raw_out", [P, DC, D])
        w_qkv = [sb(f"sa_w_qkv_{p}", [P, DC, 3 * D], HALF) for p in ("hi", "lo")]
        w_out = [sb(f"sa_w_out_{p}", [P, DC, D], HALF) for p in ("hi", "lo")]
        stats, mean_var, rstd = sb("sa_stats", [P, B, 6]), sb("sa_mean_var", [P, B, 2]), sb("sa_rstd", [P, B, 2])
        x_norm = sb("sa_x_norm", [P, 2, D])
        xT = [sb(f"sa_xT_{p}", [P, DC, 2, P], HALF) for p in ("hi", "lo")]
        x_keys = [sb(f"sa_x_keys_{p}", [P, DC, 2, SEL], HALF) for p in ("hi", "lo")]
        qT = sb("sa_qT", [P, G, 2 * P])
        kT = sb("sa_kT", [P, G, 2 * SEL])
        v = sb("sa_v", [P, D])
        row_max = sb("sa_row_max", [P, HG, 2 * G])
        probs = sb("sa_probs", [P, HG, 2 * G, SEL])
        row_sum, inv_sum = sb("sa_row_sum", [P, HG, 2 * G]), sb("sa_inv_sum", [P, HG, G, 2])
        pT = sb("sa_pT", [P, HG, G, P])
        start = sb("sa_start", [P, 1])
        o_tokens = sb("sa_o_tokens", [P, 2, D])
        oT = [sb(f"sa_oT_{p}", [P, 2, DC, P], HALF) for p in ("hi", "lo")]
        bank = [ctx.enter_context(nc.psum_tensor(f"sa_bank{i}", [P, 512], F32)) for i in range(8)]

        w_in, w_out_in, passed = [sem(f"sa_w_in{i}") for i in range(3)], sem("sa_w_out_in"), sem("sa_passed")
        w_hi, w_lo, chain, var_ready, std_ready = (sem(f"sa_{n}") for n in ("w_hi", "w_lo", "chain", "var_ready", "std_ready"))
        made = Steps(sem("sa_made"), "xT0 xT1 q0 q1 k v s0 s1 s2 s3 p0 p1 p2 p3 o0 o1 oT0 oT1 y0 y1")
        by_act = Steps(sem("sa_by_act"), "xT0 xT1 q0 v exp0 exp1 exp2 exp3 pT0 pT2 oT0 oT1")
        by_dve = Steps(sem("sa_by_dve"), "norm xT0 xT1 q1 k max0 max1 sub0 max2 sub1 max3 sub2 sub3 sum0 sum1 sum2 sum3 inv pT1 pT3 o0 o1 "
                                         "oT0 oT1 y0 y1")
        by_pool = Steps(sem("sa_by_pool"), "keys")

        block = ctx.enter_context(nc.Block())

        @block.sync
        def _(sp):
            for i in range(3):
                sp.dma_start(raw[:, :, i * D:(i + 1) * D], w_qkv_dram.rearrange("(p c) n -> p c n", c=DC)[:, :, i * D:(i + 1) * D]).then_inc(w_in[i], 16)
            sp.dma_start(raw_out[:], w_out_dram.rearrange("(c p) n -> p c n", p=P)).then_inc(w_out_in, 16)

        @block.gpsimd
        def _(pool):
            by_pool.start(nc.gpsimd.memset(pT[:, 0, 0, 0:1], 0.0))
            with pool.Fori(0, B // 2) as j:
                by_dve.done(pool, "xT1", j)
                pool.sem_inc(passed, 1)
                for part in range(2):
                    for src, to in every_second_key(xT[part][:].rearrange("p c l k -> p (c l) k")):
                        dst = x_keys[part][:].rearrange("p c l k -> p (c l) k")[:, :, to]
                        ins = nc.gpsimd.tensor_copy(dst.rearrange("p n (r t) -> p n r t", t=6) if to.stop <= 60 else dst, src)
                ins.then_inc(by_pool.sem, 1)

        @block.tensor
        def _(pe):
            made.start(nc.tensor.matmul(bank[0][0:1, 0:1], identity[:, 0:1], identity[:, 0:1], start=True, stop=True))
            with pe.Fori(0, B // 2) as j:
                for l in range(2):
                    by_dve.done(pe, f"oT{l}", j, before=True)
                    if l == 0:
                        by_dve.done(pe, "norm", j)
                    for c in range(DC):
                        ins = nc.tensor.transpose(bank[l][:, c * P:(c + 1) * P], x_norm[:, l, c::DC], identity[:])
                    ins.then_inc(made.sem, 1)
                pe.wait_ge(w_lo, 1)
                by_dve.done(pe, "xT1", j)
                right = [[x[:, c, :, :].rearrange("p l k -> p (l k)") for c in range(DC)] for x in xT]
                for half in range(2):
                    by_dve.done(pe, f"y{half}", j, before=True)
                    for gl in range(2):
                        g = 2 * half + gl
                        left = [[w[:, c, g * P:(g + 1) * P] for c in range(DC)] for w in w_qkv]
                        ins = split_product(nc, bank[2 + half][:, gl * 2 * P:(gl + 1) * 2 * P], *left, *right)
                    ins.then_inc(made.sem, 1)
                pe.wait_ge(w_lo, 2)
                by_pool.done(pe, "keys", j)
                by_act.done(pe, "pT2", j, before=True)
                keys = [[x[:, c, :, :].rearrange("p l k -> p (l k)") for c in range(DC)] for x in x_keys]
                for g in range(G):
                    left = [[w[:, c, D + g * P:D + (g + 1) * P] for c in range(DC)] for w in w_qkv]
                    ins = split_product(nc, bank[4][:, g * P:(g + 1) * P], *left, *keys)
                ins.then_inc(made.sem, 1)
                pe.wait_ge(w_lo, 3)
                by_dve.done(pe, "pT3", j, before=True)
                right = [[w[:, c, 2 * D:3 * D] for c in range(DC)] for w in w_qkv]
                split_product(nc, bank[5][:], *keys, *right).then_inc(made.sem, 1)
                by_act.done(pe, "q0", j)
                by_dve.done(pe, "k", j)
                for i in range(HG):
                    by_dve.done(pe, ("o0", "o1", "xT0", "xT1")[i], j, before=i < 2)
                    rows = slice(i * DH, (i + 1) * DH)
                    for g in range(G):
                        for l in range(2):
                            n = 2 * g + l
                            ins = nc.tensor.matmul(bank[(6 + i) % 8][:, n * SEL:(n + 1) * SEL], qT[rows, g, l * P:(l + 1) * P],
                                                   kT[rows, g, l * SEL:(l + 1) * SEL], start=True, stop=True)
                    ins.then_inc(made.sem, 1)
                for i in range(HG):
                    by_act.done(pe, f"exp{i}", j)
                    (by_act if i in (0, 3) else by_dve).done(pe, ("q0", "q1", "k", "v")[i], j)
                    for g in range(G):
                        ins = nc.tensor.transpose(bank[2 + i][:, g * P:(g + 1) * P], probs[:, i, 2 * g:2 * g + 2, :].rearrange("p n k -> p (n k)"), identity[:])
                    ins.then_inc(made.sem, 1)
                by_act.done(pe, "pT2", j)
                by_dve.done(pe, "pT3", j)
                for l in range(2):
                    by_dve.done(pe, f"sub{l}", j)
                    rows = slice(l * SEL, (l + 1) * SEL)
                    for g in range(G):
                        for i in range(HG):
                            cols = slice((HG * g + i) * DH, (HG * g + i + 1) * DH)
                            ins = nc.tensor.matmul(bank[6 + l][:, cols], pT[rows, i, g, :], v[rows, cols], start=True, stop=True)
                    ins.then_inc(made.sem, 1)
                for l in range(2):
                    by_dve.done(pe, f"o{l}", j)
                    for c in range(DC):
                        ins = nc.tensor.transpose(bank[l][:, c * P:(c + 1) * P], o_tokens[:, l, c * P:(c + 1) * P], identity[:])
                    ins.then_inc(made.sem, 1)
                for l in range(2):
                    by_dve.done(pe, f"oT{l}", j)
                    left = [[x[:, l, c, :] for c in range(DC)] for x in oT]
                    pe.wait_ge(w_lo, 4)
                    right = [[w[:, c, :] for c in range(DC)] for w in w_out]
                    split_product(nc, bank[2 + l][:], *left, *right).then_inc(made.sem, 1)

        @block.scalar
        def _(act):
            norm_stats_scalar(nc, act, rstd, var_ready, std_ready)
            for i in range(3):
                act.wait_ge(w_in[i], 16)
                nc.scalar.copy(w_qkv[0][:, :, i * D:(i + 1) * D], raw[:, :, i * D:(i + 1) * D]).then_inc(w_hi, 1)
            act.wait_ge(w_out_in, 16)
            nc.scalar.copy(w_out[0][:], raw_out[:]).then_inc(w_hi, 1)
            by_act.start(nc.scalar.copy(start[:, 0:1], identity[:, 0:1]))
            with act.Fori(0, B // 2) as j:
                for l in range(2):
                    made.done(act, f"xT{l}", j)
                    nc.scalar.copy(xT[0][:, :, l, :], bank[l][:].rearrange("p (c k) -> p c k", k=P)).then_inc(by_act.sem, 1)
                made.done(act, "q0", j)
                nc.scalar.copy(qT[:, 0:2, :].rearrange("p g k -> p (g k)"), bank[2][:]).then_inc(by_act.sem, 1)
                made.done(act, "v", j)
                nc.scalar.copy(v[:], bank[5][:]).then_inc(by_act.sem, 1)
                for i in range(HG):
                    by_dve.done(act, f"sub{i}", j)
                    p = probs[:, i, :, :].rearrange("p n k -> p (n k)")
                    nc.scalar.activation(p, p, ACT.Exp, scale=scale).then_inc(by_act.sem, 1)
                for i in (0, 2):
                    made.done(act, f"p{i}", j)
                    nc.scalar.copy(pT[:, i, :, :].rearrange("p g q -> p (g q)"), bank[2 + i][:]).then_inc(by_act.sem, 1)
                for l in range(2):
                    made.done(act, f"oT{l}", j)
                    nc.scalar.copy(oT[0][:, l, :, :].rearrange("p c k -> p (c k)"), bank[l][:]).then_inc(by_act.sem, 1)

        @block.vector
        def _(dve):
            norm_stats_vector(nc, dve, x_tokens, stats, mean_var, rstd, chain, var_ready, std_ready)
            by_dve.start(nc.vector.memset(row_max[:], 0.0))
            for i in range(3):
                dve.wait_ge(w_hi, i + 1)
                third = slice(i * D, (i + 1) * D)
                nc.vector.tensor_tensor(w_qkv[1][:, :, third], raw[:, :, third], w_qkv[0][:, :, third], ALU.subtract).then_inc(w_lo, 1)
            dve.wait_ge(w_hi, 4)
            nc.vector.tensor_tensor(w_out[1][:], raw_out[:], w_out[0][:], ALU.subtract).then_inc(w_lo, 1)
            with dve.Fori(0, B // 2) as j:
                made.done(dve, "y1", j, before=True)
                for l in range(2):
                    b = bass.ds(2 * j + l, 1)
                    ins = nc.vector.tensor_scalar(x_norm[:, l:l + 1, :], x_tokens[:, b, :], mean_var[:, b, 0], rstd[:, b, 1], ALU.subtract, ALU.mult)
                ins.then_inc(by_dve.sem, 1)
                for l in range(2):
                    by_act.done(dve, f"xT{l}", j)
                    nc.vector.tensor_tensor(xT[1][:, :, l, :], bank[l][:].rearrange("p (c k) -> p c k", k=P), xT[0][:, :, l, :],
                                            ALU.subtract).then_inc(by_dve.sem, 1)
                made.done(dve, "q1", j)
                nc.vector.tensor_copy(qT[:, 2:4, :].rearrange("p g k -> p (g k)"), bank[3][:]).then_inc(by_dve.sem, 1)
                made.done(dve, "k", j)
                nc.vector.tensor_copy(kT[:].rearrange("p g k -> p (g k)"), bank[4][:]).then_inc(by_dve.sem, 1)

                def logits(i):
                    return bank[(6 + i) % 8][:].rearrange("p (n k) -> p n k", k=SEL)

                def largest(i):
                    made.done(dve, f"s{i}", j)
                    nc.vector.tensor_reduce(row_max[:, i, :], logits(i), AX.X, ALU.max).then_inc(by_dve.sem, 1)

                def subtract(i):
                    by_dve.done(dve, f"max{i}", j)
                    nc.vector.tensor_tensor(probs[:, i, :, :], logits(i), row_max[:, i, :].unsqueeze(2).to_broadcast([P, 2 * G, SEL]),
                                            ALU.subtract).then_inc(by_dve.sem, 1)

                largest(0)
                for i in range(1, HG):
                    largest(i)
                    subtract(i - 1)
                subtract(HG - 1)
                for i in range(HG):
                    by_act.done(dve, f"exp{i}", j)
                    nc.vector.tensor_reduce(row_sum[:, i, :], probs[:, i, :, :], AX.X, ALU.add).then_inc(by_dve.sem, 1)
                by_dve.done(dve, f"sum{HG - 1}", j)
                nc.vector.reciprocal(inv_sum[:].rearrange("p i g l -> p (i g l)"), row_sum[:].rearrange("p i n -> p (i n)")).then_inc(by_dve.sem, 1)
                for i in (1, 3):
                    made.done(dve, f"p{i}", j)
                    nc.vector.tensor_copy(pT[:, i, :, :].rearrange("p g q -> p (g q)"), bank[2 + i][:]).then_inc(by_dve.sem, 1)
                for l in range(2):
                    made.done(dve, f"o{l}", j)
                    by_dve.done(dve, "inv", j)
                    nc.vector.tensor_tensor(o_tokens[:, l, :].rearrange("p (g i d) -> p g i d", g=G, i=HG),
                                            bank[6 + l][:].rearrange("p (g i d) -> p g i d", g=G, i=HG),
                                            inv_sum[:, :, :, l].rearrange("p i g -> p g i").unsqueeze(3).to_broadcast([P, G, HG, DH]),
                                            ALU.mult).then_inc(by_dve.sem, 1)
                for l in range(2):
                    by_act.done(dve, f"oT{l}", j)
                    nc.vector.tensor_tensor(oT[1][:, l, :, :].rearrange("p c k -> p (c k)"), bank[l][:],
                                            oT[0][:, l, :, :].rearrange("p c k -> p (c k)"), ALU.subtract).then_inc(by_dve.sem, 1)
                for l in range(2):
                    made.done(dve, f"y{l}", j)
                    b = bass.ds(2 * j + l, 1)
                    nc.vector.tensor_tensor(x_tokens[:, b, :], bank[2 + l][:].unsqueeze(1), x_tokens[:, b, :], ALU.add).then_inc(by_dve.sem, 1)




E = 8
PH = 64
ROT = 32
F = 2048
T = B


def keep_two(nc, link, g, sigmoid, first, rank, left, best, weight):
    def spread(row):
        return row.unsqueeze(2).to_broadcast(list(rank.shape))

    def largest(x):
        link.now(nc.vector.tensor_reduce(best, x, AX.X, ALU.max))
        link.now(nc.vector.tensor_tensor(rank, x, spread(best), ALU.is_equal))
        link.now(nc.vector.tensor_tensor(rank, rank, weight, ALU.mult))
        link.now(nc.vector.tensor_reduce(best, rank, AX.X, ALU.max))

    link.now(nc.vector.tensor_scalar(sigmoid, g, 1.0, None, ALU.mult))
    largest(sigmoid)
    link.now(nc.vector.tensor_tensor(first, rank, spread(best), ALU.is_equal))
    link.now(nc.vector.scalar_tensor_tensor(left, first, -4.0, sigmoid, ALU.mult, ALU.add))
    largest(left)
    link.now(nc.vector.tensor_tensor(rank, rank, spread(best), ALU.is_equal))
    link.now(nc.vector.tensor_tensor(first, first, rank, ALU.add))
    link.now(nc.vector.tensor_tensor(g, sigmoid, first, ALU.mult))


KEEP_TWO = 14


def gate_stage(nc, x_tokens, x_norm, xT, gates, identity, wsel_v, wsel_o):
    with ExitStack() as ctx:
        def sb(name, shape, dt=F32):
            return ctx.enter_context(nc.sbuf_tensor(name, shape, dt))

        def sem(name):
            return ctx.enter_context(nc.semaphore(f"ga_{name}"))

        stats, mean_var, rstd = sb("ga_stats", [P, B, 6]), sb("ga_mean_var", [P, B, 2]), sb("ga_rstd", [P, B, 2])
        wsel = sb("ga_wsel", [P, 2, D])
        wselT = sb("ga_wselT", [P, DC, 2 * P])
        one_more = sb("ga_one_more", [P, 2, H, E])
        xT_full = [sb(f"ga_xT_full{i}", [P, DC, P]) for i in range(2)]
        bank = [ctx.enter_context(nc.psum_tensor(f"ga_bank{i}", [P, 512], F32)) for i in range(8)]
        w_in, chain, var_ready, std_ready = (sem(n) for n in ("w_in", "chain", "var_ready", "std_ready"))
        norm_ready, wsel_turned, wsel_ready, turned, full, hi, lo, summed, taken = (
            sem(n) for n in ("norm_ready", "wsel_turned", "wsel_ready", "turned", "full", "hi", "lo", "summed", "taken"))
        block = ctx.enter_context(nc.Block())

        @block.sync
        def _(sp):
            for i, w in enumerate((wsel_v, wsel_o)):
                sp.dma_start(wsel[:, i, :], w.rearrange("h e d -> (h e) d")).then_inc(w_in, 16)

        @block.tensor
        def _(pe):
            pe.wait_ge(w_in, 32)
            for i in range(2):
                for c in range(DC):
                    ins = nc.tensor.transpose(bank[6 + i][:, c * P:(c + 1) * P], wsel[:, i, c::DC], identity[:])
                ins.then_inc(wsel_turned, 1)

            def turn(t):
                pe.wait_ge(norm_ready, t + 1)
                if t >= 4:
                    pe.wait_ge(lo, t - 3)
                for c in range(DC):
                    ins = nc.tensor.transpose(bank[t % 4][:, c * P:(c + 1) * P], x_norm[:, t, c::DC], identity[:])
                ins.then_inc(turned, 1)

            turn(0)
            for t in range(T):
                if t + 1 < T:
                    turn(t + 1)
                if t == 0:
                    pe.wait_ge(wsel_ready, 2)
                pe.wait_ge(full, t + 1)
                if t >= 2:
                    pe.wait_ge(taken, t - 1)
                for c in range(DC):
                    ins = nc.tensor.matmul(bank[4 + t % 2][:, 0:2 * P], xT_full[t % 2][:, c, :], wselT[:, c, :], start=(c == 0), stop=(c == DC - 1))
                ins.then_inc(summed, 1)

        @block.scalar
        def _(act):
            norm_stats_scalar(nc, act, rstd, var_ready, std_ready)

            def take(t):
                act.wait_ge(summed, t + 1)
                nc.scalar.activation(gates[:, :, t, :, :], bank[4 + t % 2][:, 0:2 * P].rearrange("p (s h e) -> p s h e", s=2, e=E), ACT.Exp, scale=-1.0).then_inc(taken, 1)

            for t in range(T):
                act.wait_ge(turned, t + 1)
                if t >= 2:
                    act.wait_ge(summed, t - 1)
                nc.scalar.copy(xT_full[t % 2][:].rearrange("p c k -> p (c k)"), bank[t % 4][:]).then_inc(full, 1)
                nc.scalar.copy(xT[0][:, :, t * P:(t + 1) * P], bank[t % 4][:].rearrange("p (c k) -> p c k", k=P)).then_inc(hi, 1)
                if t >= 1:
                    take(t - 1)
            take(T - 1)

        @block.vector
        def _(dve):
            link = norm_stats_vector(nc, dve, x_tokens, stats, mean_var, rstd, chain, var_ready, std_ready)
            for t in range(T):
                nc.vector.tensor_scalar(x_norm[:, t, :], x_tokens[:, t, :], mean_var[:, t, 0:1], rstd[:, t, 1:2], ALU.subtract, ALU.mult).then_inc(norm_ready, 1)
            for i in range(2):
                dve.wait_ge(wsel_turned, i + 1)
                nc.vector.tensor_copy(wselT[:, :, i * P:(i + 1) * P], bank[6 + i][:].rearrange("p (c k) -> p c k", k=P)).then_inc(wsel_ready, 1)

            def sigmoid(t):
                dve.wait_ge(taken, t + 1)
                link.now(nc.vector.tensor_scalar(one_more[:], gates[:, :, t, :, :], 1.0, None, ALU.add))
                link.now(nc.vector.reciprocal(gates[:, :, t, :, :], one_more[:]))

            for t in range(T):
                dve.wait_ge(hi, t + 1)
                tile = slice(t * P, (t + 1) * P)
                nc.vector.tensor_tensor(xT[1][:, :, tile], bank[t % 4][:].rearrange("p (c k) -> p c k", k=P), xT[0][:, :, tile], ALU.subtract).then_inc(lo, 1)
                if t >= 1:
                    sigmoid(t - 1)
            sigmoid(T - 1)


def expert_values(nc, xT, gates, v, wv_dram):
    with ExitStack() as ctx:
        def sb(name, shape, dt=F32):
            return ctx.enter_context(nc.sbuf_tensor(name, shape, dt))

        def sem(name):
            return ctx.enter_context(nc.semaphore(f"ev_{name}"))

        raw = [sb(f"ev_raw{i}", [P, E, DC, PH]) for i in range(2)]
        w = [[sb(f"ev_w{i}_{p}", [P, E, DC, PH], HALF) for p in ("hi", "lo")] for i in range(2)]
        gated = [sb(f"ev_gated{i}", [P, E, PH]) for i in range(4)]
        first, rank, left, sigmoid = (sb(f"ev_{n}", [P, T * H, E]) for n in ("first", "rank", "left", "sigmoid"))
        best, order = sb("ev_best", [P, T * H]), sb("ev_order", [P, E])
        bank = [ctx.enter_context(nc.psum_tensor(f"ev_bank{i}", [P, 512], F32)) for i in range(8)]
        raw_in = [sem(f"raw_in{i}") for i in range(2)]
        passed, w_hi, w_ready, made, gated_ready, reduced = (sem(n) for n in ("passed", "w_hi", "w_ready", "made", "gated", "reduced"))
        order_ready, chain = sem("order"), sem("chain")
        by = wv_dram.rearrange("h e (q c) p -> h q e (c p)", c=DC)
        block = ctx.enter_context(nc.Block())

        @block.sync
        def _(sp):
            for i in range(2):
                sp.dma_start(raw[i][:].rearrange("q e c p -> q e (c p)"), by[i]).then_inc(raw_in[i], 16)
            with sp.Fori(1, H // 2) as j:
                for i in range(2):
                    sp.wait_ge(w_ready, 2 * j + i - 1)
                    sp.dma_start(raw[i][:].rearrange("q e c p -> q e (c p)"), by[bass.ds(2 * j + i, 1)].rearrange("h q e n -> (h q) e n")).then_inc(raw_in[i], 16)

        @block.gpsimd
        def _(pool):
            for e in range(E):
                nc.gpsimd.memset(order[:, e:e + 1], float(E - e)).then_inc(order_ready, 1)
            pool.wait_ge(w_ready, 2)
            with pool.Fori(1, H // 2) as j:
                for i in range(2):
                    pool.wait_ge(raw_in[i], 16 * j + 16)
                    pool.wait_ge(made, T * (2 * j + i) + T)
                    pool.sem_inc(passed, 1)
                    nc.gpsimd.tensor_copy(w[i][0][:], raw[i][:]).then_inc(w_hi, 1)
                    pool.wait_ge(w_hi, 2 * j + i + 1)
                    nc.gpsimd.tensor_tensor(w[i][1][:], raw[i][:], w[i][0][:], ALU.subtract).then_inc(w_ready, 1)

        @block.tensor
        def _(pe):
            with pe.Fori(0, H // 2) as j:
                for i in range(2):
                    pe.wait_ge(w_ready, 2 * j + i + 1)
                    right = [[x[:, :, c, :] for c in range(DC)] for x in w[i]]
                    for t in range(T):
                        pe.wait_ge(gated_ready, T * (2 * j + i) + t + 1)
                        left = [[x[:, c, t * P:(t + 1) * P] for c in range(DC)] for x in xT]
                        split_product(nc, bank[t][:], *left, *right).then_inc(made, 1)

        @block.scalar
        def _(act):
            for i in range(2):
                act.wait_ge(raw_in[i], 16)
                nc.scalar.copy(w[i][0][:], raw[i][:]).then_inc(w_hi, 1)

        @block.vector
        def _(dve):
            nc.vector.memset(gated[0][:], 0.0).then_inc(gated_ready, T)
            nc.vector.memset(gated[1][:], 0.0).then_inc(made, 2 * T)
            nc.vector.memset(gated[2][:], 0.0).then_inc(reduced, 4)
            for i in range(2):
                dve.wait_ge(w_hi, i + 1)
                nc.vector.tensor_tensor(w[i][1][:], raw[i][:], w[i][0][:], ALU.subtract).then_inc(w_ready, 1)
            dve.wait_ge(order_ready, E)
            keep_two(nc, Link(dve, chain), gates[:, 0].rearrange("p t h e -> p (t h) e"), sigmoid[:], first[:], rank[:], left[:], best[:],
                     order[:].unsqueeze(1).to_broadcast([P, T * H, E]))
            with dve.Fori(0, H // 2) as j:
                keep_two(nc, Link(dve, chain, base=KEEP_TWO * (j + 1)), gates[:, 1, bass.ds(j, 1), :, :].rearrange("p a h e -> p (a h) e"),
                         *(x[:, 0:H, :] for x in (sigmoid, first, rank, left)), best[:, 0:H], order[:].unsqueeze(1).to_broadcast([P, H, E]))
                for i in range(2):
                    head = bass.ds(2 * j + i, 1)

                    def total(t):
                        dve.wait_ge(gated_ready, T * (2 * j + i) + T + t + 1)
                        nc.vector.tensor_reduce(v[:, t, head, :], gated[t % 4][:].rearrange("p e q -> p q e").unsqueeze(1),
                                                AX.X, ALU.add).then_inc(reduced, 1)

                    for t in range(T):
                        n = T * (2 * j + i) + t
                        dve.wait_ge(made, 2 * T + n + 1)
                        dve.wait_ge(reduced, n + 1)
                        gate = gates[:, 0, t, head, :].unsqueeze(3).to_broadcast([P, 1, E, PH])
                        nc.vector.tensor_tensor(gated[t % 4][:].unsqueeze(1), bank[t][:].rearrange("p (a e q) -> p a e q", a=1, e=E), gate, ALU.mult)\
                            .then_inc(gated_ready, 1)
                        if t >= 1:
                            total(t - 1)
                    total(T - 1)




def rotary_attention(nc, xT, v, identity, wq_dram, wk_dram, cos_dram, sin_dram):
    HALF_ROT = ROT // 2
    with ExitStack() as ctx:
        def sb(name, shape, dt=F32):
            return ctx.enter_context(nc.sbuf_tensor(name, shape, dt))

        def sem(name):
            return ctx.enter_context(nc.semaphore(f"ra_{name}"))

        w = [sb(f"ra_w_{p}", [P, 2 * H, DC, PH], HALF) for p in ("hi", "lo")]
        cos, sin = sb("ra_cos", [P, HALF_ROT]), sb("ra_sin", [P, HALF_ROT])
        qk = sb("ra_qk", [P, 2 * H, PH])
        by_cos, by_sin = (sb(f"ra_by_{n}", [P, 2 * H, 2, HALF_ROT]) for n in ("cos", "sin"))
        qkT = sb("ra_qkT", [P, H, P])
        row_max, row_sum, inv_sum = (sb(f"ra_{n}", [P, H]) for n in ("row_max", "row_sum", "inv_sum"))
        probs = sb("ra_probs", [P, H, P])
        pT = sb("ra_pT", [P, H, P])
        raw = [sb(f"ra_raw{i}", [P, H // 2, DC, PH]) for i in range(2)]
        bank = [ctx.enter_context(nc.psum_tensor(f"ra_bank{i}", [P, 512], F32)) for i in range(8)]
        raw_in = [sem(f"raw_in{i}") for i in range(2)]
        table_in, w_hi, w_lo = sem("table_in"), sem("w_hi"), sem("w_lo")
        qk_made, qk_taken, rotating, rotated = sem("qk_made"), sem("qk_taken"), sem("rotating"), sem("rotated")
        made = Steps(sem("made"), "qkT0 qkT1 qkT2 qkT3 s0 s1 s2 s3 pT0 pT1 pT2 pT3 o0 o1")
        by_act = Steps(sem("by_act"), "qkT0 qkT2 exp0 exp1 exp2 exp3 pT0 pT2")
        by_dve = Steps(sem("by_dve"), "qkT1 qkT3 max0 max1 sub0 max2 sub1 max3 sub2 sub3 sum0 sum1 sum2 sum3 inv pT1 pT3 o0 o1")

        def at(b):
            return bass.ds(b, 1)

        block = ctx.enter_context(nc.Block())

        @block.sync
        def _(sp):
            sp.dma_start(cos[:], cos_dram).then_inc(table_in, 16)
            sp.dma_start(sin[:], sin_dram).then_inc(table_in, 16)
            for n in range(4):
                if n >= 2:
                    sp.wait_ge(w_lo, n - 1)
                src = (wq_dram, wk_dram)[n // 2][8 * (n % 2):8 * (n % 2) + 8].rearrange("h (q c) p -> q h (c p)", c=DC)
                sp.dma_start(raw[n % 2][:].rearrange("q h c p -> q h (c p)"), src).then_inc(raw_in[n % 2], 16)

        @block.tensor
        def _(pe):
            made.start(nc.tensor.matmul(bank[7][0:1, 0:1], identity[:, 0:1], identity[:, 0:1], start=True, stop=True))

            def project(b):
                for n in range(4):
                    if isinstance(b, int):
                        pe.wait_ge(w_lo, n + 1)
                    else:
                        by_dve.done(pe, f"sub{n}", b - 1)
                    for c in range(DC):
                        left = [[x[:, c, b * P:(b + 1) * P] if isinstance(b, int) else x[:, c, bass.ds(b * P, P)]] for x in xT]
                        right = [[x[:, 8 * n:8 * n + 8, c, :]] for x in w]
                        ins = split_product(nc, bank[n][:], *left, *right, first=(c == 0), last=(c == DC - 1))
                    ins.then_inc(qk_made, 1)

            def body(b, last=False):
                pe.wait_ge(rotated, 2 * b + 2)
                for m in range(4):
                    if m < 2:
                        by_dve.done(pe, f"o{m}", b, before=True)
                    else:
                        (by_act if m == 2 else by_dve).done(pe, f"pT{m}", b, before=True)
                    for k in range(4):
                        pair = 4 * m + k
                        ins = nc.tensor.transpose(bank[4 + m][:, k * P:(k + 1) * P], qk[:, 2 * pair:2 * pair + 2, :].rearrange("p h d -> p (h d)"), identity[:])
                    ins.then_inc(made.sem, 1)
                by_act.done(pe, "qkT2", b)
                by_dve.done(pe, "qkT3", b)
                for m in range(4):
                    rows = slice(PH * (m // 2), PH * (m // 2) + PH)
                    for k in range(4):
                        pair = 4 * (m % 2) + k
                        ins = nc.tensor.matmul(bank[m][:, k * P:(k + 1) * P], qkT[rows, pair, :], qkT[rows, H // 2 + pair, :], start=True, stop=True)
                    ins.then_inc(made.sem, 1)
                if not last:
                    project(b + 1)
                for m in range(4):
                    by_act.done(pe, f"exp{m}", b)
                    for k in range(4):
                        ins = nc.tensor.transpose(bank[4 + m][:, k * P:(k + 1) * P], probs[:, 4 * m + k, :], identity[:])
                    ins.then_inc(made.sem, 1)
                by_act.done(pe, "pT2", b)
                by_dve.done(pe, "pT3", b)
                for m in range(2):
                    for k in range(8):
                        h = 8 * m + k
                        right = v[:, b, h, :] if last else v[:, at(b), h, :].rearrange("p a d -> p (a d)")
                        ins = nc.tensor.matmul(bank[4 + m][:, k * PH:(k + 1) * PH], pT[:, h // 2 + 8 * (h % 2), :], right, start=True, stop=True)
                    ins.then_inc(made.sem, 1)

            project(0)
            with pe.Fori(0, B - 1) as b:
                body(b)
            body(B - 1, last=True)

        @block.scalar
        def _(act):
            for n in range(4):
                act.wait_ge(raw_in[n % 2], 16 * (n // 2) + 16)
                nc.scalar.copy(w[0][:, 8 * n:8 * n + 8, :, :], raw[n % 2][:]).then_inc(w_hi, 1)
            act.wait_ge(table_in, 32)
            by_act.start(nc.scalar.copy(inv_sum[:, 0:1], cos[:, 0:1]))

            def take(b):
                for n in range(4):
                    act.wait_ge(qk_made, 4 * b + n + 1)
                    nc.scalar.copy(qk[:, 8 * n:8 * n + 8, :].rearrange("p h d -> p (h d)"), bank[n][:]).then_inc(qk_taken, 1)

            def body(b, last=False):
                for m in (0, 2):
                    made.done(act, f"qkT{m}", b)
                    nc.scalar.copy(qkT[:, 4 * m:4 * m + 4, :].rearrange("p h d -> p (h d)"), bank[4 + m][:]).then_inc(by_act.sem, 1)
                for m in range(4):
                    by_dve.done(act, f"sub{m}", b)
                    p = probs[:, 4 * m:4 * m + 4, :]
                    nc.scalar.activation(p, p, ACT.Exp, scale=PH ** -0.5).then_inc(by_act.sem, 1)
                if not last:
                    take(b + 1)
                for m in (0, 2):
                    made.done(act, f"pT{m}", b)
                    nc.scalar.copy(pT[:, 4 * m:4 * m + 4, :].rearrange("p h q -> p (h q)"), bank[4 + m][:]).then_inc(by_act.sem, 1)

            take(0)
            with act.Fori(0, B - 1) as b:
                body(b)
            body(B - 1, last=True)

        @block.vector
        def _(dve):
            by_dve.start(nc.vector.memset(row_max[:], 0.0))
            for n in range(4):
                dve.wait_ge(w_hi, n + 1)
                nc.vector.tensor_tensor(w[1][:, 8 * n:8 * n + 8, :, :], raw[n % 2][:], w[0][:, 8 * n:8 * n + 8, :, :], ALU.subtract).then_inc(w_lo, 1)
            dve.wait_ge(table_in, 32)

            def rotate(b):
                dve.wait_ge(qk_taken, 4 * b + 4)
                x = qk[:, :, 0:ROT]
                for table, to in ((cos, by_cos), (sin, by_sin)):
                    ins = nc.vector.tensor_tensor(to[:], x.rearrange("p h (a k) -> p h a k", a=2),
                                                  table[:].unsqueeze(1).unsqueeze(1).to_broadcast([P, 2 * H, 2, HALF_ROT]), ALU.mult)
                    ins.then_inc(rotating, 1)
                dve.wait_ge(rotating, 2 * b + 2)
                nc.vector.tensor_tensor(x[:, :, 0:HALF_ROT], by_cos[:, :, 0, :], by_sin[:, :, 1, :], ALU.subtract).then_inc(rotated, 1)
                nc.vector.tensor_tensor(x[:, :, HALF_ROT:ROT], by_cos[:, :, 1, :], by_sin[:, :, 0, :], ALU.add).then_inc(rotated, 1)

            def body(b, last=False):
                for m in (1, 3):
                    made.done(dve, f"qkT{m}", b)
                    nc.vector.tensor_copy(qkT[:, 4 * m:4 * m + 4, :].rearrange("p h d -> p (h d)"), bank[4 + m][:]).then_inc(by_dve.sem, 1)

                def logits(m):
                    return bank[m][:].rearrange("p (h k) -> p h k", k=P)

                def heads(m):
                    return slice(4 * m, 4 * m + 4)

                def largest(m):
                    made.done(dve, f"s{m}", b)
                    nc.vector.tensor_reduce(row_max[:, heads(m)], logits(m), AX.X, ALU.max).then_inc(by_dve.sem, 1)

                def subtract(m):
                    by_dve.done(dve, f"max{m}", b)
                    nc.vector.tensor_tensor(probs[:, heads(m), :], logits(m), row_max[:, heads(m)].unsqueeze(2).to_broadcast([P, 4, P]),
                                            ALU.subtract).then_inc(by_dve.sem, 1)

                largest(0)
                for m in range(1, 4):
                    largest(m)
                    subtract(m - 1)
                subtract(3)
                for m in range(4):
                    by_act.done(dve, f"exp{m}", b)
                    nc.vector.tensor_reduce(row_sum[:, heads(m)], probs[:, heads(m), :], AX.X, ALU.add).then_inc(by_dve.sem, 1)
                by_dve.done(dve, "sum3", b)
                nc.vector.reciprocal(inv_sum[:].rearrange("p (u i) -> p u i", i=2), row_sum[:].rearrange("p (i u) -> p u i", i=2)).then_inc(by_dve.sem, 1)
                for m in (1, 3):
                    made.done(dve, f"pT{m}", b)
                    nc.vector.tensor_copy(pT[:, heads(m), :].rearrange("p h q -> p (h q)"), bank[4 + m][:]).then_inc(by_dve.sem, 1)
                if not last:
                    rotate(b + 1)
                by_dve.done(dve, "inv", b)
                for m in range(2):
                    made.done(dve, f"o{m}", b)
                    out = v[:, b:b + 1, 8 * m:8 * m + 8, :] if last else v[:, at(b), 8 * m:8 * m + 8, :]
                    nc.vector.tensor_tensor(out.rearrange("p a h d -> p (a h) d"), bank[4 + m][:].rearrange("p (h d) -> p h d", d=PH),
                                            inv_sum[:, 8 * m:8 * m + 8].unsqueeze(2).to_broadcast([P, 8, PH]), ALU.mult).then_inc(by_dve.sem, 1)

            rotate(0)
            with dve.Fori(0, B - 1) as b:
                body(b)
            body(B - 1, last=True)


def expert_outputs(nc, x_norm, v, gates, identity, wo_dram):
    with ExitStack() as ctx:
        def sb(name, shape, dt=F32):
            return ctx.enter_context(nc.sbuf_tensor(name, shape, dt))

        def sem(name):
            return ctx.enter_context(nc.semaphore(f"eo_{name}"))

        raw = [sb(f"eo_raw{i}", [P, DC, D]) for i in range(2)]
        w = [[sb(f"eo_w{i}_{p}", [P, DC, D], HALF) for p in ("hi", "lo")] for i in range(4)]
        gated = [sb(f"eo_gated{i}", [P, E, PH]) for i in range(4)]
        start = sb("eo_start", [P, 3])
        gatedT = [[sb(f"eo_gatedT{i}_{p}", [P, DC, P], HALF) for p in ("hi", "lo")] for i in range(4)]
        psT = [ctx.enter_context(nc.psum_tensor(f"eo_psT{i}", [P, 512], F32)) for i in range(4)]
        psY = [ctx.enter_context(nc.psum_tensor(f"eo_psY{i}", [P, 512], F32)) for i in range(4)]
        raw_in = [sem(f"raw_in{i}") for i in range(2)]
        passed, w_hi, w_ready, gated_ready, turned, hi, lo, made, added = (sem(n) for n in ("passed", "w_hi", "w_ready", "gated", "turned", "hi", "lo", "made", "added"))
        NJ = 2 * T
        block = ctx.enter_context(nc.Block())

        @block.sync
        def _(sp):
            for i in range(2):
                sp.dma_start(raw[i][:], wo_dram[i].rearrange("e p n -> (e p) n").rearrange("(c q) n -> q c n", q=P)).then_inc(raw_in[i], 16)
            with sp.Fori(1, H // 2) as j:
                for i in range(2):
                    sp.wait_ge(w_ready, 2 * j + i - 1)
                    src = wo_dram[bass.ds(2 * j + i, 1)].rearrange("a e p n -> (a e p) n").rearrange("(c q) n -> q c n", q=P)
                    sp.dma_start(raw[i][:], src).then_inc(raw_in[i], 16)

        @block.gpsimd
        def _(pool):
            def split(quad, halves):
                for half in halves:
                    j = 2 * quad + half
                    for i in range(2):
                        hi_part, lo_part = w[2 * half + i]
                        pool.wait_ge(raw_in[i], 16 * j + 16)
                        pool.wait_ge(made, T * j + T)
                        pool.sem_inc(passed, 1)
                        nc.gpsimd.tensor_copy(hi_part[:], raw[i][:]).then_inc(w_hi, 1)
                        pool.wait_ge(w_hi, 2 * j + i + 1)
                        nc.gpsimd.tensor_tensor(lo_part[:], raw[i][:], hi_part[:], ALU.subtract).then_inc(w_ready, 1)

            pool.wait_ge(w_ready, 2)
            split(0, [1])
            with pool.Fori(1, H // 4) as quad:
                split(quad, [0, 1])

        @block.tensor
        def _(pe):
            def pair(j, half):
                def turn(n):
                    pe.wait_ge(gated_ready, NJ * j + n + 1)
                    pe.wait_ge(lo, NJ * j + n + 1)
                    flat = gated[n % 4][:].rearrange("p e d -> p (e d)")
                    for c in range(DC):
                        ins = nc.tensor.transpose(psT[n % 4][:, c * P:(c + 1) * P], flat[:, c * P:(c + 1) * P], identity[:])
                    ins.then_inc(turned, 1)

                turn(0)
                turn(1)
                pe.wait_ge(w_ready, 2 * j + 2)
                for t in range(T):
                    pe.wait_ge(added, T * j + t + 1)
                    for i in range(2):
                        n = 2 * t + i
                        if n + 2 < NJ:
                            turn(n + 2)
                        pe.wait_ge(lo, NJ * j + 4 + n + 1)
                        left = [[x[:, c, :] for c in range(DC)] for x in gatedT[n % 4]]
                        right = [[x[:, c, :] for c in range(DC)] for x in w[2 * half + i]]
                        ins = split_product(nc, psY[t % 4][:], *left, *right, first=(i == 0), last=(i == 1))
                    ins.then_inc(made, 1)

            with pe.Fori(0, H // 4) as quad:
                pair(2 * quad, 0)
                pair(2 * quad + 1, 1)

        @block.scalar
        def _(act):
            for i in range(2):
                act.wait_ge(raw_in[i], 16)
                nc.scalar.copy(w[i][0][:], raw[i][:]).then_inc(w_hi, 1)
            with act.Fori(0, H // 2) as j:
                for n in range(NJ):
                    act.wait_ge(turned, NJ * j + n + 1)
                    nc.scalar.copy(gatedT[n % 4][0][:].rearrange("p c k -> p (c k)"), psT[n % 4][:]).then_inc(hi, 1)

        @block.vector
        def _(dve):
            nc.vector.memset(start[:, 0:1], 0.0).then_inc(lo, 4)
            nc.vector.memset(start[:, 1:2], 0.0).then_inc(added, 4)
            nc.vector.memset(start[:, 2:3], 0.0).then_inc(made, 2 * T)
            for i in range(2):
                dve.wait_ge(w_hi, i + 1)
                nc.vector.tensor_tensor(w[i][1][:], raw[i][:], w[i][0][:], ALU.subtract).then_inc(w_ready, 1)
            with dve.Fori(0, H // 2) as j:
                def gate(n):
                    t, i = n // 2, n % 2
                    h = bass.ds(2 * j + i, 1)
                    nc.vector.tensor_tensor(gated[n % 4][:].unsqueeze(1), gates[:, 1, t, bass.ds(2 * j + i, 1), :].unsqueeze(3).to_broadcast([P, 1, E, PH]),
                                            v[:, t, h, :].unsqueeze(2).to_broadcast([P, 1, E, PH]), ALU.mult).then_inc(gated_ready, 1)

                def add(t):
                    dve.wait_ge(made, T * (j + 2) + t + 1)
                    nc.vector.tensor_tensor(x_norm[:, t, :], x_norm[:, t, :], psY[t % 4][:], ALU.add).then_inc(added, 1)

                dve.wait_ge(added, T * j + 4)
                for n in range(3):
                    gate(n)
                for n in range(NJ):
                    dve.wait_ge(hi, NJ * j + n + 1)
                    nc.vector.tensor_tensor(gatedT[n % 4][1][:].rearrange("p c k -> p (c k)"), psT[n % 4][:],
                                            gatedT[n % 4][0][:].rearrange("p c k -> p (c k)"), ALU.subtract).then_inc(lo, 1)
                    if n + 3 < NJ:
                        gate(n + 3)
                    if n % 2 == 1 and n >= 3:
                        add(n // 2 - 1)
                add(T - 1)


def feed_forward(nc, x_tokens, y, identity, t, out_dram):
    FT = F // P
    with ExitStack() as ctx:
        def sb(name, shape, dt=F32):
            return ctx.enter_context(nc.sbuf_tensor(name, shape, dt))

        def sem(name):
            return ctx.enter_context(nc.semaphore(f"ff_{name}"))

        stats, mean_var, rstd = sb("ff_stats", [P, B, 6]), sb("ff_mean_var", [P, B, 2]), sb("ff_rstd", [P, B, 2])
        rows = {n: sb(f"ff_{n}", [P, D]) for n in ("ln1_g", "ln1_b", "ln2_g", "ln2_b", "b2")}
        b1 = sb("ff_b1", [P, FT])
        w1 = [sb(f"ff_w1_{p}", [P, DC, F], HALF) for p in ("hi", "lo")]
        w2 = [sb(f"ff_w2_{p}", [P, FT, D], HALF) for p in ("hi", "lo")]
        yT = [sb(f"ff_yT_{p}", [P, DC, T * P], HALF) for p in ("hi", "lo")]
        hT = [sb(f"ff_hT_{p}", [P, FT, T * P], HALF) for p in ("hi", "lo")]
        raw = [sb(f"ff_raw{i}", [P, F // 2]) for i in range(2)]
        w1_raw = hT[1][:].rearrange("p f n -> p (f n)").bitcast(F32)
        shift = sb("ff_shift", [P, B])
        relu = [sb(f"ff_relu{i}", [P, 512]) for i in range(2)]
        bank = [ctx.enter_context(nc.psum_tensor(f"ff_bank{i}", [P, 512], F32)) for i in range(8)]
        raw_in = [sem(f"raw_in{i}") for i in range(2)]
        names = ("passed", "rows_in", "chain", "var_ready", "std_ready", "shift_ready", "act_normed", "w1_in", "chain2", "var2_ready", "std2_ready", "w_hi", "w_lo", "normed", "turned", "turned_hi",
                 "turned_lo", "hidden", "rectified", "hidden_hi", "hidden_lo", "made", "stored", "bank_free", "ended")
        s = {n: sem(n) for n in names}
        NW = 16
        block = ctx.enter_context(nc.Block())

        def piece(i):
            if i < 8:
                c, half = i // 2, i % 2
                cols = slice(half * (F // 2), (half + 1) * (F // 2))
                return t["W1"].rearrange("(p c) n -> p c n", c=DC)[:, c, cols], [x[:, c, cols] for x in w1]
            n = i - 8
            return t["W2"].rearrange("(f p) n -> p f n", p=P)[:, 2 * n:2 * n + 2, :], [x[:, 2 * n:2 * n + 2, :].rearrange("p f n -> p (f n)") for x in w2]

        @block.sync
        def _(sp):
            for i in range(NW):
                if i < 8:
                    sp.dma_start(w1_raw[:, i * (F // 2):(i + 1) * (F // 2)], piece(i)[0]).then_inc(s["w1_in"], 16)
                else:
                    if i >= 10:
                        sp.wait_ge(s["w_lo"], i - 1)
                    sp.dma_start(raw[i % 2][:].rearrange("p (f n) -> p f n", n=D), piece(i)[0]).then_inc(raw_in[i % 2], 16)
                if i == 1:
                    for n, row in rows.items():
                        sp.dma_start(row[:], t[n].rearrange("(a d) -> a d", a=1).broadcast_to([P, D])).then_inc(s["rows_in"], 16)
                    with nc.allow_non_contiguous_dma("a short column of biases"):
                        sp.dma_start(b1[:], t["b1"].rearrange("(f p) -> p f", p=P)).then_inc(s["rows_in"], 16)
            for b in range(B):
                sp.wait_ge(s["ended"], b + 1)
                sp.dma_start(out_dram[b], x_tokens[:, b, :]).then_inc(s["stored"], 16)
            sp.wait_ge(s["stored"], 16 * B)

        @block.gpsimd
        def _(pool):
            for i in range(NW):
                hi, lo = piece(i)[1]
                if i >= 8:
                    pool.wait_ge(raw_in[i % 2], 16 * (i // 2 - 4) + 16)
                    nc.gpsimd.tensor_copy(hi, raw[i % 2][:]).then_inc(s["w_hi"], 1)
                pool.wait_ge(s["w_hi"], i + 1)
                src = w1_raw[:, i * (F // 2):(i + 1) * (F // 2)] if i < 8 else raw[i % 2][:]
                nc.gpsimd.tensor_tensor(lo, src, hi, ALU.subtract).then_inc(s["w_lo"], 1)

        @block.tensor
        def _(pe):
            for b in range(T):
                pe.wait_ge(s["normed"], b + 1)
                if b >= 2:
                    pe.wait_ge(s["turned_lo"], b - 1)
                for c in range(DC):
                    ins = nc.tensor.transpose(bank[b % 2][:, c * P:(c + 1) * P], y[:, b, c::DC], identity[:])
                ins.then_inc(s["turned"], 1)
            pe.wait_ge(s["turned_lo"], T)
            pe.wait_ge(s["w_lo"], 8)
            with pe.Fori(0, FT) as f:
                for half in range(2):
                    pe.wait_ge(s["bank_free"], 2 * f + half + 1)
                    left = [[x[:, c, bass.ds(f * P, P)] for c in range(DC)] for x in w1]
                    right = [[x[:, c, half * 512:(half + 1) * 512] for c in range(DC)] for x in yT]
                    split_product(nc, bank[2 + half][:], *left, *right).then_inc(s["hidden"], 1)
            pe.wait_ge(s["hidden_lo"], 2 + 2 * FT)
            pe.wait_ge(s["w_lo"], NW)
            for b in range(T):
                if b >= 4:
                    pe.wait_ge(s["chain2"], 8 * (b - 4) + 1)
                left = [[x[:, f, b * P:(b + 1) * P] for f in range(FT)] for x in hT]
                right = [[x[:, f, :] for f in range(FT)] for x in w2]
                split_product(nc, bank[4 + b % 4][:], *left, *right).then_inc(s["made"], 1)

        @block.scalar
        def _(act):
            def weights(pieces):
                for i in pieces:
                    act.wait_ge(s["w1_in"], 16 * 8)
                    nc.scalar.copy(piece(i)[1][0], w1_raw[:, i * (F // 2):(i + 1) * (F // 2)]).then_inc(s["w_hi"], 1)

            norm_stats_scalar(nc, act, rstd, s["var_ready"], s["std_ready"])
            act.wait_ge(s["shift_ready"], 1)
            for b in range(B):
                nc.scalar.activation(y[:, b, :], y[:, b, :], ACT.Identity, bias=shift[:, b:b + 1], scale=rstd[:, b, 1:2]).then_inc(s["act_normed"], 1)
            for b in range(T):
                weights([b])
                act.wait_ge(s["turned"], b + 1)
                nc.scalar.copy(yT[0][:, :, b * P:(b + 1) * P], bank[b % 2][:].rearrange("p (c k) -> p c k", k=P)).then_inc(s["turned_hi"], 1)
            act.wait_ge(s["rows_in"], 96)
            with act.Fori(0, FT) as f:
                for half in range(2):
                    cols = slice(half * 512, (half + 1) * 512)
                    act.wait_ge(s["hidden"], 2 * f + half + 1)
                    act.wait_ge(s["hidden_lo"], 2 * f + half + 1)
                    act.sem_inc(s["passed"], 1)
                    nc.scalar.activation(relu[half][:], bank[2 + half][:], ACT.Relu, bias=b1[:, bass.ds(f, 1)]).then_inc(s["bank_free"], 1)
                    act.wait_ge(s["bank_free"], 2 * f + half + 3)
                    nc.scalar.copy(hT[0][:, bass.ds(f, 1), cols], relu[half][:].unsqueeze(1)).then_inc(s["hidden_hi"], 1)
            for b in range(T):
                act.wait_ge(s["var2_ready"], b + 1)
                nc.scalar.activation(rstd[:, b, 0:1], rstd[:, b, 0:1], ACT.Sqrt).then_inc(s["std2_ready"], 1)

        @block.vector
        def _(dve):
            nc.vector.memset(relu[0][:], 0.0).then_inc(s["bank_free"], 2)
            nc.vector.memset(relu[1][:], 0.0).then_inc(s["hidden_lo"], 2)
            link = norm_stats_vector(nc, dve, y, stats, mean_var, rstd, s["chain"], s["var_ready"], s["std_ready"])
            nc.vector.scalar_tensor_tensor(shift[:], mean_var[:, :, 0], -1.0, rstd[:, :, 1], ALU.mult, ALU.mult).then_inc(s["shift_ready"], 1)
            dve.wait_ge(s["rows_in"], 96)

            def lower(b):
                tile = slice(b * P, (b + 1) * P)
                dve.wait_ge(s["turned_hi"], b + 1)
                nc.vector.tensor_tensor(yT[1][:, :, tile], bank[b % 2][:].rearrange("p (c k) -> p c k", k=P), yT[0][:, :, tile], ALU.subtract).then_inc(s["turned_lo"], 1)

            for b in range(B):
                dve.wait_ge(s["act_normed"], b + 1)
                link.now(nc.vector.tensor_tensor(y[:, b, :], y[:, b, :], rows["ln1_g"][:], ALU.mult))
                nc.vector.tensor_tensor(y[:, b, :], y[:, b, :], rows["ln1_b"][:], ALU.add).then_inc(s["normed"], 1)
                if b >= 2:
                    lower(b - 2)
            lower(T - 2)
            lower(T - 1)
            with dve.Fori(0, FT) as f:
                for half in range(2):
                    cols = slice(half * 512, (half + 1) * 512)
                    dve.wait_ge(s["hidden_hi"], 2 * f + half + 1)
                    nc.vector.tensor_tensor(hT[1][:, bass.ds(f, 1), cols], relu[half][:].unsqueeze(1), hT[0][:, bass.ds(f, 1), cols], ALU.subtract)\
                        .then_inc(s["hidden_lo"], 1)
            last = Link(dve, s["chain2"])
            for b in range(T):
                tile = y[:, b, :]
                dve.wait_ge(s["made"], b + 1)
                last.now(nc.vector.tensor_tensor(tile, tile, bank[4 + b % 4][:], ALU.add))
                last.now(nc.vector.tensor_tensor(tile, tile, rows["b2"][:], ALU.add))
                last.now(nc.vector.bn_stats(stats[:, b, :], tile))
                last.now(nc.vector.bn_aggr(mean_var[:, b, :], stats[:, b, :]))
                nc.vector.tensor_scalar(rstd[:, b, 0:1], mean_var[:, b, 1:2], EPS, None, ALU.add).then_inc(s["var2_ready"], 1)
                dve.wait_ge(s["std2_ready"], b + 1)
                last.now(nc.vector.reciprocal(rstd[:, b, 1:2], rstd[:, b, 0:1]))
                last.now(nc.vector.tensor_scalar(tile, tile, mean_var[:, b, 0:1], rstd[:, b, 1:2], ALU.subtract, ALU.mult))
                last.now(nc.vector.tensor_tensor(tile, tile, rows["ln2_g"][:], ALU.mult))
                last.now(nc.vector.tensor_tensor(tile, tile, rows["ln2_b"][:], ALU.add))
                nc.vector.tensor_tensor(x_tokens[:, b, :], x_tokens[:, b, :], tile, ALU.add).then_inc(s["ended"], 1)




def perceiver(nc, x, ctx_1024, mask, t, cos, sin, out):
    xattn, ffn = ({k[len(pre):].replace("W", "w") if pre == "L0_xattn_" else k[len(pre):]: v for k, v in t.items() if k.startswith(pre)}
                  for pre in ("L0_xattn_", "L0_ffn_"))
    with ExitStack() as ctx:
        def sb(name, shape, dt=F32):
            return ctx.enter_context(nc.sbuf_tensor(name, shape, dt))

        x_tokens = sb("x_tokens", [P, B, D])
        identity = sb("identity", [P, P])
        cross_attention(nc, x_tokens, identity, xattn, ctx_1024, mask, x)
        segment_attention(nc, x_tokens, identity, t["L0_attn_W_qkv"], t["L0_attn_W_out"])
        x_norm = sb("x_norm", [P, T, D])
        with ExitStack() as moe:
            xT = [moe.enter_context(nc.sbuf_tensor(f"xT_{p}", [P, DC, T * P], HALF)) for p in ("hi", "lo")]
            gates = moe.enter_context(nc.sbuf_tensor("gates", [P, 2, T, H, E], F32))
            v = moe.enter_context(nc.sbuf_tensor("v", [P, T, H, PH], F32))
            gate_stage(nc, x_tokens, x_norm, xT, gates, identity, ffn["Wsel_v"], ffn["Wsel_o"])
            expert_values(nc, xT, gates, v, ffn["Wv"])
            rotary_attention(nc, xT, v, identity, ffn["Wq"], ffn["Wk"], cos, sin)
            expert_outputs(nc, x_norm, v, gates, identity, ffn["Wo"])
        feed_forward(nc, x_tokens, x_norm, identity, ffn, out)


def kernel(**inputs):
    import numpy as _np
    import concourse.bacc as _bacc
    from concourse import mybir as _mybir
    from concourse.bass_utils import run_bass_kernel_spmd as _run

    nc = _bacc.Bacc("TRN2", target_bir_lowering=False, num_devices=1)
    arrays = {name: _np.ascontiguousarray(a) for name, a in inputs.items()}
    arrays["mask_BxS2_bk1"] = arrays["mask_BxS2_bk1"].view(_np.int32)
    freq = _np.float32(10000.0) ** (-_np.arange(ROT // 2, dtype=_np.float32) / _np.float32(ROT // 2))
    angle = _np.arange(P, dtype=_np.float32)[:, None] * freq[None, :]
    arrays["rope_cos"], arrays["rope_sin"] = _np.cos(angle), _np.sin(angle)
    args = {name: nc.dram_tensor(f"in_{name}", a.shape, _mybir.dt.from_np(a.dtype), kind="ExternalInput").ap() for name, a in arrays.items()}
    out = nc.dram_tensor("out_x", (B, P, D), F32, kind="ExternalOutput").ap()
    x, context, mask, cos, sin = (args.pop(n) for n in ("x", "ctx_1024", "mask_BxS2_bk1", "rope_cos", "rope_sin"))
    perceiver(nc, x, context, mask, args, cos, sin, out)
    return _run(nc, [{f"in_{name}": a for name, a in arrays.items()}], core_ids=[0]).results[0]["out_x"]
```
